# Optimizing a Trainium2 kernel written in Bass

```python
import numpy as np
import jax
import jax.numpy as jnp

def _softmax(x, axis=-1):
    return jax.nn.softmax(x, axis=axis)

def _gelu(x):
    return jax.nn.gelu(x, approximate=True)

def _silu(x):
    return jax.nn.silu(x)

def _sigmoid(x):
    return jax.nn.sigmoid(x)

def _layernorm(x, axis=-1, eps=1e-05):
    m = jnp.mean(x, axis=axis, keepdims=True)
    v = jnp.var(x, axis=axis, keepdims=True)
    return (x - m) / jnp.sqrt(v + eps)

def _scatter_add(tgt, idx, src, axis=0):
    return tgt.at[idx].add(src)

def _segment_sum(src, seg, n):
    return jax.ops.segment_sum(src, seg, n)
kernel_name = 'mk_gnn_resnorm_d2_gnn_r16_1235fe'

def setup_inputs(seed: int=0):
    np.random.seed(seed)
    _w = jnp.asarray

    def _rec_inputs():
        import jax
        import jax.numpy as jnp
        _gk = jax.random.key(seed)
        x = -0.0003019 + 1 * jax.random.normal(jax.random.fold_in(_gk, 1), (625, 1024), jnp.float32)
        src = jax.random.randint(jax.random.fold_in(_gk, 2), (20000,), 0, 625, jnp.int32)
        dst = jax.random.randint(jax.random.fold_in(_gk, 3), (20000,), 0, 625, jnp.int32)
        _o = jnp.argsort(dst, stable=True)
        src = src[_o]
        dst = dst[_o]
        edge_type_2 = jax.random.randint(jax.random.fold_in(_gk, 12), (20000,), 0, 2, jnp.int32)
        edge_type_8 = jax.random.randint(jax.random.fold_in(_gk, 13), (20000,), 0, 8, jnp.int32)
        return (x, src, dst, edge_type_2, edge_type_8)
    x, src, dst, edge_type_2, edge_type_8 = _rec_inputs()

    def _L0_gnn_setup():
        import jax, jax.numpy as jnp
        import numpy as np
        D_MODEL = 1024
        D_FF = 286
        NUM_REL = 2
        EPS = 1e-06

        def t5_layer_norm(x, weight):
            var = jnp.mean(jnp.square(x.astype(jnp.float32)), axis=-1, keepdims=True)
            return weight * (x * jax.lax.rsqrt(var + EPS))

        def rgcn_conv(x, edge_index, edge_type, W_rel, W_root, bias):
            N = x.shape[0]
            src, dst = (edge_index[0], edge_index[1])
            h_src = x[src]
            out = x @ W_root + bias
            for r in range(NUM_REL):
                w = (edge_type == r).astype(x.dtype)
                msg = h_src @ W_rel[r] * w[:, None]
                sums = jax.ops.segment_sum(msg, dst, num_segments=N)
                cnt = jax.ops.segment_sum(w, dst, num_segments=N)
                out = out + sums / jnp.maximum(cnt, 1.0)[:, None]
            return out
        key = jax.random.key(seed)
        ks = jax.random.split(key, 8)
        N, E = (1250, 20000)
        hidden_states = jax.random.normal(ks[0], (N, D_MODEL), dtype=jnp.float32)
        edge_index = jax.random.randint(ks[1], (2, E), 0, N, dtype=jnp.int64)
        edge_type = jax.random.randint(ks[2], (E,), 0, NUM_REL, dtype=jnp.int64)
        ln_weight = jnp.ones((D_MODEL,), dtype=jnp.float32)
        W_rel = jax.random.normal(ks[3], (NUM_REL, D_MODEL, D_FF), dtype=jnp.float32) * (1.0 / np.sqrt(D_MODEL))
        W_root = jax.random.normal(ks[4], (D_MODEL, D_FF), dtype=jnp.float32) * (1.0 / np.sqrt(D_MODEL))
        conv_bias = jnp.zeros((D_FF,), dtype=jnp.float32)
        wo_weight = jax.random.normal(ks[5], (D_FF, D_MODEL), dtype=jnp.float32) * (1.0 / np.sqrt(D_FF))
        return {'hidden_states': hidden_states, 'edge_index': edge_index, 'edge_type': edge_type, 'ln_weight': ln_weight, 'W_rel': W_rel, 'W_root': W_root, 'conv_bias': conv_bias, 'wo_weight': wo_weight}
    _L0_gnn_all = _L0_gnn_setup()
    _L0_gnn_in = {k: v for k, v in _L0_gnn_all.items() if k in ('ln_weight', 'W_rel', 'W_root', 'conv_bias', 'wo_weight')}
    del _L0_gnn_all

    def _L1_gnn_setup():
        import jax, jax.numpy as jnp
        import numpy as np
        N, D, R, E = (625, 1024, 8, 5000)

        def _rgcn(x, edge_index, edge_type, weight, root, bias):
            src, dst = (edge_index[0], edge_index[1])
            msgs = x[src]
            out = x @ root + bias
            n = x.shape[0]
            for r in range(weight.shape[0]):
                mask = (edge_type == r).astype(x.dtype)
                sums = jax.ops.segment_sum(msgs * mask[:, None], dst, num_segments=n)
                cnt = jax.ops.segment_sum(mask, dst, num_segments=n)
                mean = sums / jnp.maximum(cnt, 1.0)[:, None]
                out = out + mean @ weight[r]
            return out
        key = jax.random.key(seed)
        ks = jax.random.split(key, 8)
        s = 1.0 / np.sqrt(D)
        x = jax.random.normal(ks[0], (N, D), dtype=jnp.float32)
        edge_index = jax.random.randint(ks[1], (2, E), 0, N, dtype=jnp.int64)
        edge_type = jax.random.randint(ks[2], (E,), 0, R, dtype=jnp.int64)
        weight = jax.random.normal(ks[3], (R, D, D), dtype=jnp.float32) * s
        root = jax.random.normal(ks[4], (D, D), dtype=jnp.float32) * s
        bias = jnp.zeros((D,), dtype=jnp.float32)
        w_gate = jax.random.normal(ks[5], (2 * D, D), dtype=jnp.float32) * (1.0 / np.sqrt(2 * D))
        b_gate = jnp.zeros((D,), dtype=jnp.float32)
        return {'x': x, 'edge_index': edge_index, 'edge_type': edge_type, 'weight': weight, 'root': root, 'bias': bias, 'w_gate': w_gate, 'b_gate': b_gate}
    _L1_gnn_all = _L1_gnn_setup()
    _L1_gnn_in = {k: v for k, v in _L1_gnn_all.items() if k in ('weight', 'root', 'bias', 'w_gate', 'b_gate')}
    del _L1_gnn_all
    return {'x': x, 'src': src, 'dst': dst, 'edge_type_2': edge_type_2, 'edge_type_8': edge_type_8, 'L0_gnn_ln_weight': _L0_gnn_in['ln_weight'], 'L0_gnn_W_rel': _L0_gnn_in['W_rel'], 'L0_gnn_W_root': _L0_gnn_in['W_root'], 'L0_gnn_conv_bias': _L0_gnn_in['conv_bias'], 'L0_gnn_wo_weight': _L0_gnn_in['wo_weight'], 'L1_gnn_weight': _L1_gnn_in['weight'], 'L1_gnn_root': _L1_gnn_in['root'], 'L1_gnn_bias': _L1_gnn_in['bias'], 'L1_gnn_w_gate': _L1_gnn_in['w_gate'], 'L1_gnn_b_gate': _L1_gnn_in['b_gate']}

def reference(x, src, dst, edge_type_2, edge_type_8, L0_gnn_ln_weight, L0_gnn_W_rel, L0_gnn_W_root, L0_gnn_conv_bias, L0_gnn_wo_weight, L1_gnn_weight, L1_gnn_root, L1_gnn_bias, L1_gnn_w_gate, L1_gnn_b_gate):
    import jax
    import jax.numpy as jnp

    def _L0_gnn_ref(hidden_states, edge_index, edge_type, ln_weight, W_rel, W_root, conv_bias, wo_weight):
        import jax, jax.numpy as jnp
        import numpy as np
        D_MODEL = 1024
        D_FF = 286
        NUM_REL = 2
        EPS = 1e-06

        def t5_layer_norm(x, weight):
            var = jnp.mean(jnp.square(x.astype(jnp.float32)), axis=-1, keepdims=True)
            return weight * (x * jax.lax.rsqrt(var + EPS))

        def rgcn_conv(x, edge_index, edge_type, W_rel, W_root, bias):
            N = x.shape[0]
            src, dst = (edge_index[0], edge_index[1])
            h_src = x[src]
            out = x @ W_root + bias
            for r in range(NUM_REL):
                w = (edge_type == r).astype(x.dtype)
                msg = h_src @ W_rel[r] * w[:, None]
                sums = jax.ops.segment_sum(msg, dst, num_segments=N)
                cnt = jax.ops.segment_sum(w, dst, num_segments=N)
                out = out + sums / jnp.maximum(cnt, 1.0)[:, None]
            return out
        norm_x = t5_layer_norm(hidden_states, ln_weight)
        y = jax.nn.elu(rgcn_conv(norm_x, edge_index, edge_type, W_rel, W_root, conv_bias))
        y = y @ wo_weight
        return hidden_states + y

    def _L1_gnn_ref(x, edge_index, edge_type, weight, root, bias, w_gate, b_gate):
        import jax, jax.numpy as jnp
        import numpy as np
        N, D, R, E = (625, 1024, 8, 5000)

        def _rgcn(x, edge_index, edge_type, weight, root, bias):
            src, dst = (edge_index[0], edge_index[1])
            msgs = x[src]
            out = x @ root + bias
            n = x.shape[0]
            for r in range(weight.shape[0]):
                mask = (edge_type == r).astype(x.dtype)
                sums = jax.ops.segment_sum(msgs * mask[:, None], dst, num_segments=n)
                cnt = jax.ops.segment_sum(mask, dst, num_segments=n)
                mean = sums / jnp.maximum(cnt, 1.0)[:, None]
                out = out + mean @ weight[r]
            return out
        u = _rgcn(x, edge_index, edge_type, weight, root, bias)
        z = jnp.concatenate([u, x], axis=1) @ w_gate + b_gate
        h = jnp.tanh(u) * z + x * (1.0 - z)
        return h
    edge_index = jnp.stack([src, dst])
    x = _layernorm(x + _L0_gnn_ref(x, edge_index, edge_type_2, L0_gnn_ln_weight, L0_gnn_W_rel, L0_gnn_W_root, L0_gnn_conv_bias, L0_gnn_wo_weight), axis=-1)
    x = _layernorm(x + _L1_gnn_ref(x, edge_index, edge_type_8, L1_gnn_weight, L1_gnn_root, L1_gnn_bias, L1_gnn_w_gate, L1_gnn_b_gate), axis=-1)
    return x

_drawn_inputs = setup_inputs


def setup_inputs(seed=0):
    import zlib

    import numpy as np

    out = dict(_drawn_inputs(seed))
    spreads = {'L0_gnn_ln_weight': (1.0, 0.2),
     'L0_gnn_conv_bias': (0.0, 0.1),
     'L1_gnn_bias': (0.0, 0.1),
     'L1_gnn_b_gate': (0.0, 0.1)}
    factors = {}
    for name, (base, spread) in spreads.items():
        noise = np.random.default_rng([zlib.crc32(name.encode()), seed]).standard_normal(out[name].shape)
        drawn = base * np.exp(spread * noise) if base else spread * noise
        out[name] = jnp.asarray(drawn.astype(out[name].dtype))
    for name, factor in factors.items():
        out[name] = (out[name] * factor).astype(out[name].dtype)
    return out
```

```python
from contextlib import ExitStack

import concourse.bass as bass
from concourse import mybir

ALU = mybir.AluOpType
ACT = mybir.ActivationFunctionType
AX = mybir.AxisListType
F32 = mybir.dt.float32
F16 = mybir.dt.float16
I32 = mybir.dt.int32
RMAX = bass.bass_isa.ReduceOp.max

P = 128
NODES, D = 625, 1024
NT = -(-NODES // P)
NPAD = NT * P
TAIL = NODES - (NT - 1) * P
DC = D // P
HALF = D // 2
F = 286
FC = -(-F // P)
FPAD = FC * P
R0, R1 = 2, 8
EDGES = 20000
EC = 125
CH = EDGES // EC
CP = CH // 2
WIN = 16
NWIN = NPAD // WIN
WCOLS = WIN * (R0 + R1)
PAIRS = 3
RING = 2 * PAIRS
BLOCK = NWIN // NT

TOP = 13
EXP_MASK = 0x7F800000
EXP_ONE = 1 << 23
EXP_LEAST = 27
LN_GAIN = 2.0 ** -4
X_GAIN = 2.0 ** 9
PROD_GAIN = 2.0 ** -19
EPS_RMS, EPS_LN = 1e-6, 1e-5

U_W0, U_WO, U_ROOT, U_REL = 0, 1, 2, 4
F3 = (1 + R0) * F
FH = F3 // 2
U_GX = U_REL + 2 * R1
U_GU = U_GX + 2
UNITS = U_GU + 2


def build(nc, x_d, src_d, dst_d, t2_d, t8_d, lnw_d, wrel_d, wroot_d, cb_d, wo_d,
          w1_d, root_d, b1_d, wg_d, bg_d, out_d):
    with ExitStack() as ctx:
        def sb(name, shape, dt):
            return ctx.enter_context(nc.sbuf_tensor(name, shape, dt))

        def ps(name, shape, dt):
            return ctx.enter_context(nc.psum_tensor(name, shape, dt))

        def sem(name):
            return ctx.enter_context(nc.semaphore(name))

        x = sb("x", [P, NT, D], F32)
        u_mem = sb("u_mem", [P, NT * D], F32)
        xT = sb("xT", [P, 2, DC, NPAD], F16)
        stage = sb("stage", [P, 2, DC * HALF], F32)
        wsplit = sb("wsplit", [P, 2, 2, DC * HALF], F16)
        p_mem = sb("p_mem", [P, 2 * NT * HALF], F32)
        c_mem = sb("c_mem", [P, R1 * NT * NPAD], F16)
        vec = sb("vec", [P, D], F32)
        convb = sb("convb", [P, F], F32)
        ident = sb("ident", [P, P], F32)
        iota_src = sb("iota_src", [P, NPAD], F16)
        iota_win = sb("iota_win", [P, WCOLS], F16)
        win_base = sb("win_base", [P, NWIN], F32)
        keyT = sb("keyT", [EC, CH, 3], F32)
        ones = sb("ones", [P, 1], F16)
        eps = sb("eps", [P, 2], F32)
        table = sb("table", [1, NWIN, 4], I32)
        most = sb("most", [1, 1], I32)
        key_src = sb("key_src", [EC, 2, 2 * PAIRS], F32)
        key_win = sb("key_win", [EC, 2, 2 * PAIRS, 2], F16)
        rcnt0 = sb("rcnt0", [P, R0, NT], F32)
        rcnt = sb("rcnt", [P, NT], F32)
        sc = sb("sc", [P, 4, 4], I32)
        rows = sb("rows", [P, 2, 4, NT], I32)
        lnsc = sb("lnsc", [P, 4], I32)
        am = sb("am", [P, 2], F32)
        ar = sb("ar", [P, 2], F32)
        lnmax = sb("lnmax", [P, 1], F32)
        rowmax = sb("rowmax", [P, 2, NT], F32)
        ss = sb("ss", [P, NT], F32)
        std = sb("std", [P, 3, NT], F32)
        rstd = sb("rstd", [P, 3, NT], F32)
        stats = sb("stats", [P, 2, NT, 2, 6], F32)
        mv = sb("mv", [P, 2, NT, 2], F32)
        coef0 = sb("coef0", [P, R0, NT], F32)
        coef = sb("coef", [P, NT], F32)
        cy = sb("cy", [P, NT], F32)
        cz = sb("cz", [P, 2, NT], F32)
        ci = sb("ci", [P, 4], F32)

        xs = u_mem[:, :].rearrange("p (t d) -> p t d", t=NT)
        u = xs
        w_cnt = R0 * NT * NPAD // 2
        cnt2 = u_mem[:, 0:w_cnt].bitcast(F16).rearrange("p (r s n) -> p r s n", r=R0, s=NT)
        yT = u_mem[:, w_cnt:w_cnt + FC * NPAD].bitcast(F16).rearrange("p (a c n) -> p a c n", a=2, c=FC)
        cnt8 = c_mem[:, :].rearrange("p (r s n) -> p r s n", r=R1, s=NT)
        us = c_mem[:, 0:2 * NT * D].bitcast(F32).rearrange("p (t d) -> p t d", t=NT)
        uT = c_mem[:, 2 * NT * D:4 * NT * D].rearrange("p (a c n) -> p a c n", a=2, c=DC)
        w_src = RING * 2 * NPAD // 2
        oh_src = p_mem[0:EC, 0:w_src].bitcast(F16).rearrange("p (q e n) -> p q e n", q=RING, e=2)
        oh_win = p_mem[0:EC, w_src:w_src + RING * WCOLS].bitcast(F16).rearrange("p (q e n) -> p q e n", q=RING, e=2)
        oh_win6 = p_mem[0:EC, w_src:w_src + RING * WCOLS].bitcast(F16).rearrange(
            "p (b k n) -> p b k n", b=2, k=2 * PAIRS)
        st_mem = stage[:, :, :].rearrange("p s w -> p (s w)")
        w_q = NT * R0 * F // 2
        q_part = [st_mem[:, a * w_q:(a + 1) * w_q].bitcast(F16).rearrange("p (s f) -> p s f", s=NT) for a in range(2)]
        acc0 = st_mem[:, 2 * w_q:2 * w_q + NT * FPAD].rearrange("p (t f) -> p t f", t=NT)
        wo_at = 2 * DC * HALF - FC * D
        sp_mem = wsplit[:, :, :, :].rearrange("p s a w -> p (s a w)")
        elu_tmp = sp_mem[:, 0:4 * F].bitcast(F32).rearrange("p (b f) -> p b f", b=2)
        wo_tmp = p_mem[:, 0:2 * HALF].rearrange("p (b f) -> p b f", b=2)
        w_p = NT * HALF
        p_part = [[p_mem[:, s * w_p + a * w_p // 2:s * w_p + (a + 1) * w_p // 2].bitcast(F16).rearrange(
            "p (t f) -> p t f", t=NT) for a in range(2)] for s in range(2)]
        zx = [p_mem[:, s * w_p:(s + 1) * w_p].rearrange("p (t f) -> p t f", t=NT) for s in range(2)]
        e_at = DC * F3
        edges = st_mem[0:CP, e_at:e_at + 4 * 2 * EC].bitcast(I32).rearrange("p (a h e) -> p a h e", a=4, h=2)
        ekey = c_mem[0:CP, 0:3 * 2 * EC * 2].bitcast(F32).rearrange("p (a h e) -> p a h e", a=3, h=2)
        w0 = 3 * 2 * EC * 2
        wtmp = c_mem[0:CP, w0:w0 + 2 * 24 * NWIN].bitcast(F32).rearrange("p (a j) -> p a j", a=24)
        ctmp = c_mem[0:CP, w0 + 2 * 24 * NWIN:w0 + 2 * 24 * NWIN + 2 * 16].bitcast(F32).rearrange("p (a h) -> p a h", a=8)
        sc_f, rows_f, lnsc_f = sc[:, :, :].bitcast(F32), rows[:, :, :, :].bitcast(F32), lnsc[:, :].bitcast(F32)

        psP = ps("psP", [P, NT, 512], F32)
        psA = ps("psA", [P, 2, 512], F32)
        psC = ps("psC", [P, 512], F32)

        x_padded = sem("x_padded")
        x_loaded = sem("x_loaded")
        edges_loaded = sem("edges_loaded")
        lnw_loaded = sem("lnw_loaded")
        bias_loaded = sem("bias_loaded")
        gate_bias_loaded = sem("gate_bias_loaded")
        convb_loaded = sem("convb_loaded")
        stage_full = [sem(f"stage_full{s}") for s in range(2)]
        wo_tail_loaded = sem("wo_tail_loaded")
        consts_ready = sem("consts_ready")
        pool_steps = sem("pool_steps")
        pool_turns = sem("pool_turns")
        dve_steps = sem("dve_steps")
        act_steps = sem("act_steps")
        keys_ready = sem("keys_ready")
        keys_turned = sem("keys_turned")
        keyT_ready = sem("keyT_ready")
        bounds_ready = sem("bounds_ready")
        bounds_max = sem("bounds_max")
        table_ready = sem("table_ready")
        onehot_free = sem("onehot_free")
        onehot_ready = sem("onehot_ready")
        keys_cut = sem("keys_cut")
        pair_free = sem("pair_free")
        pair_ready = sem("pair_ready")
        win_free = sem("win_free")
        deg0_full = sem("deg0_full")
        deg_full = sem("deg_full")
        rcnt_step = sem("rcnt_step")
        sumsq_ready = sem("sumsq_ready")
        rms_std_ready = sem("rms_std_ready")
        xs_ready = sem("xs_ready")
        turned = sem("turned")
        turned_hi = sem("turned_hi")
        turned_split = sem("turned_split")
        absmax_ready = sem("absmax_ready")
        max_ready = sem("max_ready")
        scale_step = sem("scale_step")
        whi_ready = sem("whi_ready")
        wlo_ready = sem("wlo_ready")
        w_used = sem("w_used")
        wo_padded = sem("wo_padded")
        q_full = sem("q_full")
        q_hi = sem("q_hi")
        q_done = sem("q_done")
        acc_padded = sem("acc_padded")
        agg0_full = sem("agg0_full")
        agg0_done = sem("agg0_done")
        elu_neg = sem("elu_neg")
        elu_exp = sem("elu_exp")
        elu_done = sem("elu_done")
        y_ready = sem("y_ready")
        y_turned = sem("y_turned")
        y_hi = sem("y_hi")
        y_lo = sem("y_lo")
        cy_ready = sem("cy_ready")
        wo_full = sem("wo_full")
        wo_copied = sem("wo_copied")
        wo_added = sem("wo_added")
        ln_var = [sem(f"ln_var{k}") for k in range(2)]
        ln_std = [sem(f"ln_std{k}") for k in range(2)]
        x1_ready = sem("x1_ready")
        p_full = sem("p_full")
        p_hi = sem("p_hi")
        p_done = sem("p_done")
        coef_ready = sem("coef_ready")
        agg_full = sem("agg_full")
        agg_done = sem("agg_done")
        row_scaled = sem("row_scaled")
        us_ready = sem("us_ready")
        tanh_ready = sem("tanh_ready")
        z_full = sem("z_full")
        z_done = sem("z_done")
        out_ready = sem("out_ready")
        out_stored = sem("out_stored")

        block = ctx.enter_context(nc.Block())

        def unit_weights(i, slot):
            st, hi, lo = flat_weights(i, slot)
            c = FC if i == U_WO else DC
            return [v.rearrange("p (c f) -> p c f", c=c) for v in (st, hi, lo)]

        def flat_weights(i, slot):
            n = DC * F3 if i == U_W0 else FC * D if i == U_WO else DC * HALF
            if i == U_W0:
                return st_mem[:, 0:n], sp_mem[:, 0:n], sp_mem[:, n:2 * n]
            st = st_mem[:, wo_at:wo_at + n] if i == U_WO else stage[:, slot, :]
            return st, wsplit[:, slot, 0, 0:n], wsplit[:, slot, 1, 0:n]

        def scale_col(i, slot):
            return i if i <= U_WO else 2 + slot

        REL = U_REL

        def slot_load(i):
            return 16 * (i // 2) + 48 if i % 2 == 0 else 16 * (i // 2 + 1)

        @block.sync
        def _(sp):
            for a, v in enumerate((src_d, dst_d, t8_d, t2_d)):
                sp.dma_start(edges[:, a, :, :], v.rearrange("(h p e) -> p h e", p=CP, e=EC)).then_inc(edges_loaded, 16)
            sp.dma_start(x[:, 0:NT - 1, :], x_d[0:(NT - 1) * P, :].rearrange("(t p) d -> p t d", p=P)).then_inc(x_loaded, 16)
            sp.wait_ge(x_padded, 1)
            sp.dma_start(x[0:TAIL, NT - 1, :], x_d[(NT - 1) * P:NODES, :]).then_inc(x_loaded, 16)
            sp.dma_start(vec[:, :], lnw_d.partition_broadcast(P)).then_inc(lnw_loaded, 16)

            def by_chunk(v):
                return v.rearrange("(c p) f -> p c f", p=P)

            st0 = unit_weights(U_W0, 0)[0]
            for n, v in enumerate((wroot_d, wrel_d[0], wrel_d[1])):
                sp.dma_start(st0[:, :, n * F:(n + 1) * F], by_chunk(v)).then_inc(stage_full[0], 16)
            sp.dma_start(convb[:, :], cb_d.partition_broadcast(P)).then_inc(convb_loaded, 16)
            sp.wait_ge(xs_ready, NT)
            sp.dma_start(vec[:, :], b1_d.partition_broadcast(P)).then_inc(bias_loaded, 16)

            def load(i, slot, src):
                sp.wait_ge(wlo_ready, i - 1)
                sp.dma_start(unit_weights(REL, slot)[0], src).then_inc(stage_full[slot], 16)

            sp.wait_ge(wlo_ready, 1)
            sp.wait_ge(wo_padded, 1)
            st_wo = unit_weights(U_WO, 1)[0]
            sp.dma_start(st_wo[:, 0:FC - 1, :], by_chunk(wo_d[0:(FC - 1) * P, :])).then_inc(stage_full[1], 16)
            sp.dma_start(st_wo[0:F - (FC - 1) * P, FC - 1, :], wo_d[(FC - 1) * P:F, :]).then_inc(wo_tail_loaded, 16)
            sp.wait_ge(y_turned, NT)
            for h in range(2):
                load(U_ROOT + h, h, by_chunk(root_d[:, h * HALF:(h + 1) * HALF]))
            w1_v = w1_d.rearrange("r (c p) f -> p (r c) f", p=P)
            with sp.Fori(0, R1) as r:
                for h in range(2):
                    load(U_REL + 2 * r + h, h, w1_v[:, bass.ts(r, DC), h * HALF:(h + 1) * HALF])
            sp.wait_ge(p_done, 2 * NT)
            sp.dma_start(vec[:, :], bg_d.partition_broadcast(P)).then_inc(gate_bias_loaded, 16)
            for k, top in ((U_GX, D), (U_GU, 0)):
                for h in range(2):
                    load(k + h, h, by_chunk(wg_d[top:top + D, h * HALF:(h + 1) * HALF]))
            for t in range(NT):
                n = P if t < NT - 1 else TAIL
                sp.wait_ge(out_ready, t + 1)
                sp.dma_start(out_d[t * P:t * P + n, :], x[0:n, t, :]).then_inc(out_stored, 16)
            sp.wait_ge(out_stored, 16 * NT)

        @block.gpsimd
        def _(pool):
            nc.gpsimd.memset(x[:, NT - 1, :], 0.0).then_inc(x_padded, 1)
            nc.gpsimd.memset(ident[:, :], 0.0).then_inc(pool_steps, 1)
            pool.wait_ge(pool_steps, 1)
            nc.gpsimd.affine_select(out=ident[:, :], in_=ident[:, :], compare_op=ALU.not_equal, fill=1.0, base=0,
                                    pattern=[[-1, P]], channel_multiplier=1).then_inc(consts_ready, 1)
            loose = dict(channel_multiplier=0, allow_small_or_imprecise_dtypes=True)
            nc.gpsimd.iota(win_base[:, :], pattern=[[256, NWIN]], base=0, **loose).then_inc(consts_ready, 1)
            nc.gpsimd.iota(ctmp[:, 0, :], pattern=[[-CP, 2]], base=200, channel_multiplier=-1,
                           allow_small_or_imprecise_dtypes=True).then_inc(consts_ready, 1)
            nc.gpsimd.iota(ctmp[:, 1, :], pattern=[[CP, 2]], base=1, channel_multiplier=1,
                           allow_small_or_imprecise_dtypes=True).then_inc(consts_ready, 1)
            nc.gpsimd.iota(iota_src[:, :], pattern=[[1, NPAD]], base=0, **loose).then_inc(consts_ready, 1)
            nc.gpsimd.iota(iota_win[:, 0:WIN * R1].rearrange("p (w r) -> p w r", r=R1), pattern=[[16, WIN], [1, R1]],
                           base=0, **loose).then_inc(consts_ready, 1)
            nc.gpsimd.iota(iota_win[:, WIN * R1:WCOLS].rearrange("p (w r) -> p w r", r=R0), pattern=[[16, WIN], [1, R0]],
                           base=0, **loose).then_inc(consts_ready, 1)
            nc.gpsimd.memset(ones[:, :], 1.0).then_inc(consts_ready, 1)
            nc.gpsimd.memset(eps[:, 0:1], EPS_RMS).then_inc(consts_ready, 1)
            nc.gpsimd.memset(eps[:, 1:2], EPS_LN).then_inc(consts_ready, 1)
            nc.gpsimd.memset(wtmp[:, 22, :], 1.0).then_inc(consts_ready, 1)
            pool.wait_ge(bounds_ready, 1)
            nc.gpsimd.partition_all_reduce(wtmp[:, 10:12, :].rearrange("p a j -> p (a j)"),
                                           wtmp[:, 8:10, :].rearrange("p a j -> p (a j)"), CP, RMAX).then_inc(bounds_max, 1)

            def unit_max(i, slot):
                pool.wait_ge(absmax_ready, i + 1)
                pool.sem_inc(pool_turns, 1)
                nc.gpsimd.partition_all_reduce(ar[:, slot:slot + 1], am[:, slot:slot + 1], P, RMAX).then_inc(max_ready, 1)

            unit_max(U_W0, 0)
            pool.wait_ge(wlo_ready, 1)
            nc.gpsimd.memset(unit_weights(U_WO, 1)[0][:, FC - 1, :], 0.0).then_inc(wo_padded, 1)
            unit_max(U_WO, 1)
            with pool.Fori(1, UNITS // 2) as k:
                for s in range(2):
                    unit_max(2 * k + s, s)

        @block.scalar
        def _(act):
            act.wait_ge(x_loaded, 32)
            for t in range(NT):
                nc.scalar.activation(xs[:, t, :], x[:, t, :], ACT.Square, accum_out=ss[:, t:t + 1]).then_inc(sumsq_ready, 1)
            act.wait_ge(sumsq_ready, NT)
            act.wait_ge(consts_ready, 11)
            nc.scalar.activation(std[:, 0, :], ss[:, :], ACT.Sqrt, bias=eps[:, 0:1], scale=1.0 / D).then_inc(rms_std_ready, 1)

            def split_hi(k, t, dst, gain):
                for g in range(2):
                    n = 2 * NT * k + 2 * t + g
                    act.wait_ge(turned, n + 1)
                    nc.scalar.activation(dst[:, 0, 4 * g:4 * g + 4, t * P:(t + 1) * P],
                                         psA[:, g, :].rearrange("p (c n) -> p c n", c=4),
                                         ACT.Copy, scale=gain).then_inc(turned_hi, 1)

            def weight_hi(i, slot, shape_of=None):
                j = shape_of if shape_of is not None else i
                st, hi, _ = flat_weights(j, slot)
                act.wait_ge(scale_step, 4 * i + 4)
                if j == U_WO:
                    act.wait_ge(w_used, 1)
                elif j != U_W0:
                    act.wait_ge(w_used, i - 1)
                nc.scalar.activation(hi, st, ACT.Copy, scale=sc_f[:, scale_col(j, slot), 2:3]).then_inc(whi_ready, 1)

            for t in range(NT):
                split_hi(0, t, xT, 1.0)
            weight_hi(U_W0, 0)

            act.wait_ge(table_ready, 1)
            most_pairs = act.value_load(most[0:1, 0:1], min_val=PAIRS, max_val=CP)

            def copy_window(j, b):
                for bank, s0, s1 in ((2 * b, 0, 3), (2 * b + 1, 3, NT)):
                    w = psP[:, bank, 0:(s1 - s0) * WCOLS].rearrange("p (s k) -> p s k", k=WCOLS)
                    w8 = w[:, :, 0:WIN * R1].rearrange("p s (w r) -> p s r w", r=R1)
                    w2 = w[:, :, WIN * R1:WCOLS].rearrange("p s (w r) -> p s r w", r=R0)
                    o8 = cnt8[:, :, s0:s1, bass.ts(j, WIN)].rearrange("p r s w -> p s r w")
                    o2 = cnt2[:, :, s0:s1, bass.ts(j, WIN)].rearrange("p r s w -> p s r w")
                    nc.scalar.activation(o8, w8, ACT.Copy)
                    last = nc.scalar.activation(o2, w2, ACT.Copy)
                last.then_inc(win_free, 1)

            def copy_block(m):
                with act.If(most_pairs <= PAIRS):
                    with act.Fori(m * BLOCK // 2, (m + 1) * BLOCK // 2) as it:
                        for b in range(2):
                            j = 2 * it + b
                            act.wait_ge(pair_free, PAIRS * (j + 1) + RING)
                            copy_window(j, b)
                with act.Else():
                    with act.Fori(m * BLOCK // 2, (m + 1) * BLOCK // 2) as it:
                        for b in range(2):
                            j = 2 * it + b
                            after = act.value_load(table[0:1, j, 3:4], min_val=1, max_val=CH * NWIN)
                            act.wait_ge(onehot_free, after + RING)
                            copy_window(j, b)

            def q_high(t):
                act.wait_ge(q_full, t + 1)
                nc.scalar.activation(q_part[0][:, t, 0:FH - F], psA[:, 0, F:FH], ACT.Copy, scale=PROD_GAIN).then_inc(q_hi, 1)
                nc.scalar.activation(q_part[0][:, t, FH - F:F3 - F], psA[:, 1, 0:FH], ACT.Copy, scale=PROD_GAIN).then_inc(q_hi, 1)

            copy_block(0)
            copy_block(1)
            for m in range(2, NT):
                q_high(m - 2)
                copy_block(m)
            q_high(NT - 2)
            q_high(NT - 1)
            act.wait_ge(wo_tail_loaded, 16)
            weight_hi(U_WO, 1)
            for t in range(NT):
                act.wait_ge(elu_neg, t + 1)
                nc.scalar.activation(elu_tmp[:, t % 2, :], elu_tmp[:, t % 2, :], ACT.Exp).then_inc(elu_exp, 1)
            for t in range(NT):
                act.wait_ge(y_turned, t + 1)
                if t >= 2:
                    act.wait_ge(y_lo, t - 1)
                nc.scalar.activation(yT[:, 0, :, t * P:(t + 1) * P],
                                     psA[:, t % 2, 0:FPAD].rearrange("p (c n) -> p c n", c=FC), ACT.Copy).then_inc(y_hi, 1)

            def wo_copy(t):
                for n in range(2 * t, 2 * t + 2):
                    act.wait_ge(wo_full, n + 1)
                    act.wait_ge(cy_ready, 1)
                    if n >= 2:
                        act.wait_ge(wo_added, n - 1)
                    nc.scalar.activation(wo_tmp[:, n % 2, :], psP[:, n % NT, :], ACT.Copy, scale=cy[:, t:t + 1]).then_inc(wo_copied, 1)

            def ln_deviation(k, t):
                act.wait_ge(ln_var[k], t + 1)
                nc.scalar.activation(std[:, 1 + k, t:t + 1], mv[:, k, t, 1:2], ACT.Sqrt, bias=eps[:, 1:2]).then_inc(ln_std[k], 1)

            wo_copy(0)
            for t in range(NT):
                if t + 1 < NT:
                    wo_copy(t + 1)
                ln_deviation(0, t)
                if t == 2:
                    weight_hi(U_ROOT, 0)
                if t >= 1:
                    split_hi(1, t - 1, xT, X_GAIN)
            split_hi(1, NT - 1, xT, X_GAIN)

            def p_high(i, slot, tiles, first=False):
                j = i - U_REL
                for t in tiles:
                    act.wait_ge(p_full, NT * (i - U_ROOT) + t + 1)
                    if t == 0 and not first:
                        act.wait_ge(agg_full, NT * (j - 1))
                    nc.scalar.activation(p_part[slot][0][:, t, :], psP[:, t, :], ACT.Copy, scale=PROD_GAIN).then_inc(p_hi, 1)

            weight_hi(U_ROOT + 1, 1)
            weight_hi(U_REL, 0)

            def rel_step(i, slot, first=False):
                p_high(i, slot, range(0, 2), first)
                weight_hi(i + 1, 1 - slot, shape_of=REL)
                p_high(i, slot, range(2, NT), first)

            rel_step(U_REL, 0, first=True)
            rel_step(U_REL + 1, 1, first=True)
            rel_step(U_REL + 2, 0)
            with act.Fori(0, R1 - 2) as k:
                for s in range(2):
                    rel_step(U_REL + 3 + 2 * k + s, 1 - s)
            rel_step(U_GX - 1, 1)
            weight_hi(U_GX + 1, 1)
            act.wait_ge(row_scaled, 1)
            for t in range(NT):
                nc.scalar.activation(us[:, t, :], u[:, t, :], ACT.Copy, scale=rows_f[:, 1, 2, t:t + 1]).then_inc(us_ready, 1)
            weight_hi(U_GU, 0)
            for t in range(NT):
                act.wait_ge(us_ready, t + 1)
                nc.scalar.activation(u[:, t, :], u[:, t, :], ACT.Tanh).then_inc(tanh_ready, 1)
            split_hi(2, 0, uT, 1.0)
            weight_hi(U_GU + 1, 1)
            split_hi(2, 1, uT, 1.0)
            for t in range(NT):
                if t + 2 < NT:
                    split_hi(2, t + 2, uT, 1.0)
                ln_deviation(1, t)

        @block.tensor
        def _(pe):
            pe.wait_ge(consts_ready, 1)
            pe.wait_ge(keys_ready, 5)
            for a in range(3):
                for h in range(2):
                    last = nc.tensor.transpose(psC[0:EC, (2 * a + h) * CP:(2 * a + h + 1) * CP], ekey[:, a, h, :], ident[0:CP, 0:CP])
            last.then_inc(keys_turned, 1)

            def turn(k, t, src, ready):
                pe.wait_ge(ready, t + 1)
                for g in range(2):
                    n = 2 * NT * k + 2 * t + g
                    if n >= 2:
                        pe.wait_ge(turned_split, n - 1)
                    for c in range(4):
                        last = nc.tensor.transpose(psA[:, g, c * P:(c + 1) * P],
                                                   src[:, t, (4 * g + c) * P:(4 * g + c + 1) * P], ident[:, :])
                    last.then_inc(turned, 1)

            for t in range(NT):
                turn(0, t, xs, xs_ready)

            pe.wait_ge(table_ready, 1)
            most_pairs = pe.value_load(most[0:1, 0:1], min_val=PAIRS, max_val=CP)

            def count_pair(b, slot, first):
                for e in range(2):
                    for s in range(NT):
                        col = (s % 3) * WCOLS
                        last = nc.tensor.matmul(
                            psP[:, 2 * b + s // 3, col:col + WCOLS], oh_src[:, slot, e, s * P:(s + 1) * P],
                            oh_win[:, slot, e, :], start=(first and e == 0 and s % 3 == 0), stop=False,
                            skip_group_check=True)
                return last

            def count_block(m):
                with pe.If(most_pairs <= PAIRS):
                    with pe.Fori(m * BLOCK // 2, (m + 1) * BLOCK // 2) as it:
                        for b in range(2):
                            j = 2 * it + b
                            pe.wait_ge(win_free, j + 1)
                            for n in range(PAIRS):
                                pe.wait_ge(pair_ready, PAIRS * j + n + 1)
                                count_pair(b, PAIRS * b + n, n == 0).then_inc(pair_free, 1)
                with pe.Else():
                    with pe.Fori(m * BLOCK // 2, (m + 1) * BLOCK // 2) as it:
                        for b in range(2):
                            j = 2 * it + b
                            pairs = pe.value_load(table[0:1, j, 1:2], min_val=PAIRS, max_val=CP)
                            before = pe.value_load(table[0:1, j, 2:3], min_val=0, max_val=CP * NWIN)
                            pe.wait_ge(win_free, j + 1)
                            pe.wait_ge(onehot_ready, before + 1)
                            count_pair(b, before % RING, True).then_inc(onehot_free, 1)
                            with pe.Fori(1, pairs) as p:
                                pe.wait_ge(onehot_ready, before + p + 1)
                                count_pair(b, (before + p) % RING, False).then_inc(onehot_free, 1)

            def product(out, lhs, i, slot, t, cols):
                _, hi, lo = unit_weights(i, slot)
                chunks = FC if i == U_WO else DC
                for c in range(chunks):
                    for a, w, first in ((0, hi, c == 0), (0, lo, False), (1, hi, False)):
                        last = nc.tensor.matmul(out, lhs[:, a, c, t * P:(t + 1) * P], w[:, c, cols],
                                                start=first, stop=(c == chunks - 1 and a == 1))
                return last

            def weights_ready(i):
                pe.wait_ge(whi_ready, i + 1)
                pe.wait_ge(wlo_ready, i + 1)

            def first_products(t):
                if t == 0:
                    weights_ready(U_W0)
                    pe.wait_ge(turned_split, 2 * NT)
                else:
                    pe.wait_ge(q_done, 3 * t)
                product(psA[:, 0, 0:FH], xT, U_W0, 0, t, slice(0, FH))
                return product(psA[:, 1, 0:FH], xT, U_W0, 0, t, slice(FH, F3)).then_inc(q_full, 1)

            count_block(0)
            count_block(1)
            for m in range(2, NT):
                first_products(m - 2)
                count_block(m)
            first_products(NT - 2)

            degrees = psC[:, 0:(R1 + R0) * NT].rearrange("p (r t) -> p r t", t=NT)

            def degree(r, counts):
                for t in range(NT):
                    for s in range(NT):
                        last = nc.tensor.matmul(degrees[:, r, t:t + 1], counts[:, s, t * P:(t + 1) * P], ones[:, :],
                                                start=(s == 0), stop=(s == NT - 1))
                return last

            pe.wait_ge(win_free, NWIN + 2)
            pe.wait_ge(keyT_ready, 1)
            for r in range(R0):
                last = degree(R1 + r, cnt2[:, r, :, :])
            last.then_inc(deg0_full, 1)
            first_products(NT - 1)
            pe.wait_ge(q_full, NT)
            pe.sem_inc(w_used, 1)

            pe.wait_ge(q_done, 3 * NT)
            for t in range(NT):
                for r in range(R0):
                    n = R0 * t + r
                    if n >= 4:
                        pe.wait_ge(agg0_done, n - 3)
                    for s in range(NT):
                        for a in range(2):
                            last = nc.tensor.matmul(psP[:, n % 4, 0:F], cnt2[:, r, s, t * P:(t + 1) * P],
                                                    q_part[a][:, s, r * F:(r + 1) * F],
                                                    start=(s == 0 and a == 0), stop=(s == NT - 1 and a == 1))
                    last.then_inc(agg0_full, 1)
            for t in range(NT):
                pe.wait_ge(y_ready, t + 1)
                if t >= 2:
                    pe.wait_ge(y_lo, t - 1)
                for c in range(FC):
                    last = nc.tensor.transpose(psA[:, t % 2, c * P:(c + 1) * P], acc0[:, t, c * P:(c + 1) * P], ident[:, :])
                last.then_inc(y_turned, 1)
            weights_ready(U_WO)
            pe.wait_ge(agg0_done, R0 * NT)

            def wo_product(t):
                pe.wait_ge(y_hi, t + 1)
                pe.wait_ge(y_lo, t + 1)
                for h in range(2):
                    n = 2 * t + h
                    if n >= NT:
                        pe.wait_ge(wo_copied, n - NT + 1)
                    last = product(psP[:, n % NT, :], yT, U_WO, 1, t, slice(h * HALF, (h + 1) * HALF))
                    last.then_inc(wo_full, 1)

            def tile_product(i, slot, t, first=False):
                if not first:
                    pe.wait_ge(p_done, NT * (i - U_ROOT - 1) + t + 1)
                product(psP[:, t, :], xT, REL, slot, t, slice(0, HALF)).then_inc(p_full, 1)

            def unit_used(i):
                pe.wait_ge(p_full, NT * (i - U_ROOT + 1))
                pe.sem_inc(w_used, 1)

            def root_product(t):
                if t == 0:
                    pe.wait_ge(wo_copied, 2 * NT)
                    weights_ready(U_ROOT)
                pe.wait_ge(turned_split, 2 * NT + 2 * t + 2)
                tile_product(U_ROOT, 0, t, first=True)

            wo_product(0)
            wo_product(1)
            wo_product(2)
            turn(1, 0, x, x1_ready)
            wo_product(3)
            turn(1, 1, x, x1_ready)
            wo_product(4)
            pe.wait_ge(wo_full, 2 * NT)
            pe.sem_inc(w_used, 1)
            for t in range(2, NT):
                turn(1, t, x, x1_ready)
                root_product(t - 2)
            root_product(NT - 2)
            root_product(NT - 1)
            unit_used(U_ROOT)

            def products(i, slot):
                weights_ready(i)
                for t in range(NT):
                    tile_product(i, slot, t)
                unit_used(i)

            def aggregate(j, r, h, first=False):
                pe.wait_ge(p_done, NT * (j + U_REL - U_ROOT + 1))
                for t in range(NT):
                    if not (first and t < 2):
                        pe.wait_ge(agg_done, NT * j + t - 1)
                    for s in range(NT):
                        for a in range(2):
                            last = nc.tensor.matmul(psA[:, (NT * h + t) % 2, :], cnt8[:, r, s, t * P:(t + 1) * P],
                                                    p_part[h][a][:, s, :], start=(s == 0 and a == 0), stop=(s == NT - 1 and a == 1))
                    last.then_inc(agg_full, 1)

            def degree8(r):
                degree(r, cnt8[:, r, :, :]).then_inc(deg_full, 1)

            products(U_ROOT + 1, 1)
            pe.wait_ge(turned_split, 4 * NT)
            products(U_REL, 0)
            degree8(0)
            products(U_REL + 1, 1)
            aggregate(0, 0, 0, first=True)
            products(U_REL + 2, 0)
            aggregate(1, 0, 1)
            with pe.Fori(0, R1 - 2) as k:
                degree8(k + 1)
                products(U_REL + 3 + 2 * k, 1)
                aggregate(2 + 2 * k, k + 1, 0)
                products(U_REL + 4 + 2 * k, 0)
                aggregate(3 + 2 * k, k + 1, 1)
            degree8(R1 - 1)
            products(U_GX - 1, 1)
            aggregate(2 * R1 - 2, R1 - 1, 0)
            products(U_GX, 0)
            aggregate(2 * R1 - 1, R1 - 1, 1)
            products(U_GX + 1, 1)

            pe.wait_ge(p_done, NT * (U_GU - U_ROOT))
            pe.wait_ge(agg_done, NT * 2 * R1)

            def gate_product(t):
                pe.wait_ge(turned_hi, 4 * NT + 2 * t + 2)
                pe.wait_ge(turned_split, 4 * NT + 2 * t + 2)
                for h in range(2):
                    n = 2 * t + h
                    if t == 0:
                        weights_ready(U_GU + h)
                    if n >= NT:
                        pe.wait_ge(z_done, n - NT + 1)
                    product(psP[:, n % NT, :], uT, REL, h, t, slice(0, HALF)).then_inc(z_full, 1)

            turn(2, 0, us, us_ready)
            for t in range(NT):
                if t + 1 < NT:
                    turn(2, t + 1, us, us_ready)
                gate_product(t)

        @block.vector
        def _(dve):
            steps = [0]

            def step(ins):
                steps[0] += 1
                ins.then_inc(dve_steps, 1)
                dve.wait_ge(dve_steps, steps[0])

            ts, stt, tt = nc.vector.tensor_scalar, nc.vector.scalar_tensor_tensor, nc.vector.tensor_tensor

            def exponents(dst, bits):
                return (lambda: ts(dst[0], bits, EXP_MASK, None, ALU.bitwise_and),
                        lambda: ts(dst[1], dst[0], float(EXP_LEAST * EXP_ONE), None, ALU.max),
                        lambda: ts(dst[2], dst[1], -1.0, float((254 + TOP) * EXP_ONE), ALU.mult, ALU.add),
                        lambda: ts(dst[3], dst[1], float(TOP * EXP_ONE), None, ALU.subtract))

            def row_scales(dst, bits, ready=None):
                *chain, last = exponents(dst, bits)
                for f in chain:
                    step(f())
                if ready:
                    last().then_inc(ready, 1)
                    dve.wait_ge(ready, 1)
                else:
                    step(last())

            dve.wait_ge(edges_loaded, 64)
            nc.vector.tensor_copy(ekey[:, 0, :, :], edges[:, 0, :, :]).then_inc(keys_ready, 1)
            stt(ekey[:, 1, :, :], edges[:, 1, :, :], 16.0, edges[:, 2, :, :], ALU.mult, ALU.add).then_inc(keys_ready, 1)
            stt(ekey[:, 2, :, :], edges[:, 1, :, :], 16.0, edges[:, 3, :, :], ALU.mult, ALU.add).then_inc(keys_ready, 1)
            nc.vector.tensor_reduce(ctmp[:, 2, :], edges[:, 1, :, :], AX.X, ALU.min).then_inc(keys_ready, 1)
            nc.vector.tensor_reduce(ctmp[:, 3, :], edges[:, 1, :, :], AX.X, ALU.max).then_inc(keys_ready, 1)
            dve.wait_ge(keys_ready, 5)
            step(ts(ctmp[:, 4, :], ctmp[:, 2, :], 16.0, 256.0 - 16.0, ALU.mult, ALU.subtract))
            step(ts(ctmp[:, 5, :], ctmp[:, 3, :], 16.0, None, ALU.mult))
            dve.wait_ge(consts_ready, 11)
            base = win_base[0:CP, :]
            for h in range(2):
                step(ts(wtmp[:, h, :], base, ctmp[:, 5, h:h + 1], None, ALU.is_le))
                step(stt(wtmp[:, 2 + h, :], base, ctmp[:, 4, h:h + 1], wtmp[:, h, :], ALU.is_ge, ALU.mult))
                step(ts(wtmp[:, 4 + h, :], wtmp[:, 2 + h, :], ctmp[:, 0, h:h + 1], None, ALU.mult))
                step(ts(wtmp[:, 6 + h, :], wtmp[:, 2 + h, :], ctmp[:, 1, h:h + 1], None, ALU.mult))
            step(tt(wtmp[:, 8, :], wtmp[:, 4, :], wtmp[:, 5, :], ALU.max))
            tt(wtmp[:, 9, :], wtmp[:, 6, :], wtmp[:, 7, :], ALU.max).then_inc(bounds_ready, 1)
            dve.wait_ge(keys_turned, 1)
            nc.vector.tensor_copy(keyT[:, :, :].rearrange("p k a -> p a k"),
                                  psC[0:EC, 0:3 * CH].rearrange("p (a k) -> p a k", a=3)).then_inc(keyT_ready, 1)

            dve.wait_ge(bounds_max, 1)

            def row(a):
                return wtmp[0:1, a, :]
            step(ts(row(12), row(10), -1.0, 200.0, ALU.mult, ALU.add))
            step(tt(row(13), row(11), row(12), ALU.subtract))
            pairs_i = wtmp[0:1, 14, :].bitcast(I32)
            step(ts(pairs_i, row(13), 0.5, 0.25, ALU.mult, ALU.add))
            step(ts(row(15), pairs_i, float(PAIRS), None, ALU.max))
            step(ts(row(16), row(15), -2.0, float(CH), ALU.mult, ALU.add))
            step(nc.vector.tensor_tensor_scan(row(17), row(22), row(15), 0.0, ALU.mult, ALU.add))
            step(tt(table[:, :, 0], row(12), row(16), ALU.min))
            step(nc.vector.tensor_copy(table[:, :, 1], row(15)))
            step(tt(table[:, :, 2], row(17), row(15), ALU.subtract))
            step(nc.vector.tensor_copy(table[:, :, 3], row(17)))
            nc.vector.tensor_reduce(most[:, :], row(15), AX.X, ALU.max).then_inc(table_ready, 1)

            dve.wait_ge(lnw_loaded, 16)
            step(nc.vector.tensor_reduce(lnmax[:, :], vec[:, :], AX.X, ALU.max, apply_absolute_value=True))
            row_scales([lnsc[:, a:a + 1] for a in range(4)], lnmax[:, :].bitcast(I32))
            step(ts(vec[:, :], vec[:, :], lnsc_f[:, 2:3], LN_GAIN, ALU.mult, ALU.mult))
            dve.wait_ge(rms_std_ready, 1)
            step(nc.vector.reciprocal(rstd[:, 0, :], std[:, 0, :]))
            for t in range(NT):
                stt(xs[:, t, :], x[:, t, :], rstd[:, 0, t:t + 1], vec[:, :], ALU.mult, ALU.mult).then_inc(xs_ready, 1)

            def split_lo(k, t, dst, gain):
                for g in range(2):
                    n = 2 * NT * k + 2 * t + g
                    dve.wait_ge(turned_hi, n + 1)
                    hi = dst[:, 0, 4 * g:4 * g + 4, t * P:(t + 1) * P]
                    lo = dst[:, 1, 4 * g:4 * g + 4, t * P:(t + 1) * P]
                    stt(lo, psA[:, g, :].rearrange("p (c n) -> p c n", c=4), gain, hi,
                        ALU.mult, ALU.subtract).then_inc(turned_split, 1)

            def unit_absmax(i, slot, loads, shape_of=None):
                j = shape_of if shape_of is not None else i
                dve.wait_ge(stage_full[slot], loads)
                nc.vector.tensor_reduce(am[:, slot:slot + 1], flat_weights(j, slot)[0], AX.X, ALU.max,
                                        apply_absolute_value=True).then_inc(absmax_ready, 1)

            def unit_scale(i, slot, shape_of=None):
                j = shape_of if shape_of is not None else i
                c = scale_col(j, slot)
                dve.wait_ge(max_ready, i + 1)
                for k, f in enumerate(exponents([sc[:, c, a:a + 1] for a in range(4)], ar[:, slot:slot + 1].bitcast(I32))):
                    if k in (1, 2):
                        dve.wait_ge(scale_step, 4 * i + k)
                    f().then_inc(scale_step, 1)

            def unit_lo(i, slot, shape_of=None):
                j = shape_of if shape_of is not None else i
                st, hi, lo = flat_weights(j, slot)
                dve.wait_ge(whi_ready, i + 1)
                stt(lo, st, sc_f[:, scale_col(j, slot), 2:3], hi, ALU.mult, ALU.subtract).then_inc(wlo_ready, 1)

            for t in range(NT - 1):
                split_lo(0, t, xT, 1.0)
            unit_absmax(U_W0, 0, 48)
            split_lo(0, NT - 1, xT, 1.0)
            unit_scale(U_W0, 0)
            unit_lo(U_W0, 0)

            nc.vector.memset(psP[:, 0, 0:1], 0.0).then_inc(onehot_free, RING)
            nc.vector.memset(psP[:, 1, 0:1], 0.0).then_inc(pair_free, RING)
            nc.vector.memset(psP[:, 2, 0:1], 0.0).then_inc(win_free, 2)
            dve.wait_ge(table_ready, 1)
            dve.wait_ge(keyT_ready, 1)
            most_pairs = dve.value_load(most[0:1, 0:1], min_val=PAIRS, max_val=CP)
            win8 = iota_win[0:EC, 0:WIN * R1]
            win2 = iota_win[0:EC, WIN * R1:WCOLS]

            def onehot_block(m):
                with dve.If(most_pairs <= PAIRS):
                    with dve.Fori(m * BLOCK // 2, (m + 1) * BLOCK // 2) as it:
                        for b in range(2):
                            j = 2 * it + b
                            chunk = dve.value_load(table[0:1, j, 0:1], min_val=0, max_val=CH - 2 * PAIRS)
                            cut = keyT[:, bass.ds(chunk, 2 * PAIRS), :]
                            nc.vector.tensor_copy(key_src[:, b, :], cut[:, :, 0]).then_inc(keys_cut, 1)
                            ts(key_win[:, b, :, :], cut[:, :, 1:3], win_base[0:EC, bass.ts(j, 1)], None,
                               ALU.subtract).then_inc(keys_cut, 1)
                        for b in range(2):
                            j = 2 * it + b
                            dve.wait_ge(keys_cut, 4 * it + 2 * b + 2)
                            dve.wait_ge(pair_free, PAIRS * (j + 1))
                            for r, w in ((0, win8), (1, win2)):
                                n = w.shape[1]
                                tt(oh_win6[:, b, :, r * WIN * R1:r * WIN * R1 + n],
                                   w.unsqueeze(1).broadcast_to([EC, 2 * PAIRS, n]),
                                   key_win[:, b, :, r:r + 1].broadcast_to([EC, 2 * PAIRS, n]), ALU.is_equal)
                            for n in range(PAIRS):
                                for e in range(2):
                                    k = 2 * n + e
                                    last = ts(oh_src[:, PAIRS * b + n, e, :], iota_src[0:EC, :], key_src[:, b, k:k + 1], None,
                                              ALU.is_equal)
                                last.then_inc(pair_ready, 1)
                        dve.wait_ge(pair_ready, PAIRS * (2 * it + 2))
                with dve.Else():
                    with dve.Fori(m * BLOCK, (m + 1) * BLOCK) as j:
                        chunk = dve.value_load(table[0:1, j, 0:1], min_val=0, max_val=CH - 2 * PAIRS)
                        pairs = dve.value_load(table[0:1, j, 1:2], min_val=PAIRS, max_val=CP)
                        before = dve.value_load(table[0:1, j, 2:3], min_val=0, max_val=CP * NWIN)
                        with dve.Fori(0, pairs) as p:
                            q = before + p
                            dve.wait_ge(onehot_free, q + 1)
                            slot = q % RING
                            wb = win_base[0:EC, bass.ts(j, 1)]
                            for e in range(2):
                                k = (chunk + 2 * p).with_bounds(min_val=0, max_val=CH - 2) + e
                                ts(oh_src[:, slot, e, :], iota_src[0:EC, :], keyT[:, k, 0:1], None, ALU.is_equal)
                                ts(oh_win[:, slot, e, 0:WIN * R1], win8, wb, keyT[:, k, 1:2], ALU.add, ALU.is_equal)
                                last = ts(oh_win[:, slot, e, WIN * R1:WCOLS], win2, wb, keyT[:, k, 2:3],
                                          ALU.add, ALU.is_equal)
                            last.then_inc(onehot_ready, 1)

            def first_sums(t):
                dve.wait_ge(q_hi, 2 * t + 1)
                stt(acc0[:, t, 0:F], psA[:, 0, 0:F], ci[:, 0:1], convb[:, :], ALU.mult, ALU.add).then_inc(q_done, 1)
                for n, (src, cols) in enumerate(((psA[:, 0, F:FH], slice(0, FH - F)), (psA[:, 1, 0:FH], slice(FH - F, F3 - F)))):
                    dve.wait_ge(q_hi, 2 * t + n + 1)
                    stt(q_part[1][:, t, cols], src, PROD_GAIN, q_part[0][:, t, cols], ALU.mult, ALU.subtract).then_inc(q_done, 1)

            onehot_block(0)
            dve.wait_ge(wlo_ready, 1)
            nc.vector.memset(acc0[:, :, F:FPAD], 0.0).then_inc(acc_padded, 1)
            step(tt(ci[:, 0:1], sc_f[:, U_W0, 3:4], lnsc_f[:, 3:4], ALU.mult))
            step(ts(ci[:, 1:2], ci[:, 0:1], 1.0 / (LN_GAIN * PROD_GAIN), None, ALU.mult))
            step(ts(ci[:, 0:1], ci[:, 0:1], 1.0 / LN_GAIN, None, ALU.mult))
            dve.wait_ge(convb_loaded, 16)
            onehot_block(1)
            onehot_block(2)
            first_sums(0)
            onehot_block(3)
            first_sums(1)
            onehot_block(4)
            first_sums(2)
            dve.wait_ge(wo_tail_loaded, 16)
            unit_absmax(U_WO, 1, slot_load(U_WO))
            first_sums(3)
            unit_scale(U_WO, 1)
            dve.wait_ge(deg0_full, 1)
            rc0 = rcnt0[:, :, :].rearrange("p r t -> p (r t)")
            step(ts(rc0, psC[:, R1 * NT:(R1 + R0) * NT], 1.0, None, ALU.max))
            step(nc.vector.reciprocal(rc0, rc0))
            step(ts(coef0[:, :, :].rearrange("p r t -> p (r t)"), rc0, ci[:, 1:2], None, ALU.mult))
            first_sums(4)
            dve.wait_ge(acc_padded, 1)
            dve.wait_ge(q_done, 3 * NT)

            def elu_end(t):
                dve.wait_ge(elu_exp, t + 1)
                step(stt(acc0[:, t, 0:F], acc0[:, t, 0:F], 0.0, elu_tmp[:, t % 2, :], ALU.max, ALU.add))
                nc.vector.tensor_reduce(rowmax[:, 0, t:t + 1], acc0[:, t, 0:F], AX.X, ALU.max).then_inc(elu_done, 1)

            for t in range(NT):
                for r in range(R0):
                    n = R0 * t + r
                    dve.wait_ge(agg0_full, n + 1)
                    if r:
                        dve.wait_ge(agg0_done, n)
                    stt(acc0[:, t, 0:F], psP[:, n % 4, 0:F], coef0[:, r, t:t + 1], acc0[:, t, 0:F], ALU.mult, ALU.add).then_inc(agg0_done, 1)
                dve.wait_ge(agg0_done, R0 * t + R0)
                if t >= 2:
                    dve.wait_ge(elu_done, t - 1)
                ts(elu_tmp[:, t % 2, :], acc0[:, t, 0:F], 0.0, None, ALU.min).then_inc(elu_neg, 1)
                if t:
                    elu_end(t - 1)
            elu_end(NT - 1)
            dve.wait_ge(elu_done, NT)
            step(ts(rowmax[:, 0, :], rowmax[:, 0, :], 1.0, None, ALU.max))
            row_scales([rows[:, 0, a, :] for a in range(4)], rowmax[:, 0, :].bitcast(I32))
            for t in range(NT):
                ts(acc0[:, t, 0:F], acc0[:, t, 0:F], -1.0, rows_f[:, 0, 2, t:t + 1], ALU.add, ALU.mult).then_inc(y_ready, 1)
            ts(cy[:, :], rows_f[:, 0, 3, :], sc_f[:, U_WO, 3:4], None, ALU.mult).then_inc(cy_ready, 1)
            unit_lo(U_WO, 1)
            for t in range(NT):
                dve.wait_ge(y_hi, t + 1)
                tt(yT[:, 1, :, t * P:(t + 1) * P], psA[:, t % 2, 0:FPAD].rearrange("p (c n) -> p c n", c=FC),
                   yT[:, 0, :, t * P:(t + 1) * P], ALU.subtract).then_inc(y_lo, 1)

            def norm_stats(k, t, h):
                step(nc.vector.bn_stats(stats[:, k, t, h, :], x[:, t, h * HALF:(h + 1) * HALF]))

            def norm_var(k, t):
                nc.vector.bn_aggr(mv[:, k, t, :], stats[:, k, t, :, :].rearrange("p h s -> p (h s)")).then_inc(ln_var[k], 1)

            def norm_apply(k, t, ready):
                dve.wait_ge(ln_std[k], t + 1)
                dve.wait_ge(ln_var[k], t + 1)
                step(nc.vector.reciprocal(rstd[:, 1 + k, t:t + 1], std[:, 1 + k, t:t + 1]))
                ts(x[:, t, :], x[:, t, :], mv[:, k, t, 0:1], rstd[:, 1 + k, t:t + 1], ALU.subtract, ALU.mult).then_inc(ready, 1)

            for t in range(NT):
                for h in range(2):
                    n = 2 * t + h
                    dve.wait_ge(wo_copied, n + 1)
                    xv = x[:, t, h * HALF:(h + 1) * HALF]
                    stt(xv, xv, 2.0, wo_tmp[:, n % 2, :], ALU.mult, ALU.add).then_inc(wo_added, 1)
                    dve.wait_ge(wo_added, n + 1)
                    norm_stats(0, t, h)
                norm_var(0, t)
                if t == 1:
                    unit_absmax(U_ROOT, 0, slot_load(U_ROOT))
                if t:
                    norm_apply(0, t - 1, x1_ready)
                if t == 1:
                    unit_scale(U_ROOT, 0)
                if t >= 2:
                    split_lo(1, t - 2, xT, X_GAIN)
                if t == 3:
                    unit_lo(U_ROOT, 0)
            norm_apply(0, NT - 1, x1_ready)
            split_lo(1, NT - 2, xT, X_GAIN)
            split_lo(1, NT - 1, xT, X_GAIN)

            def evacuate(i, slot, t, kind, h=0):
                k = NT * (i - U_ROOT) + t + 1
                src = psP[:, t, :]
                if kind == "rel":
                    dve.wait_ge(p_hi, NT * (i - U_REL) + t + 1)
                    ins = stt(p_part[slot][1][:, t, :], src, PROD_GAIN, p_part[slot][0][:, t, :], ALU.mult, ALU.subtract)
                else:
                    dve.wait_ge(p_full, k)
                    dst = u[:, t, h * HALF:(h + 1) * HALF] if kind == "root" else zx[h][:, t, :]
                    ins = stt(dst, src, ci[:, 3:4], vec[:, h * HALF:(h + 1) * HALF], ALU.mult, ALU.add)
                ins.then_inc(p_done, 1)

            def reciprocals(r, first):
                if not first:
                    dve.wait_ge(coef_ready, 2 * r)
                dve.wait_ge(deg_full, r + 1)
                ts(rcnt[:, :], degrees[:, r, :], 1.0, None, ALU.max).then_inc(rcnt_step, 1)
                dve.wait_ge(rcnt_step, 2 * r + 1)
                nc.vector.reciprocal(rcnt[:, :], rcnt[:, :]).then_inc(rcnt_step, 1)
                dve.wait_ge(rcnt_step, 2 * r + 2)

            degrees = psC[:, 0:(R1 + R0) * NT].rearrange("p (r t) -> p r t", t=NT)

            def agg_coef(j, slot, first=False):
                if not first:
                    dve.wait_ge(agg_done, NT * j)
                ts(coef[:, :], rcnt[:, :], sc_f[:, scale_col(REL, slot), 3:4], 1.0 / (X_GAIN * PROD_GAIN),
                   ALU.mult, ALU.mult).then_inc(coef_ready, 1)

            def agg_add(j, h):
                dve.wait_ge(coef_ready, j + 1)
                for t in range(NT):
                    uv = u[:, t, h * HALF:(h + 1) * HALF]
                    dve.wait_ge(agg_full, NT * j + t + 1)
                    stt(uv, psA[:, (NT * h + t) % 2, :], coef[:, t:t + 1], uv, ALU.mult, ALU.add).then_inc(agg_done, 1)

            def plain_factor(i, slot):
                if i != U_ROOT:
                    dve.wait_ge(p_done, NT * (i - U_ROOT))
                step(ts(ci[:, 3:4], sc_f[:, scale_col(REL, slot), 3:4], 1.0 / X_GAIN, None, ALU.mult))

            def root_step(i, slot):
                plain_factor(i, slot)
                unit_absmax(i + 1, 1 - slot, slot_load(i + 1), REL)
                evacuate(i, slot, 0, "root", slot)
                unit_scale(i + 1, 1 - slot, REL)
                evacuate(i, slot, 1, "root", slot)
                unit_lo(i + 1, 1 - slot, REL)
                for t in range(2, NT):
                    evacuate(i, slot, t, "root", slot)

            def rel_step(i, slot, loads, agg=None):
                unit_absmax(i + 1, 1 - slot, loads, REL)
                if agg:
                    if slot:
                        reciprocals(agg[1], agg[2])
                    agg_coef(agg[0], 1 - slot, agg[2])
                evacuate(i, slot, 0, "rel")
                unit_scale(i + 1, 1 - slot, REL)
                evacuate(i, slot, 1, "rel")
                evacuate(i, slot, 2, "rel")
                unit_lo(i + 1, 1 - slot, REL)
                evacuate(i, slot, 3, "rel")
                evacuate(i, slot, 4, "rel")
                if agg:
                    agg_add(agg[0], 1 - slot)

            dve.wait_ge(bias_loaded, 16)
            root_step(U_ROOT, 0)
            root_step(U_ROOT + 1, 1)
            rel_step(U_REL, 0, slot_load(U_REL + 1))
            rel_step(U_REL + 1, 1, slot_load(U_REL + 2), (0, 0, True))
            rel_step(U_REL + 2, 0, slot_load(U_REL + 3), (1, 0, False))
            with dve.Fori(0, R1 - 2) as k:
                rel_step(U_REL + 3 + 2 * k, 1, slot_load(U_REL + 4) + 16 * k, (2 + 2 * k, k + 1, False))
                rel_step(U_REL + 4 + 2 * k, 0, slot_load(U_REL + 5) + 16 * k, (3 + 2 * k, k + 1, False))
            rel_step(U_GX - 1, 1, slot_load(U_GX), (2 * R1 - 2, R1 - 1, False))

            dve.wait_ge(gate_bias_loaded, 16)
            agg_coef(2 * R1 - 1, 1)
            plain_factor(U_GX, 0)
            unit_absmax(U_GX + 1, 1, slot_load(U_GX + 1))
            evacuate(U_GX, 0, 0, "gate", 0)
            unit_scale(U_GX + 1, 1)
            evacuate(U_GX, 0, 1, "gate", 0)
            evacuate(U_GX, 0, 2, "gate", 0)
            unit_lo(U_GX + 1, 1)
            evacuate(U_GX, 0, 3, "gate", 0)
            evacuate(U_GX, 0, 4, "gate", 0)
            unit_absmax(U_GU, 0, slot_load(U_GU))
            unit_scale(U_GU, 0)
            agg_add(2 * R1 - 1, 1)
            plain_factor(U_GX + 1, 1)
            dve.wait_ge(agg_done, 2 * R1 * NT)
            for t in range(NT):
                step(nc.vector.tensor_reduce(rowmax[:, 1, t:t + 1], u[:, t, :], AX.X, ALU.max, apply_absolute_value=True))
            row_scales([rows[:, 1, a, :] for a in range(4)], rowmax[:, 1, :].bitcast(I32), row_scaled)
            unit_lo(U_GU, 0)
            step(ts(cz[:, 0, :], rows_f[:, 1, 3, :], sc_f[:, scale_col(REL, 0), 3:4], None, ALU.mult))
            unit_absmax(U_GU + 1, 1, slot_load(U_GU + 1))
            for t in range(NT):
                evacuate(U_GX + 1, 1, t, "gate", 1)
            unit_scale(U_GU + 1, 1)
            split_lo(2, 0, uT, 1.0)
            unit_lo(U_GU + 1, 1)
            dve.wait_ge(scale_step, 4 * UNITS)
            step(ts(cz[:, 1, :], rows_f[:, 1, 3, :], sc_f[:, scale_col(REL, 1), 3:4], None, ALU.mult))
            for t in range(NT):
                if t + 1 < NT:
                    split_lo(2, t + 1, uT, 1.0)
                dve.wait_ge(tanh_ready, t + 1)
                step(tt(u[:, t, :], u[:, t, :], x[:, t, :], ALU.subtract))
                for h in range(2):
                    n = 2 * t + h
                    cols = slice(h * HALF, (h + 1) * HALF)
                    dve.wait_ge(z_full, n + 1)
                    stt(zx[h][:, t, :], psP[:, n % NT, :], cz[:, h, t:t + 1], zx[h][:, t, :], ALU.mult, ALU.add).then_inc(z_done, 1)
                    dve.wait_ge(z_done, n + 1)
                    step(tt(zx[h][:, t, :], zx[h][:, t, :], u[:, t, cols], ALU.mult))
                    step(stt(x[:, t, cols], x[:, t, cols], 2.0, zx[h][:, t, :], ALU.mult, ALU.add))
                    norm_stats(1, t, h)
                norm_var(1, t)
                if t:
                    norm_apply(1, t - 1, out_ready)
            norm_apply(1, NT - 1, out_ready)


_INS = ["x", "src", "dst", "edge_type_2", "edge_type_8", "L0_gnn_ln_weight", "L0_gnn_W_rel", "L0_gnn_W_root",
        "L0_gnn_conv_bias", "L0_gnn_wo_weight", "L1_gnn_weight", "L1_gnn_root", "L1_gnn_bias", "L1_gnn_w_gate",
        "L1_gnn_b_gate"]


def kernel(**inputs):
    import numpy as np
    import concourse.bacc as bacc
    from concourse.bass_utils import run_bass_kernel_spmd

    nc = bacc.Bacc("TRN2", target_bir_lowering=False, num_devices=1)
    arrays, args = {}, []
    for name in _INS:
        a = np.ascontiguousarray(inputs[name])
        arrays[f"in_{name}"] = a
        args.append(nc.dram_tensor(f"in_{name}", a.shape, mybir.dt.from_np(a.dtype), kind="ExternalInput").ap())
    out = nc.dram_tensor("out", (NODES, D), F32, kind="ExternalOutput").ap()
    build(nc, *args, out)
    r = run_bass_kernel_spmd(nc, [arrays], core_ids=[0])
    return r.results[0]["out"]
```

```python
from contextlib import ExitStack

import concourse.bass as bass
from concourse import mybir

ALU = mybir.AluOpType
ACT = mybir.ActivationFunctionType
AX = mybir.AxisListType
F32 = mybir.dt.float32
F16 = mybir.dt.float16
I32 = mybir.dt.int32
RMAX = bass.bass_isa.ReduceOp.max

P = 128
NODES, D = 625, 1024
NT = -(-NODES // P)
NPAD = NT * P
TAIL = NODES - (NT - 1) * P
DC = D // P
HALF = D // 2
F = 286
FC = -(-F // P)
FPAD = FC * P
R0, R1 = 2, 8
EDGES = 20000
EC = 125
CH = EDGES // EC
CP = CH // 2
WIN = 14
NWIN = -(-NODES // WIN)
WPAD = NPAD - NWIN * WIN
WCOLS = WIN * (R0 + R1)
MEET = 5
PAIRS = 3
RING = 2 * PAIRS
BLOCK = 4
AHEAD = NWIN - 2 * NT * BLOCK

TOP = 13
EXP_MASK = 0x7F800000
EXP_ONE = 1 << 23
EXP_LEAST = 27
LN_GAIN = 2.0 ** -4
X_GAIN = 2.0 ** 9
PROD_GAIN = 2.0 ** -19
EPS_RMS, EPS_LN = 1e-6, 1e-5

U_W0, U_WO, U_ROOT, U_REL = 0, 1, 2, 4
F3 = (1 + R0) * F
FH = F3 // 2
U_GX = U_REL + 2 * R1
U_GU = U_GX + 2
UNITS = U_GU + 2


def build(nc, x_d, src_d, dst_d, t2_d, t8_d, lnw_d, wrel_d, wroot_d, cb_d, wo_d,
          w1_d, root_d, b1_d, wg_d, bg_d, out_d):
    with ExitStack() as ctx:
        def sb(name, shape, dt):
            return ctx.enter_context(nc.sbuf_tensor(name, shape, dt))

        def ps(name, shape, dt):
            return ctx.enter_context(nc.psum_tensor(name, shape, dt))

        def sem(name):
            return ctx.enter_context(nc.semaphore(name))

        x = sb("x", [P, NT, D], F32)
        u_mem = sb("u_mem", [P, NT * D], F32)
        xT = sb("xT", [P, 2, DC, NPAD], F16)
        stage = sb("stage", [P, 2, DC * HALF], F32)
        wsplit = sb("wsplit", [P, 2, 2, DC * HALF], F16)
        p_mem = sb("p_mem", [P, 2 * NT * HALF], F32)
        c_mem = sb("c_mem", [P, R1 * NT * NPAD], F16)
        vec = sb("vec", [P, D], F32)
        convb = sb("convb", [P, F], F32)
        ident = sb("ident", [P, P], F32)
        iota_src = sb("iota_src", [P, NPAD], F16)
        iota_win = sb("iota_win", [P, WCOLS], F16)
        win_base = sb("win_base", [P, NWIN], F32)
        keyT = sb("keyT", [EC, CH, 3], F32)
        ones = sb("ones", [P, 1], F16)
        eps = sb("eps", [P, 2], F32)
        table = sb("table", [1, NWIN, 5], I32)
        most = sb("most", [1, 1], I32)
        rcnt0 = sb("rcnt0", [P, R0, NT], F32)
        rcnt = sb("rcnt", [P, NT], F32)
        sc = sb("sc", [P, 4, 4], I32)
        rows = sb("rows", [P, 2, 4, NT], I32)
        lnsc = sb("lnsc", [P, 4], I32)
        am = sb("am", [P, 2], F32)
        ar = sb("ar", [P, 2], F32)
        lnmax = sb("lnmax", [P, 1], F32)
        rowmax = sb("rowmax", [P, 2, NT], F32)
        ss = sb("ss", [P, NT], F32)
        std = sb("std", [P, 3, NT], F32)
        rstd = sb("rstd", [P, 3, NT], F32)
        stats = sb("stats", [P, 2, NT, 2, 6], F32)
        mv = sb("mv", [P, 2, NT, 2], F32)
        coef0 = sb("coef0", [P, R0, NT], F32)
        coef = sb("coef", [P, NT], F32)
        cy = sb("cy", [P, NT], F32)
        cz = sb("cz", [P, 2, NT], F32)
        ci = sb("ci", [P, 4], F32)

        u = u_mem[:, :].rearrange("p (t d) -> p t d", t=NT)
        w_cnt = R0 * NT * NPAD // 2
        cnt2 = u_mem[:, 0:w_cnt].bitcast(F16).rearrange("p (r s n) -> p r s n", r=R0, s=NT)
        yT = u_mem[:, w_cnt:w_cnt + FC * NPAD].bitcast(F16).rearrange("p (a c n) -> p a c n", a=2, c=FC)
        cnt8 = c_mem[:, :].rearrange("p (r s n) -> p r s n", r=R1, s=NT)
        us = c_mem[:, 0:2 * NT * D].bitcast(F32).rearrange("p (t d) -> p t d", t=NT)
        uT = c_mem[:, 2 * NT * D:4 * NT * D].rearrange("p (a c n) -> p a c n", a=2, c=DC)
        w_src = RING * 2 * NPAD // 2
        src_mem = p_mem[0:EC, 0:w_src].bitcast(F16)
        win_mem = p_mem[0:EC, w_src:w_src + RING * WCOLS].bitcast(F16)
        ring_src = src_mem.rearrange("p (q e n) -> p q e n", q=RING, e=2)
        ring_win = win_mem.rearrange("p (q e n) -> p q e n", q=RING, e=2)
        oh_src = src_mem[:, 0:2 * MEET * NPAD].rearrange("p (b k n) -> p b k n", b=2, k=MEET)
        oh_win = win_mem[:, 0:2 * MEET * WCOLS].rearrange("p (b k n) -> p b k n", b=2, k=MEET)
        st_mem = stage[:, :, :].rearrange("p s w -> p (s w)")
        w_q = NT * R0 * F // 2
        q_part = [st_mem[:, a * w_q:(a + 1) * w_q].bitcast(F16).rearrange("p (s f) -> p s f", s=NT) for a in range(2)]
        acc0 = st_mem[:, 2 * w_q:2 * w_q + NT * FPAD].rearrange("p (t f) -> p t f", t=NT)
        wo_at = 2 * DC * HALF - FC * D
        sp_mem = wsplit[:, :, :, :].rearrange("p s a w -> p (s a w)")
        xs = sp_mem[:, 0:2 * NT * D].bitcast(F32).rearrange("p (t d) -> p t d", t=NT)
        elu_tmp = sp_mem[:, 0:4 * F].bitcast(F32).rearrange("p (b f) -> p b f", b=2)
        wo_tmp = p_mem[:, 0:2 * HALF].rearrange("p (b f) -> p b f", b=2)
        w_p = NT * HALF
        p_part = [[p_mem[:, s * w_p + a * w_p // 2:s * w_p + (a + 1) * w_p // 2].bitcast(F16).rearrange(
            "p (t f) -> p t f", t=NT) for a in range(2)] for s in range(2)]
        zx = [p_mem[:, s * w_p:(s + 1) * w_p].rearrange("p (t f) -> p t f", t=NT) for s in range(2)]
        e_at = DC * F3
        edges = st_mem[0:CP, e_at:e_at + 4 * 2 * EC].bitcast(I32).rearrange("p (a h e) -> p a h e", a=4, h=2)
        w_ekey, w_wtmp = 3 * 2 * EC, 24 * NWIN
        ekey = u_mem[0:CP, w_cnt:w_cnt + w_ekey].rearrange("p (a h e) -> p a h e", a=3, h=2)
        wtmp = u_mem[0:CP, w_cnt + w_ekey:w_cnt + w_ekey + w_wtmp].rearrange("p (a j) -> p a j", a=24)
        ctmp = u_mem[0:CP, w_cnt + w_ekey + w_wtmp:w_cnt + w_ekey + w_wtmp + 16].rearrange("p (a h) -> p a h", a=8)
        sc_f, rows_f, lnsc_f = sc[:, :, :].bitcast(F32), rows[:, :, :, :].bitcast(F32), lnsc[:, :].bitcast(F32)

        psP = ps("psP", [P, NT, 512], F32)
        psA = ps("psA", [P, 2, 512], F32)
        psC = ps("psC", [P, 512], F32)

        x_padded = sem("x_padded")
        x_loaded = sem("x_loaded")
        edges_loaded = sem("edges_loaded")
        lnw_loaded = sem("lnw_loaded")
        bias_loaded = sem("bias_loaded")
        gate_bias_loaded = sem("gate_bias_loaded")
        convb_loaded = sem("convb_loaded")
        stage_full = [sem(f"stage_full{s}") for s in range(2)]
        wo_tail_loaded = sem("wo_tail_loaded")
        consts_ready = sem("consts_ready")
        pool_steps = sem("pool_steps")
        pool_turns = sem("pool_turns")
        dve_steps = sem("dve_steps")
        act_steps = sem("act_steps")
        keys_ready = sem("keys_ready")
        keys_turned = sem("keys_turned")
        keyT_ready = sem("keyT_ready")
        bounds_ready = sem("bounds_ready")
        bounds_max = sem("bounds_max")
        table_ready = sem("table_ready")
        onehot_free = sem("onehot_free")
        onehot_ready = sem("onehot_ready")
        chunk_ready = sem("chunk_ready")
        win_counted = sem("win_counted")
        counts_padded = sem("counts_padded")
        win_free = sem("win_free")
        deg0_full = sem("deg0_full")
        deg_full = sem("deg_full")
        rcnt_step = sem("rcnt_step")
        sumsq_ready = sem("sumsq_ready")
        rms_std_ready = sem("rms_std_ready")
        xs_ready = sem("xs_ready")
        turned = sem("turned")
        turned_hi = sem("turned_hi")
        turned_split = sem("turned_split")
        absmax_ready = sem("absmax_ready")
        max_ready = sem("max_ready")
        scale_step = sem("scale_step")
        whi_ready = sem("whi_ready")
        wlo_ready = sem("wlo_ready")
        w_used = sem("w_used")
        wo_padded = sem("wo_padded")
        q_full = sem("q_full")
        q_hi = sem("q_hi")
        q_done = sem("q_done")
        acc_padded = sem("acc_padded")
        agg0_full = sem("agg0_full")
        agg0_done = sem("agg0_done")
        elu_neg = sem("elu_neg")
        elu_exp = sem("elu_exp")
        elu_done = sem("elu_done")
        y_ready = sem("y_ready")
        y_turned = sem("y_turned")
        y_hi = sem("y_hi")
        y_lo = sem("y_lo")
        cy_ready = sem("cy_ready")
        wo_full = sem("wo_full")
        wo_copied = sem("wo_copied")
        wo_added = sem("wo_added")
        ln_var = [sem(f"ln_var{k}") for k in range(2)]
        ln_std = [sem(f"ln_std{k}") for k in range(2)]
        x1_ready = sem("x1_ready")
        p_full = sem("p_full")
        p_hi = sem("p_hi")
        p_done = sem("p_done")
        coef_ready = sem("coef_ready")
        agg_full = sem("agg_full")
        agg_done = sem("agg_done")
        row_scaled = sem("row_scaled")
        us_ready = sem("us_ready")
        tanh_ready = sem("tanh_ready")
        z_full = sem("z_full")
        z_done = sem("z_done")
        out_ready = sem("out_ready")
        out_stored = sem("out_stored")

        block = ctx.enter_context(nc.Block())

        def unit_weights(i, slot):
            st, hi, lo = flat_weights(i, slot)
            c = FC if i == U_WO else DC
            return [v.rearrange("p (c f) -> p c f", c=c) for v in (st, hi, lo)]

        def flat_weights(i, slot):
            n = DC * F3 if i == U_W0 else FC * D if i == U_WO else DC * HALF
            if i == U_W0:
                return st_mem[:, 0:n], sp_mem[:, 0:n], sp_mem[:, n:2 * n]
            st = st_mem[:, wo_at:wo_at + n] if i == U_WO else stage[:, slot, :]
            return st, wsplit[:, slot, 0, 0:n], wsplit[:, slot, 1, 0:n]

        def scale_col(i, slot):
            return i if i <= U_WO else 2 + slot

        def block_start(t, h):
            return AHEAD + (2 * t + h) * BLOCK

        def by_twos(engine, j0, j1, window):
            if j1 - j0 > 2:
                with engine.Fori(0, (j1 - j0) // 2) as it:
                    for b in range(2):
                        window(2 * it + (j0 + b), (j0 + b) % 2)
                j0 = j1 - (j1 - j0) % 2
            for j in range(j0, j1):
                window(j, j % 2)

        REL = U_REL

        def slot_load(i):
            return 16 * (i // 2) + 48 if i % 2 == 0 else 16 * (i // 2 + 1)

        @block.sync
        def _(sp):
            for a, v in enumerate((src_d, dst_d, t8_d, t2_d)):
                sp.dma_start(edges[:, a, :, :], v.rearrange("(h p e) -> p h e", p=CP, e=EC)).then_inc(edges_loaded, 16)
            sp.dma_start(x[:, 0:NT - 1, :], x_d[0:(NT - 1) * P, :].rearrange("(t p) d -> p t d", p=P)).then_inc(x_loaded, 16)
            sp.wait_ge(x_padded, 1)
            sp.dma_start(x[0:TAIL, NT - 1, :], x_d[(NT - 1) * P:NODES, :]).then_inc(x_loaded, 16)
            sp.dma_start(vec[:, :], lnw_d.partition_broadcast(P)).then_inc(lnw_loaded, 16)

            def by_chunk(v):
                return v.rearrange("(c p) f -> p c f", p=P)

            st0 = unit_weights(U_W0, 0)[0]
            for n, v in enumerate((wroot_d, wrel_d[0], wrel_d[1])):
                sp.dma_start(st0[:, :, n * F:(n + 1) * F], by_chunk(v)).then_inc(stage_full[0], 16)
            sp.dma_start(convb[:, :], cb_d.partition_broadcast(P)).then_inc(convb_loaded, 16)
            sp.wait_ge(xs_ready, NT)
            sp.dma_start(vec[:, :], b1_d.partition_broadcast(P)).then_inc(bias_loaded, 16)

            def load(i, slot, src):
                sp.wait_ge(wlo_ready, i - 1)
                sp.dma_start(unit_weights(REL, slot)[0], src).then_inc(stage_full[slot], 16)

            sp.wait_ge(wlo_ready, 1)
            sp.wait_ge(wo_padded, 1)
            st_wo = unit_weights(U_WO, 1)[0]
            sp.dma_start(st_wo[:, 0:FC - 1, :], by_chunk(wo_d[0:(FC - 1) * P, :])).then_inc(stage_full[1], 16)
            sp.dma_start(st_wo[0:F - (FC - 1) * P, FC - 1, :], wo_d[(FC - 1) * P:F, :]).then_inc(wo_tail_loaded, 16)
            sp.wait_ge(y_turned, NT)
            for h in range(2):
                load(U_ROOT + h, h, by_chunk(root_d[:, h * HALF:(h + 1) * HALF]))
            w1_v = w1_d.rearrange("r (c p) f -> p (r c) f", p=P)
            with sp.Fori(0, R1) as r:
                for h in range(2):
                    load(U_REL + 2 * r + h, h, w1_v[:, bass.ts(r, DC), h * HALF:(h + 1) * HALF])
            sp.wait_ge(p_done, 2 * NT)
            sp.dma_start(vec[:, :], bg_d.partition_broadcast(P)).then_inc(gate_bias_loaded, 16)
            for k, top in ((U_GX, D), (U_GU, 0)):
                for h in range(2):
                    load(k + h, h, by_chunk(wg_d[top:top + D, h * HALF:(h + 1) * HALF]))
            for t in range(NT):
                n = P if t < NT - 1 else TAIL
                sp.wait_ge(out_ready, t + 1)
                sp.dma_start(out_d[t * P:t * P + n, :], x[0:n, t, :]).then_inc(out_stored, 16)
            sp.wait_ge(out_stored, 16 * NT)

        @block.gpsimd
        def _(pool):
            nc.gpsimd.memset(x[:, NT - 1, :], 0.0).then_inc(x_padded, 1)
            nc.gpsimd.memset(ident[:, :], 0.0).then_inc(pool_steps, 1)
            pool.wait_ge(pool_steps, 1)
            nc.gpsimd.affine_select(out=ident[:, :], in_=ident[:, :], compare_op=ALU.not_equal, fill=1.0, base=0,
                                    pattern=[[-1, P]], channel_multiplier=1).then_inc(consts_ready, 1)
            loose = dict(channel_multiplier=0, allow_small_or_imprecise_dtypes=True)
            nc.gpsimd.iota(win_base[:, :], pattern=[[16 * WIN, NWIN]], base=0, **loose).then_inc(consts_ready, 1)
            nc.gpsimd.iota(ctmp[:, 0, :], pattern=[[-CP, 2]], base=200, channel_multiplier=-1,
                           allow_small_or_imprecise_dtypes=True).then_inc(consts_ready, 1)
            nc.gpsimd.iota(ctmp[:, 1, :], pattern=[[CP, 2]], base=1, channel_multiplier=1,
                           allow_small_or_imprecise_dtypes=True).then_inc(consts_ready, 1)
            nc.gpsimd.iota(iota_src[:, :], pattern=[[1, NPAD]], base=0, **loose).then_inc(consts_ready, 1)
            nc.gpsimd.iota(iota_win[:, 0:WIN * R1].rearrange("p (w r) -> p w r", r=R1), pattern=[[16, WIN], [1, R1]],
                           base=0, **loose).then_inc(consts_ready, 1)
            nc.gpsimd.iota(iota_win[:, WIN * R1:WCOLS].rearrange("p (w r) -> p w r", r=R0), pattern=[[16, WIN], [1, R0]],
                           base=0, **loose).then_inc(consts_ready, 1)
            nc.gpsimd.memset(ones[:, :], 1.0).then_inc(consts_ready, 1)
            nc.gpsimd.memset(eps[:, 0:1], EPS_RMS).then_inc(consts_ready, 1)
            nc.gpsimd.memset(eps[:, 1:2], EPS_LN).then_inc(consts_ready, 1)
            nc.gpsimd.memset(wtmp[:, 22, :], 1.0).then_inc(consts_ready, 1)
            nc.gpsimd.memset(cnt8[:, :, :, NPAD - WPAD:NPAD], 0.0).then_inc(counts_padded, 1)
            nc.gpsimd.memset(cnt2[:, :, :, NPAD - WPAD:NPAD], 0.0).then_inc(counts_padded, 1)
            pool.wait_ge(bounds_ready, 1)
            nc.gpsimd.partition_all_reduce(wtmp[:, 10:12, :].rearrange("p a j -> p (a j)"),
                                           wtmp[:, 8:10, :].rearrange("p a j -> p (a j)"), CP, RMAX).then_inc(bounds_max, 1)

            def unit_max(i, slot):
                pool.wait_ge(absmax_ready, i + 1)
                pool.sem_inc(pool_turns, 1)
                nc.gpsimd.partition_all_reduce(ar[:, slot:slot + 1], am[:, slot:slot + 1], P, RMAX).then_inc(max_ready, 1)

            unit_max(U_W0, 0)
            pool.wait_ge(wlo_ready, 1)
            nc.gpsimd.memset(unit_weights(U_WO, 1)[0][:, FC - 1, :], 0.0).then_inc(wo_padded, 1)
            unit_max(U_WO, 1)
            with pool.Fori(1, UNITS // 2) as k:
                for s in range(2):
                    unit_max(2 * k + s, s)

        @block.scalar
        def _(act):
            act.wait_ge(x_loaded, 32)
            for t in range(NT):
                nc.scalar.activation(xs[:, t, :], x[:, t, :], ACT.Square, accum_out=ss[:, t:t + 1]).then_inc(sumsq_ready, 1)
            act.wait_ge(sumsq_ready, NT)
            act.wait_ge(consts_ready, 11)
            nc.scalar.activation(std[:, 0, :], ss[:, :], ACT.Sqrt, bias=eps[:, 0:1], scale=1.0 / D).then_inc(rms_std_ready, 1)

            def split_hi(k, t, dst, gain):
                for g in range(2):
                    n = 2 * NT * k + 2 * t + g
                    act.wait_ge(turned, n + 1)
                    nc.scalar.activation(dst[:, 0, 4 * g:4 * g + 4, t * P:(t + 1) * P],
                                         psA[:, g, :].rearrange("p (c n) -> p c n", c=4),
                                         ACT.Copy, scale=gain).then_inc(turned_hi, 1)

            def weight_hi(i, slot, shape_of=None):
                j = shape_of if shape_of is not None else i
                st, hi, _ = flat_weights(j, slot)
                act.wait_ge(scale_step, 4 * i + 4)
                if j == U_WO:
                    act.wait_ge(w_used, 1)
                elif j != U_W0:
                    act.wait_ge(w_used, i - 1)
                nc.scalar.activation(hi, st, ACT.Copy, scale=sc_f[:, scale_col(j, slot), 2:3]).then_inc(whi_ready, 1)

            act.wait_ge(table_ready, 1)
            most_chunks = act.value_load(most[0:1, 0:1], min_val=1, max_val=CH)

            def copy_window(j, b):
                for bank, s0, s1 in ((2 * b, 0, 3), (2 * b + 1, 3, NT)):
                    w = psP[:, bank, 0:(s1 - s0) * WCOLS].rearrange("p (s k) -> p s k", k=WCOLS)
                    w8 = w[:, :, 0:WIN * R1].rearrange("p s (w r) -> p s r w", r=R1)
                    w2 = w[:, :, WIN * R1:WCOLS].rearrange("p s (w r) -> p s r w", r=R0)
                    o8 = cnt8[:, :, s0:s1, bass.ts(j, WIN)].rearrange("p r s w -> p s r w")
                    o2 = cnt2[:, :, s0:s1, bass.ts(j, WIN)].rearrange("p r s w -> p s r w")
                    nc.scalar.activation(o8, w8, ACT.Copy)
                    last = nc.scalar.activation(o2, w2, ACT.Copy)
                last.then_inc(win_free, 1)

            def copy_windows(j0, j1):
                def few(j, b):
                    act.wait_ge(win_counted, j + 1 + 2)
                    copy_window(j, b)

                def any_number(j, b):
                    after = act.value_load(table[0:1, j, 3:4], min_val=1, max_val=CH * NWIN)
                    act.wait_ge(onehot_free, after + RING)
                    copy_window(j, b)
                with act.If(most_chunks <= MEET):
                    by_twos(act, j0, j1, few)
                with act.Else():
                    by_twos(act, j0, j1, any_number)

            def q_high(t, h):
                act.wait_ge(q_full, 2 * t + h + 1)
                src, cols = ((psA[:, 0, F:FH], slice(0, FH - F)), (psA[:, 1, 0:FH], slice(FH - F, F3 - F)))[h]
                nc.scalar.activation(q_part[0][:, t, cols], src, ACT.Copy, scale=PROD_GAIN).then_inc(q_hi, 1)

            split_hi(0, 0, xT, 1.0)
            copy_windows(0, 1)
            split_hi(0, 1, xT, 1.0)
            split_hi(0, 2, xT, 1.0)
            copy_windows(1, 2)
            split_hi(0, 3, xT, 1.0)
            split_hi(0, 4, xT, 1.0)
            weight_hi(U_W0, 0)
            copy_windows(2, AHEAD)
            for t in range(NT):
                for h in range(2):
                    q_high(t, h)
                    copy_windows(block_start(t, h), block_start(t, h + 1))
            act.wait_ge(wo_tail_loaded, 16)
            weight_hi(U_WO, 1)
            for t in range(NT):
                act.wait_ge(elu_neg, t + 1)
                nc.scalar.activation(elu_tmp[:, t % 2, :], elu_tmp[:, t % 2, :], ACT.Exp).then_inc(elu_exp, 1)
            for t in range(NT):
                act.wait_ge(y_turned, t + 1)
                if t >= 2:
                    act.wait_ge(y_lo, t - 1)
                nc.scalar.activation(yT[:, 0, :, t * P:(t + 1) * P],
                                     psA[:, t % 2, 0:FPAD].rearrange("p (c n) -> p c n", c=FC), ACT.Copy).then_inc(y_hi, 1)

            def wo_copy(t):
                for n in range(2 * t, 2 * t + 2):
                    act.wait_ge(wo_full, n + 1)
                    act.wait_ge(cy_ready, 1)
                    if n >= 2:
                        act.wait_ge(wo_added, n - 1)
                    nc.scalar.activation(wo_tmp[:, n % 2, :], psP[:, n % NT, :], ACT.Copy, scale=cy[:, t:t + 1]).then_inc(wo_copied, 1)

            def ln_deviation(k, t):
                act.wait_ge(ln_var[k], t + 1)
                nc.scalar.activation(std[:, 1 + k, t:t + 1], mv[:, k, t, 1:2], ACT.Sqrt, bias=eps[:, 1:2]).then_inc(ln_std[k], 1)

            wo_copy(0)
            for t in range(NT):
                if t + 1 < NT:
                    wo_copy(t + 1)
                ln_deviation(0, t)
                if t == 2:
                    weight_hi(U_ROOT, 0)
                if t >= 1:
                    split_hi(1, t - 1, xT, X_GAIN)
            split_hi(1, NT - 1, xT, X_GAIN)

            def p_high(i, slot, tiles, first=False):
                j = i - U_REL
                for t in tiles:
                    act.wait_ge(p_full, NT * (i - U_ROOT) + t + 1)
                    if t == 0 and not first:
                        act.wait_ge(agg_full, NT * (j - 1))
                    nc.scalar.activation(p_part[slot][0][:, t, :], psP[:, t, :], ACT.Copy, scale=PROD_GAIN).then_inc(p_hi, 1)

            weight_hi(U_ROOT + 1, 1)
            weight_hi(U_REL, 0)

            def rel_step(i, slot, first=False):
                p_high(i, slot, range(0, 2), first)
                weight_hi(i + 1, 1 - slot, shape_of=REL)
                p_high(i, slot, range(2, NT), first)

            rel_step(U_REL, 0, first=True)
            rel_step(U_REL + 1, 1, first=True)
            rel_step(U_REL + 2, 0)
            with act.Fori(0, R1 - 2) as k:
                for s in range(2):
                    rel_step(U_REL + 3 + 2 * k + s, 1 - s)
            rel_step(U_GX - 1, 1)
            weight_hi(U_GX + 1, 1)
            act.wait_ge(row_scaled, 1)
            for t in range(NT):
                nc.scalar.activation(us[:, t, :], u[:, t, :], ACT.Copy, scale=rows_f[:, 1, 2, t:t + 1]).then_inc(us_ready, 1)
            weight_hi(U_GU, 0)
            for t in range(NT):
                act.wait_ge(us_ready, t + 1)
                nc.scalar.activation(u[:, t, :], u[:, t, :], ACT.Tanh).then_inc(tanh_ready, 1)
            split_hi(2, 0, uT, 1.0)
            weight_hi(U_GU + 1, 1)
            split_hi(2, 1, uT, 1.0)
            for t in range(NT):
                if t + 2 < NT:
                    split_hi(2, t + 2, uT, 1.0)
                ln_deviation(1, t)

        @block.tensor
        def _(pe):
            pe.wait_ge(consts_ready, 1)
            pe.wait_ge(keys_ready, 5)
            for a in range(3):
                for h in range(2):
                    last = nc.tensor.transpose(psC[0:EC, (2 * a + h) * CP:(2 * a + h + 1) * CP], ekey[:, a, h, :], ident[0:CP, 0:CP])
            last.then_inc(keys_turned, 1)

            def turn(k, t, src, ready):
                pe.wait_ge(ready, t + 1)
                for g in range(2):
                    n = 2 * NT * k + 2 * t + g
                    if n >= 2:
                        pe.wait_ge(turned_split, n - 1)
                    for c in range(4):
                        last = nc.tensor.transpose(psA[:, g, c * P:(c + 1) * P],
                                                   src[:, t, (4 * g + c) * P:(4 * g + c + 1) * P], ident[:, :])
                    last.then_inc(turned, 1)

            pe.wait_ge(table_ready, 1)
            most_chunks = pe.value_load(most[0:1, 0:1], min_val=1, max_val=CH)

            def count_chunk(b, src, win, first):
                for s in range(NT):
                    col = (s % 3) * WCOLS
                    last = nc.tensor.matmul(psP[:, 2 * b + s // 3, col:col + WCOLS], src[:, s * P:(s + 1) * P], win,
                                            start=(first and s % 3 == 0), stop=False, skip_group_check=True)
                return last

            def count_pair(b, slot, first):
                count_chunk(b, ring_src[:, slot, 0, :], ring_win[:, slot, 0, :], first)
                return count_chunk(b, ring_src[:, slot, 1, :], ring_win[:, slot, 1, :], False)

            def count_windows(j0, j1):
                def few(j, b):
                    pe.wait_ge(win_free, j + 1)
                    for k in range(MEET):
                        pe.wait_ge(chunk_ready, MEET * j + k + 1)
                        last = count_chunk(b, oh_src[:, b, k, :], oh_win[:, b, k, :], k == 0)
                    last.then_inc(win_counted, 1)

                def any_number(j, b):
                    pairs = pe.value_load(table[0:1, j, 1:2], min_val=PAIRS, max_val=CP)
                    before = pe.value_load(table[0:1, j, 2:3], min_val=0, max_val=CP * NWIN)
                    pe.wait_ge(win_free, j + 1)
                    pe.wait_ge(onehot_ready, before + 1)
                    count_pair(b, before % RING, True).then_inc(onehot_free, 1)
                    with pe.Fori(1, pairs) as p:
                        pe.wait_ge(onehot_ready, before + p + 1)
                        count_pair(b, (before + p) % RING, False).then_inc(onehot_free, 1)
                with pe.If(most_chunks <= MEET):
                    by_twos(pe, j0, j1, few)
                with pe.Else():
                    by_twos(pe, j0, j1, any_number)

            def product(out, lhs, i, slot, t, cols):
                _, hi, lo = unit_weights(i, slot)
                chunks = FC if i == U_WO else DC
                for c in range(chunks):
                    for a, w, first in ((0, hi, c == 0), (0, lo, False), (1, hi, False)):
                        last = nc.tensor.matmul(out, lhs[:, a, c, t * P:(t + 1) * P], w[:, c, cols],
                                                start=first, stop=(c == chunks - 1 and a == 1))
                return last

            def weights_ready(i):
                pe.wait_ge(whi_ready, i + 1)
                pe.wait_ge(wlo_ready, i + 1)

            def first_products(t, h):
                if t == 0:
                    weights_ready(U_W0)
                    pe.wait_ge(turned_split, 2 * NT)
                else:
                    pe.wait_ge(q_done, 3 * t - 1 + h)
                product(psA[:, h, 0:FH], xT, U_W0, 0, t, slice(h * FH, (h + 1) * FH)).then_inc(q_full, 1)

            turn(0, 0, xs, xs_ready)
            count_windows(0, 1)
            turn(0, 1, xs, xs_ready)
            turn(0, 2, xs, xs_ready)
            count_windows(1, 2)
            turn(0, 3, xs, xs_ready)
            turn(0, 4, xs, xs_ready)
            count_windows(2, AHEAD)
            for t in range(NT):
                for h in range(2):
                    first_products(t, h)
                    count_windows(block_start(t, h), block_start(t, h + 1))

            degrees = psC[:, 0:(R1 + R0) * NT].rearrange("p (r t) -> p r t", t=NT)

            def degree(r, counts):
                for t in range(NT):
                    for s in range(NT):
                        last = nc.tensor.matmul(degrees[:, r, t:t + 1], counts[:, s, t * P:(t + 1) * P], ones[:, :],
                                                start=(s == 0), stop=(s == NT - 1))
                return last

            pe.wait_ge(win_free, NWIN + 2)
            pe.wait_ge(keyT_ready, 1)
            pe.wait_ge(counts_padded, 2)
            for r in range(R0):
                last = degree(R1 + r, cnt2[:, r, :, :])
            last.then_inc(deg0_full, 1)
            pe.wait_ge(q_full, 2 * NT)
            pe.sem_inc(w_used, 1)

            pe.wait_ge(q_done, 3 * NT)
            for t in range(NT):
                for r in range(R0):
                    n = R0 * t + r
                    if n >= 4:
                        pe.wait_ge(agg0_done, n - 3)
                    for s in range(NT):
                        for a in range(2):
                            last = nc.tensor.matmul(psP[:, n % 4, 0:F], cnt2[:, r, s, t * P:(t + 1) * P],
                                                    q_part[a][:, s, r * F:(r + 1) * F],
                                                    start=(s == 0 and a == 0), stop=(s == NT - 1 and a == 1))
                    last.then_inc(agg0_full, 1)
            for t in range(NT):
                pe.wait_ge(y_ready, t + 1)
                if t >= 2:
                    pe.wait_ge(y_lo, t - 1)
                for c in range(FC):
                    last = nc.tensor.transpose(psA[:, t % 2, c * P:(c + 1) * P], acc0[:, t, c * P:(c + 1) * P], ident[:, :])
                last.then_inc(y_turned, 1)
            weights_ready(U_WO)
            pe.wait_ge(agg0_done, R0 * NT)

            def wo_product(t):
                pe.wait_ge(y_hi, t + 1)
                pe.wait_ge(y_lo, t + 1)
                for h in range(2):
                    n = 2 * t + h
                    if n >= NT:
                        pe.wait_ge(wo_copied, n - NT + 1)
                    last = product(psP[:, n % NT, :], yT, U_WO, 1, t, slice(h * HALF, (h + 1) * HALF))
                    last.then_inc(wo_full, 1)

            def tile_product(i, slot, t, first=False):
                if not first:
                    pe.wait_ge(p_done, NT * (i - U_ROOT - 1) + t + 1)
                product(psP[:, t, :], xT, REL, slot, t, slice(0, HALF)).then_inc(p_full, 1)

            def unit_used(i):
                pe.wait_ge(p_full, NT * (i - U_ROOT + 1))
                pe.sem_inc(w_used, 1)

            def root_product(t):
                if t == 0:
                    pe.wait_ge(wo_copied, 2 * NT)
                    weights_ready(U_ROOT)
                pe.wait_ge(turned_split, 2 * NT + 2 * t + 2)
                tile_product(U_ROOT, 0, t, first=True)

            wo_product(0)
            wo_product(1)
            wo_product(2)
            turn(1, 0, x, x1_ready)
            wo_product(3)
            turn(1, 1, x, x1_ready)
            wo_product(4)
            pe.wait_ge(wo_full, 2 * NT)
            pe.sem_inc(w_used, 1)
            for t in range(2, NT):
                turn(1, t, x, x1_ready)
                root_product(t - 2)
            root_product(NT - 2)
            root_product(NT - 1)
            unit_used(U_ROOT)

            def products(i, slot):
                weights_ready(i)
                for t in range(NT):
                    tile_product(i, slot, t)
                unit_used(i)

            def aggregate(j, r, h, first=False):
                pe.wait_ge(p_done, NT * (j + U_REL - U_ROOT + 1))
                for t in range(NT):
                    if not (first and t < 2):
                        pe.wait_ge(agg_done, NT * j + t - 1)
                    for s in range(NT):
                        for a in range(2):
                            last = nc.tensor.matmul(psA[:, (NT * h + t) % 2, :], cnt8[:, r, s, t * P:(t + 1) * P],
                                                    p_part[h][a][:, s, :], start=(s == 0 and a == 0), stop=(s == NT - 1 and a == 1))
                    last.then_inc(agg_full, 1)

            def degree8(r):
                degree(r, cnt8[:, r, :, :]).then_inc(deg_full, 1)

            products(U_ROOT + 1, 1)
            pe.wait_ge(turned_split, 4 * NT)
            products(U_REL, 0)
            degree8(0)
            products(U_REL + 1, 1)
            aggregate(0, 0, 0, first=True)
            products(U_REL + 2, 0)
            aggregate(1, 0, 1)
            with pe.Fori(0, R1 - 2) as k:
                degree8(k + 1)
                products(U_REL + 3 + 2 * k, 1)
                aggregate(2 + 2 * k, k + 1, 0)
                products(U_REL + 4 + 2 * k, 0)
                aggregate(3 + 2 * k, k + 1, 1)
            degree8(R1 - 1)
            products(U_GX - 1, 1)
            aggregate(2 * R1 - 2, R1 - 1, 0)
            products(U_GX, 0)
            aggregate(2 * R1 - 1, R1 - 1, 1)
            products(U_GX + 1, 1)

            pe.wait_ge(p_done, NT * (U_GU - U_ROOT))
            pe.wait_ge(agg_done, NT * 2 * R1)

            def gate_product(t):
                pe.wait_ge(turned_hi, 4 * NT + 2 * t + 2)
                pe.wait_ge(turned_split, 4 * NT + 2 * t + 2)
                for h in range(2):
                    n = 2 * t + h
                    if t == 0:
                        weights_ready(U_GU + h)
                    if n >= NT:
                        pe.wait_ge(z_done, n - NT + 1)
                    product(psP[:, n % NT, :], uT, REL, h, t, slice(0, HALF)).then_inc(z_full, 1)

            turn(2, 0, us, us_ready)
            for t in range(NT):
                if t + 1 < NT:
                    turn(2, t + 1, us, us_ready)
                gate_product(t)

        @block.vector
        def _(dve):
            steps = [0]

            def step(ins):
                steps[0] += 1
                ins.then_inc(dve_steps, 1)
                dve.wait_ge(dve_steps, steps[0])

            ts, stt, tt = nc.vector.tensor_scalar, nc.vector.scalar_tensor_tensor, nc.vector.tensor_tensor

            def exponents(dst, bits):
                return (lambda: ts(dst[0], bits, EXP_MASK, None, ALU.bitwise_and),
                        lambda: ts(dst[1], dst[0], float(EXP_LEAST * EXP_ONE), None, ALU.max),
                        lambda: ts(dst[2], dst[1], -1.0, float((254 + TOP) * EXP_ONE), ALU.mult, ALU.add),
                        lambda: ts(dst[3], dst[1], float(TOP * EXP_ONE), None, ALU.subtract))

            def row_scales(dst, bits, ready=None):
                *chain, last = exponents(dst, bits)
                for f in chain:
                    step(f())
                if ready:
                    last().then_inc(ready, 1)
                    dve.wait_ge(ready, 1)
                else:
                    step(last())

            dve.wait_ge(edges_loaded, 64)
            nc.vector.tensor_copy(ekey[:, 0, :, :], edges[:, 0, :, :]).then_inc(keys_ready, 1)
            stt(ekey[:, 1, :, :], edges[:, 1, :, :], 16.0, edges[:, 2, :, :], ALU.mult, ALU.add).then_inc(keys_ready, 1)
            stt(ekey[:, 2, :, :], edges[:, 1, :, :], 16.0, edges[:, 3, :, :], ALU.mult, ALU.add).then_inc(keys_ready, 1)
            nc.vector.tensor_reduce(ctmp[:, 2, :], edges[:, 1, :, :], AX.X, ALU.min).then_inc(keys_ready, 1)
            nc.vector.tensor_reduce(ctmp[:, 3, :], edges[:, 1, :, :], AX.X, ALU.max).then_inc(keys_ready, 1)
            dve.wait_ge(keys_ready, 5)
            step(ts(ctmp[:, 4, :], ctmp[:, 2, :], 16.0, 16.0 * (WIN - 1), ALU.mult, ALU.subtract))
            step(ts(ctmp[:, 5, :], ctmp[:, 3, :], 16.0, None, ALU.mult))
            dve.wait_ge(consts_ready, 11)
            base = win_base[0:CP, :]
            for h in range(2):
                step(ts(wtmp[:, h, :], base, ctmp[:, 5, h:h + 1], None, ALU.is_le))
                step(stt(wtmp[:, 2 + h, :], base, ctmp[:, 4, h:h + 1], wtmp[:, h, :], ALU.is_ge, ALU.mult))
                step(ts(wtmp[:, 4 + h, :], wtmp[:, 2 + h, :], ctmp[:, 0, h:h + 1], None, ALU.mult))
                step(ts(wtmp[:, 6 + h, :], wtmp[:, 2 + h, :], ctmp[:, 1, h:h + 1], None, ALU.mult))
            step(tt(wtmp[:, 8, :], wtmp[:, 4, :], wtmp[:, 5, :], ALU.max))
            tt(wtmp[:, 9, :], wtmp[:, 6, :], wtmp[:, 7, :], ALU.max).then_inc(bounds_ready, 1)
            dve.wait_ge(keys_turned, 1)
            nc.vector.tensor_copy(keyT[:, :, :].rearrange("p k a -> p a k"),
                                  psC[0:EC, 0:3 * CH].rearrange("p (a k) -> p a k", a=3)).then_inc(keyT_ready, 1)

            dve.wait_ge(bounds_max, 1)

            def row(a):
                return wtmp[0:1, a, :]
            step(ts(row(12), row(10), -1.0, 200.0, ALU.mult, ALU.add))
            step(tt(row(13), row(11), row(12), ALU.subtract))
            pairs_i = wtmp[0:1, 14, :].bitcast(I32)
            step(ts(pairs_i, row(13), 0.5, 0.25, ALU.mult, ALU.add))
            step(ts(row(15), pairs_i, float(PAIRS), None, ALU.max))
            step(ts(row(16), row(15), -2.0, float(CH), ALU.mult, ALU.add))
            step(nc.vector.tensor_tensor_scan(row(17), row(22), row(15), 0.0, ALU.mult, ALU.add))
            step(tt(table[:, :, 0], row(12), row(16), ALU.min))
            step(nc.vector.tensor_copy(table[:, :, 1], row(15)))
            step(tt(table[:, :, 2], row(17), row(15), ALU.subtract))
            step(nc.vector.tensor_copy(table[:, :, 3], row(17)))
            step(ts(table[:, :, 4], row(12), float(CH - MEET), None, ALU.min))
            nc.vector.tensor_reduce(most[:, :], row(13), AX.X, ALU.max).then_inc(table_ready, 1)

            dve.wait_ge(lnw_loaded, 16)
            step(nc.vector.tensor_reduce(lnmax[:, :], vec[:, :], AX.X, ALU.max, apply_absolute_value=True))
            row_scales([lnsc[:, a:a + 1] for a in range(4)], lnmax[:, :].bitcast(I32))
            step(ts(vec[:, :], vec[:, :], lnsc_f[:, 2:3], LN_GAIN, ALU.mult, ALU.mult))
            def split_lo(k, t, dst, gain):
                for g in range(2):
                    n = 2 * NT * k + 2 * t + g
                    dve.wait_ge(turned_hi, n + 1)
                    hi = dst[:, 0, 4 * g:4 * g + 4, t * P:(t + 1) * P]
                    lo = dst[:, 1, 4 * g:4 * g + 4, t * P:(t + 1) * P]
                    stt(lo, psA[:, g, :].rearrange("p (c n) -> p c n", c=4), gain, hi,
                        ALU.mult, ALU.subtract).then_inc(turned_split, 1)

            def unit_absmax(i, slot, loads, shape_of=None):
                j = shape_of if shape_of is not None else i
                dve.wait_ge(stage_full[slot], loads)
                nc.vector.tensor_reduce(am[:, slot:slot + 1], flat_weights(j, slot)[0], AX.X, ALU.max,
                                        apply_absolute_value=True).then_inc(absmax_ready, 1)

            def unit_scale(i, slot, shape_of=None):
                j = shape_of if shape_of is not None else i
                c = scale_col(j, slot)
                dve.wait_ge(max_ready, i + 1)
                for k, f in enumerate(exponents([sc[:, c, a:a + 1] for a in range(4)], ar[:, slot:slot + 1].bitcast(I32))):
                    if k in (1, 2):
                        dve.wait_ge(scale_step, 4 * i + k)
                    f().then_inc(scale_step, 1)

            def unit_lo(i, slot, shape_of=None):
                j = shape_of if shape_of is not None else i
                st, hi, lo = flat_weights(j, slot)
                dve.wait_ge(whi_ready, i + 1)
                stt(lo, st, sc_f[:, scale_col(j, slot), 2:3], hi, ALU.mult, ALU.subtract).then_inc(wlo_ready, 1)

            dve.sem_inc(onehot_free, RING)
            dve.sem_inc(win_counted, 2)
            dve.sem_inc(win_free, 2)
            dve.wait_ge(table_ready, 1)
            dve.wait_ge(keyT_ready, 1)
            most_chunks = dve.value_load(most[0:1, 0:1], min_val=1, max_val=CH)
            win8 = iota_win[0:EC, 0:WIN * R1]
            win2 = iota_win[0:EC, WIN * R1:WCOLS]

            def onehot_windows(j0, j1):
                def few(j, b):
                    chunk = dve.value_load(table[0:1, j, 4:5], min_val=0, max_val=CH - MEET)
                    wb = win_base[0:EC, bass.ts(j, 1)]
                    dve.wait_ge(win_counted, j + 1)
                    for a, w, cols in ((1, win8, slice(0, WIN * R1)), (2, win2, slice(WIN * R1, WCOLS))):
                        n = w.shape[1]
                        stt(oh_win[:, b, :, cols], w.unsqueeze(1).broadcast_to([EC, MEET, n]), wb,
                            keyT[:, bass.ds(chunk, MEET), a:a + 1].broadcast_to([EC, MEET, n]), ALU.add, ALU.is_equal)
                    for k in range(MEET):
                        ts(oh_src[:, b, k, :], iota_src[0:EC, :], keyT[:, chunk + k, 0:1], None,
                           ALU.is_equal).then_inc(chunk_ready, 1)

                with dve.If(most_chunks <= MEET):
                    by_twos(dve, j0, j1, few)
                with dve.Else():
                    with dve.Fori(j0, j1) as j:
                        chunk = dve.value_load(table[0:1, j, 0:1], min_val=0, max_val=CH - 2 * PAIRS)
                        pairs = dve.value_load(table[0:1, j, 1:2], min_val=PAIRS, max_val=CP)
                        before = dve.value_load(table[0:1, j, 2:3], min_val=0, max_val=CP * NWIN)
                        with dve.Fori(0, pairs) as p:
                            q = before + p
                            dve.wait_ge(onehot_free, q + 1)
                            slot = q % RING
                            wb = win_base[0:EC, bass.ts(j, 1)]
                            for e in range(2):
                                k = (chunk + 2 * p).with_bounds(min_val=0, max_val=CH - 2) + e
                                ts(ring_src[:, slot, e, :], iota_src[0:EC, :], keyT[:, k, 0:1], None, ALU.is_equal)
                                ts(ring_win[:, slot, e, 0:WIN * R1], win8, wb, keyT[:, k, 1:2], ALU.add, ALU.is_equal)
                                last = ts(ring_win[:, slot, e, WIN * R1:WCOLS], win2, wb, keyT[:, k, 2:3],
                                          ALU.add, ALU.is_equal)
                            last.then_inc(onehot_ready, 1)

            def first_sums(t, h):
                dve.wait_ge(q_hi, 2 * t + h + 1)
                if h == 0:
                    stt(acc0[:, t, 0:F], psA[:, 0, 0:F], ci[:, 0:1], convb[:, :], ALU.mult, ALU.add).then_inc(q_done, 1)
                src, cols = ((psA[:, 0, F:FH], slice(0, FH - F)), (psA[:, 1, 0:FH], slice(FH - F, F3 - F)))[h]
                stt(q_part[1][:, t, cols], src, PROD_GAIN, q_part[0][:, t, cols], ALU.mult, ALU.subtract).then_inc(q_done, 1)

            onehot_windows(0, 1)
            dve.wait_ge(rms_std_ready, 1)
            step(nc.vector.reciprocal(rstd[:, 0, :], std[:, 0, :]))
            for t in range(NT):
                stt(xs[:, t, :], x[:, t, :], rstd[:, 0, t:t + 1], vec[:, :], ALU.mult, ALU.mult).then_inc(xs_ready, 1)
            split_lo(0, 0, xT, 1.0)
            split_lo(0, 1, xT, 1.0)
            onehot_windows(1, 2)
            split_lo(0, 2, xT, 1.0)
            split_lo(0, 3, xT, 1.0)
            unit_absmax(U_W0, 0, 48)
            split_lo(0, 4, xT, 1.0)
            unit_scale(U_W0, 0)
            onehot_windows(2, AHEAD)
            unit_lo(U_W0, 0)
            dve.wait_ge(wlo_ready, 1)
            nc.vector.memset(acc0[:, :, F:FPAD], 0.0).then_inc(acc_padded, 1)
            step(tt(ci[:, 0:1], sc_f[:, U_W0, 3:4], lnsc_f[:, 3:4], ALU.mult))
            step(ts(ci[:, 1:2], ci[:, 0:1], 1.0 / (LN_GAIN * PROD_GAIN), None, ALU.mult))
            step(ts(ci[:, 0:1], ci[:, 0:1], 1.0 / LN_GAIN, None, ALU.mult))
            dve.wait_ge(convb_loaded, 16)
            for t in range(NT):
                for h in range(2):
                    onehot_windows(block_start(t, h), block_start(t, h + 1))
                    first_sums(t, h)
                if t == 2:
                    dve.wait_ge(wo_tail_loaded, 16)
                    unit_absmax(U_WO, 1, slot_load(U_WO))
                if t == 3:
                    unit_scale(U_WO, 1)
            dve.wait_ge(deg0_full, 1)
            rc0 = rcnt0[:, :, :].rearrange("p r t -> p (r t)")
            step(ts(rc0, psC[:, R1 * NT:(R1 + R0) * NT], 1.0, None, ALU.max))
            step(nc.vector.reciprocal(rc0, rc0))
            step(ts(coef0[:, :, :].rearrange("p r t -> p (r t)"), rc0, ci[:, 1:2], None, ALU.mult))
            dve.wait_ge(acc_padded, 1)
            dve.wait_ge(q_done, 3 * NT)

            def elu_end(t):
                dve.wait_ge(elu_exp, t + 1)
                step(stt(acc0[:, t, 0:F], acc0[:, t, 0:F], 0.0, elu_tmp[:, t % 2, :], ALU.max, ALU.add))
                nc.vector.tensor_reduce(rowmax[:, 0, t:t + 1], acc0[:, t, 0:F], AX.X, ALU.max).then_inc(elu_done, 1)

            for t in range(NT):
                for r in range(R0):
                    n = R0 * t + r
                    dve.wait_ge(agg0_full, n + 1)
                    if r:
                        dve.wait_ge(agg0_done, n)
                    stt(acc0[:, t, 0:F], psP[:, n % 4, 0:F], coef0[:, r, t:t + 1], acc0[:, t, 0:F], ALU.mult, ALU.add).then_inc(agg0_done, 1)
                dve.wait_ge(agg0_done, R0 * t + R0)
                if t >= 2:
                    dve.wait_ge(elu_done, t - 1)
                ts(elu_tmp[:, t % 2, :], acc0[:, t, 0:F], 0.0, None, ALU.min).then_inc(elu_neg, 1)
                if t:
                    elu_end(t - 1)
            elu_end(NT - 1)
            dve.wait_ge(elu_done, NT)
            step(ts(rowmax[:, 0, :], rowmax[:, 0, :], 1.0, None, ALU.max))
            row_scales([rows[:, 0, a, :] for a in range(4)], rowmax[:, 0, :].bitcast(I32))
            for t in range(NT):
                ts(acc0[:, t, 0:F], acc0[:, t, 0:F], -1.0, rows_f[:, 0, 2, t:t + 1], ALU.add, ALU.mult).then_inc(y_ready, 1)
            ts(cy[:, :], rows_f[:, 0, 3, :], sc_f[:, U_WO, 3:4], None, ALU.mult).then_inc(cy_ready, 1)
            unit_lo(U_WO, 1)
            for t in range(NT):
                dve.wait_ge(y_hi, t + 1)
                tt(yT[:, 1, :, t * P:(t + 1) * P], psA[:, t % 2, 0:FPAD].rearrange("p (c n) -> p c n", c=FC),
                   yT[:, 0, :, t * P:(t + 1) * P], ALU.subtract).then_inc(y_lo, 1)

            def norm_stats(k, t, h):
                step(nc.vector.bn_stats(stats[:, k, t, h, :], x[:, t, h * HALF:(h + 1) * HALF]))

            def norm_var(k, t):
                nc.vector.bn_aggr(mv[:, k, t, :], stats[:, k, t, :, :].rearrange("p h s -> p (h s)")).then_inc(ln_var[k], 1)

            def norm_apply(k, t, ready):
                dve.wait_ge(ln_std[k], t + 1)
                dve.wait_ge(ln_var[k], t + 1)
                step(nc.vector.reciprocal(rstd[:, 1 + k, t:t + 1], std[:, 1 + k, t:t + 1]))
                ts(x[:, t, :], x[:, t, :], mv[:, k, t, 0:1], rstd[:, 1 + k, t:t + 1], ALU.subtract, ALU.mult).then_inc(ready, 1)

            for t in range(NT):
                for h in range(2):
                    n = 2 * t + h
                    dve.wait_ge(wo_copied, n + 1)
                    xv = x[:, t, h * HALF:(h + 1) * HALF]
                    stt(xv, xv, 2.0, wo_tmp[:, n % 2, :], ALU.mult, ALU.add).then_inc(wo_added, 1)
                    dve.wait_ge(wo_added, n + 1)
                    norm_stats(0, t, h)
                norm_var(0, t)
                if t == 1:
                    unit_absmax(U_ROOT, 0, slot_load(U_ROOT))
                if t:
                    norm_apply(0, t - 1, x1_ready)
                if t == 1:
                    unit_scale(U_ROOT, 0)
                if t >= 2:
                    split_lo(1, t - 2, xT, X_GAIN)
                if t == 3:
                    unit_lo(U_ROOT, 0)
            norm_apply(0, NT - 1, x1_ready)
            split_lo(1, NT - 2, xT, X_GAIN)
            split_lo(1, NT - 1, xT, X_GAIN)

            def evacuate(i, slot, t, kind, h=0):
                k = NT * (i - U_ROOT) + t + 1
                src = psP[:, t, :]
                if kind == "rel":
                    dve.wait_ge(p_hi, NT * (i - U_REL) + t + 1)
                    ins = stt(p_part[slot][1][:, t, :], src, PROD_GAIN, p_part[slot][0][:, t, :], ALU.mult, ALU.subtract)
                else:
                    dve.wait_ge(p_full, k)
                    dst = u[:, t, h * HALF:(h + 1) * HALF] if kind == "root" else zx[h][:, t, :]
                    ins = stt(dst, src, ci[:, 3:4], vec[:, h * HALF:(h + 1) * HALF], ALU.mult, ALU.add)
                ins.then_inc(p_done, 1)

            def reciprocals(r, first):
                if not first:
                    dve.wait_ge(coef_ready, 2 * r)
                dve.wait_ge(deg_full, r + 1)
                ts(rcnt[:, :], degrees[:, r, :], 1.0, None, ALU.max).then_inc(rcnt_step, 1)
                dve.wait_ge(rcnt_step, 2 * r + 1)
                nc.vector.reciprocal(rcnt[:, :], rcnt[:, :]).then_inc(rcnt_step, 1)
                dve.wait_ge(rcnt_step, 2 * r + 2)

            degrees = psC[:, 0:(R1 + R0) * NT].rearrange("p (r t) -> p r t", t=NT)

            def agg_coef(j, slot, first=False):
                if not first:
                    dve.wait_ge(agg_done, NT * j)
                ts(coef[:, :], rcnt[:, :], sc_f[:, scale_col(REL, slot), 3:4], 1.0 / (X_GAIN * PROD_GAIN),
                   ALU.mult, ALU.mult).then_inc(coef_ready, 1)

            def agg_add(j, h):
                dve.wait_ge(coef_ready, j + 1)
                for t in range(NT):
                    uv = u[:, t, h * HALF:(h + 1) * HALF]
                    dve.wait_ge(agg_full, NT * j + t + 1)
                    stt(uv, psA[:, (NT * h + t) % 2, :], coef[:, t:t + 1], uv, ALU.mult, ALU.add).then_inc(agg_done, 1)

            def plain_factor(i, slot):
                if i != U_ROOT:
                    dve.wait_ge(p_done, NT * (i - U_ROOT))
                step(ts(ci[:, 3:4], sc_f[:, scale_col(REL, slot), 3:4], 1.0 / X_GAIN, None, ALU.mult))

            def root_step(i, slot):
                plain_factor(i, slot)
                unit_absmax(i + 1, 1 - slot, slot_load(i + 1), REL)
                evacuate(i, slot, 0, "root", slot)
                unit_scale(i + 1, 1 - slot, REL)
                evacuate(i, slot, 1, "root", slot)
                unit_lo(i + 1, 1 - slot, REL)
                for t in range(2, NT):
                    evacuate(i, slot, t, "root", slot)

            def rel_step(i, slot, loads, agg=None):
                unit_absmax(i + 1, 1 - slot, loads, REL)
                if agg:
                    if slot:
                        reciprocals(agg[1], agg[2])
                    agg_coef(agg[0], 1 - slot, agg[2])
                evacuate(i, slot, 0, "rel")
                unit_scale(i + 1, 1 - slot, REL)
                evacuate(i, slot, 1, "rel")
                evacuate(i, slot, 2, "rel")
                unit_lo(i + 1, 1 - slot, REL)
                evacuate(i, slot, 3, "rel")
                evacuate(i, slot, 4, "rel")
                if agg:
                    agg_add(agg[0], 1 - slot)

            dve.wait_ge(bias_loaded, 16)
            root_step(U_ROOT, 0)
            root_step(U_ROOT + 1, 1)
            rel_step(U_REL, 0, slot_load(U_REL + 1))
            rel_step(U_REL + 1, 1, slot_load(U_REL + 2), (0, 0, True))
            rel_step(U_REL + 2, 0, slot_load(U_REL + 3), (1, 0, False))
            with dve.Fori(0, R1 - 2) as k:
                rel_step(U_REL + 3 + 2 * k, 1, slot_load(U_REL + 4) + 16 * k, (2 + 2 * k, k + 1, False))
                rel_step(U_REL + 4 + 2 * k, 0, slot_load(U_REL + 5) + 16 * k, (3 + 2 * k, k + 1, False))
            rel_step(U_GX - 1, 1, slot_load(U_GX), (2 * R1 - 2, R1 - 1, False))

            dve.wait_ge(gate_bias_loaded, 16)
            agg_coef(2 * R1 - 1, 1)
            plain_factor(U_GX, 0)
            unit_absmax(U_GX + 1, 1, slot_load(U_GX + 1))
            evacuate(U_GX, 0, 0, "gate", 0)
            unit_scale(U_GX + 1, 1)
            evacuate(U_GX, 0, 1, "gate", 0)
            evacuate(U_GX, 0, 2, "gate", 0)
            unit_lo(U_GX + 1, 1)
            evacuate(U_GX, 0, 3, "gate", 0)
            evacuate(U_GX, 0, 4, "gate", 0)
            unit_absmax(U_GU, 0, slot_load(U_GU))
            unit_scale(U_GU, 0)
            agg_add(2 * R1 - 1, 1)
            plain_factor(U_GX + 1, 1)
            dve.wait_ge(agg_done, 2 * R1 * NT)
            for t in range(NT):
                step(nc.vector.tensor_reduce(rowmax[:, 1, t:t + 1], u[:, t, :], AX.X, ALU.max, apply_absolute_value=True))
            row_scales([rows[:, 1, a, :] for a in range(4)], rowmax[:, 1, :].bitcast(I32), row_scaled)
            unit_lo(U_GU, 0)
            step(ts(cz[:, 0, :], rows_f[:, 1, 3, :], sc_f[:, scale_col(REL, 0), 3:4], None, ALU.mult))
            unit_absmax(U_GU + 1, 1, slot_load(U_GU + 1))
            for t in range(NT):
                evacuate(U_GX + 1, 1, t, "gate", 1)
            unit_scale(U_GU + 1, 1)
            split_lo(2, 0, uT, 1.0)
            unit_lo(U_GU + 1, 1)
            dve.wait_ge(scale_step, 4 * UNITS)
            step(ts(cz[:, 1, :], rows_f[:, 1, 3, :], sc_f[:, scale_col(REL, 1), 3:4], None, ALU.mult))
            for t in range(NT):
                if t + 1 < NT:
                    split_lo(2, t + 1, uT, 1.0)
                dve.wait_ge(tanh_ready, t + 1)
                step(tt(u[:, t, :], u[:, t, :], x[:, t, :], ALU.subtract))
                for h in range(2):
                    n = 2 * t + h
                    cols = slice(h * HALF, (h + 1) * HALF)
                    dve.wait_ge(z_full, n + 1)
                    stt(zx[h][:, t, :], psP[:, n % NT, :], cz[:, h, t:t + 1], zx[h][:, t, :], ALU.mult, ALU.add).then_inc(z_done, 1)
                    dve.wait_ge(z_done, n + 1)
                    step(tt(zx[h][:, t, :], zx[h][:, t, :], u[:, t, cols], ALU.mult))
                    step(stt(x[:, t, cols], x[:, t, cols], 2.0, zx[h][:, t, :], ALU.mult, ALU.add))
                    norm_stats(1, t, h)
                norm_var(1, t)
                if t:
                    norm_apply(1, t - 1, out_ready)
            norm_apply(1, NT - 1, out_ready)


_INS = ["x", "src", "dst", "edge_type_2", "edge_type_8", "L0_gnn_ln_weight", "L0_gnn_W_rel", "L0_gnn_W_root",
        "L0_gnn_conv_bias", "L0_gnn_wo_weight", "L1_gnn_weight", "L1_gnn_root", "L1_gnn_bias", "L1_gnn_w_gate",
        "L1_gnn_b_gate"]


def kernel(**inputs):
    import numpy as np
    import concourse.bacc as bacc
    from concourse.bass_utils import run_bass_kernel_spmd

    nc = bacc.Bacc("TRN2", target_bir_lowering=False, num_devices=1)
    arrays, args = {}, []
    for name in _INS:
        a = np.ascontiguousarray(inputs[name])
        arrays[f"in_{name}"] = a
        args.append(nc.dram_tensor(f"in_{name}", a.shape, mybir.dt.from_np(a.dtype), kind="ExternalInput").ap())
    out = nc.dram_tensor("out", (NODES, D), F32, kind="ExternalOutput").ap()
    build(nc, *args, out)
    r = run_bass_kernel_spmd(nc, [arrays], core_ids=[0])
    return r.results[0]["out"]
```

```python
from contextlib import ExitStack

import concourse.bass as bass
from concourse import mybir

ALU = mybir.AluOpType
ACT = mybir.ActivationFunctionType
AX = mybir.AxisListType
F32 = mybir.dt.float32
F16 = mybir.dt.float16
I32 = mybir.dt.int32
RMAX = bass.bass_isa.ReduceOp.max

P = 128
NODES, D = 625, 1024
NT = -(-NODES // P)
NPAD = NT * P
TAIL = NODES - (NT - 1) * P
DC = D // P
HALF = D // 2
F = 286
FC = -(-F // P)
FPAD = FC * P
R0, R1 = 2, 8
EDGES = 20000
EC = 125
CH = EDGES // EC
CP = CH // 2
WIN = 14
NWIN = -(-NODES // WIN)
WPAD = NPAD - NWIN * WIN
WCOLS = WIN * (R0 + R1)
MEET = 5
PAIRS = 3
RING = 2 * PAIRS
BLOCKS0 = (1, 1, 1, 1)
BLOCKS = (2, 2, 2, 2)
AHEAD = NWIN - sum(BLOCKS0) - (NT - 1) * sum(BLOCKS)
FIRST = AHEAD + BLOCKS0[0] + BLOCKS0[1]

TOP = 13
EXP_MASK = 0x7F800000
EXP_ONE = 1 << 23
EXP_LEAST = 27
X_GAIN = 2.0 ** 9
PROD_GAIN = 2.0 ** -17
EPS_RMS, EPS_LN = 1e-6, 1e-5

U_W0, U_WO, U_ROOT, U_REL = 0, 1, 2, 4
F3 = (1 + R0) * F
FH = F3 // 2
U_GX = U_REL + 2 * R1
U_GU = U_GX + 2
UNITS = U_GU + 2


def build(nc, x_d, src_d, dst_d, t2_d, t8_d, lnw_d, wrel_d, wroot_d, cb_d, wo_d,
          w1_d, root_d, b1_d, wg_d, bg_d, out_d):
    with ExitStack() as ctx:
        def sb(name, shape, dt):
            return ctx.enter_context(nc.sbuf_tensor(name, shape, dt))

        def ps(name, shape, dt):
            return ctx.enter_context(nc.psum_tensor(name, shape, dt))

        def sem(name):
            return ctx.enter_context(nc.semaphore(name))

        x = sb("x", [P, NT, D], F32)
        u_mem = sb("u_mem", [P, NT * D], F32)
        xT = sb("xT", [P, 2, DC, NPAD], F16)
        stage = sb("stage", [P, 2, DC * HALF], F32)
        wsplit = sb("wsplit", [P, 2, 2, DC * HALF], F16)
        p_mem = sb("p_mem", [P, 2 * NT * HALF], F32)
        c_mem = sb("c_mem", [P, R1 * NT * NPAD], F16)
        vec = sb("vec", [P, D], F32)
        convb = sb("convb", [P, F], F32)
        ident = sb("ident", [P, P], F32)
        iota_src = sb("iota_src", [P, NPAD], F16)
        iota_win = sb("iota_win", [P, WCOLS], F16)
        win_base = sb("win_base", [P, NWIN], F32)
        keyT = sb("keyT", [EC, CH, 3], F32)
        ones = sb("ones", [P, 1], F16)
        eps = sb("eps", [P, 3], F32)
        table = sb("table", [1, NWIN, 5], I32)
        most = sb("most", [1, 1], I32)
        rcnt0 = sb("rcnt0", [P, R0, NT], F32)
        rcnt = sb("rcnt", [P, R1, NT], F32)
        sc = sb("sc", [P, 4, 4], I32)
        rows = sb("rows", [P, 2, 4, NT], I32)
        am = sb("am", [P, 2], F32)
        ar = sb("ar", [P, 2], F32)
        lnw = sb("lnw", [DC, P], F32)
        lnwT = sb("lnwT", [P, DC], F32)
        w0_scale = sb("w0_scale", [P, DC], F32)
        am0 = sb("am0", [P, DC], F32)
        ar0 = sb("ar0", [P, DC], F32)
        rowmax = sb("rowmax", [P, 2, NT], F32)
        ss = sb("ss", [P, NT], F32)
        std = sb("std", [P, 3, NT], F32)
        rstd = sb("rstd", [P, 3, NT], F32)
        stats = sb("stats", [P, 2, NT, 2, 6], F32)
        mv = sb("mv", [P, 2, NT, 2], F32)
        coef0 = sb("coef0", [P, R0, NT], F32)
        coef = sb("coef", [P, NT], F32)
        cy = sb("cy", [P, NT], F32)
        cz = sb("cz", [P, 2, NT], F32)
        ci = sb("ci", [P, 4], F32)
        shift = sb("shift", [P, NT], F32)

        u = u_mem[:, :].rearrange("p (t d) -> p t d", t=NT)
        w_cnt = R0 * NT * NPAD // 2
        cnt2 = u_mem[:, 0:w_cnt].bitcast(F16).rearrange("p (r s n) -> p r s n", r=R0, s=NT)
        acc0 = u_mem[:, w_cnt:w_cnt + NT * FPAD].rearrange("p (t f) -> p t f", t=NT)
        cnt8 = c_mem[:, :].rearrange("p (r s n) -> p r s n", r=R1, s=NT)
        us = c_mem[:, 0:2 * NT * D].bitcast(F32).rearrange("p (t d) -> p t d", t=NT)
        uT = c_mem[:, 2 * NT * D:4 * NT * D].rearrange("p (a c n) -> p a c n", a=2, c=DC)
        gate_land = c_mem[:, 4 * NT * D:4 * NT * D + DC * HALF]
        w_src = RING * 2 * NPAD // 2
        src_mem = p_mem[0:EC, 0:w_src].bitcast(F16)
        win_mem = p_mem[0:EC, w_src:w_src + RING * WCOLS].bitcast(F16)
        ring_src = src_mem.rearrange("p (q e n) -> p q e n", q=RING, e=2)
        ring_win = win_mem.rearrange("p (q e n) -> p q e n", q=RING, e=2)
        oh_src = src_mem[:, 0:2 * MEET * NPAD].rearrange("p (b k n) -> p b k n", b=2, k=MEET)
        oh_win = win_mem[:, 0:2 * MEET * WCOLS].rearrange("p (b k n) -> p b k n", b=2, k=MEET)
        st_mem = stage[:, :, :].rearrange("p s w -> p (s w)")
        w_q = NT * R0 * F // 2
        q_part = [st_mem[:, a * w_q:(a + 1) * w_q].bitcast(F16).rearrange("p (s f) -> p s f", s=NT) for a in range(2)]
        root_stage = xT[:, :, :, :].rearrange("p a c n -> p (a c n)")[:, 0:2 * DC * HALF].bitcast(F32)
        w0_land = u_mem[:, w_cnt:w_cnt + DC // 2 * F3 // 2].bitcast(F16).rearrange("p (c f) -> p c f", c=DC // 2)
        wo_at = 2 * DC * HALF - FC * D
        wo_land = st_mem[:, 2 * w_q:2 * w_q + FC * D // 2].bitcast(F16)
        sp_mem = wsplit[:, :, :, :].rearrange("p s a w -> p (s a w)")
        xs = sp_mem[:, 0:2 * NT * D].bitcast(F32).rearrange("p (t d) -> p t d", t=NT)
        yT = p_mem[:, 0:FC * NPAD].bitcast(F16).rearrange("p (a c n) -> p a c n", a=2, c=FC)
        elu_tmp = p_mem[:, FC * NPAD:FC * NPAD + NT * F].rearrange("p (t f) -> p t f", t=NT)
        w_p = NT * HALF
        p_part = [[p_mem[:, s * w_p + a * w_p // 2:s * w_p + (a + 1) * w_p // 2].bitcast(F16).rearrange(
            "p (t f) -> p t f", t=NT) for a in range(2)] for s in range(2)]
        zx = [p_mem[:, s * w_p:(s + 1) * w_p].rearrange("p (t f) -> p t f", t=NT) for s in range(2)]
        e_at = DC * F3
        edges = st_mem[0:CP, e_at:e_at + 4 * 2 * EC].bitcast(I32).rearrange("p (a h e) -> p a h e", a=4, h=2)
        w_ekey, w_wtmp = 3 * 2 * EC, 24 * NWIN
        ekey = u_mem[0:CP, w_cnt:w_cnt + w_ekey].rearrange("p (a h e) -> p a h e", a=3, h=2)
        wtmp = u_mem[0:CP, w_cnt + w_ekey:w_cnt + w_ekey + w_wtmp].rearrange("p (a j) -> p a j", a=24)
        ctmp = u_mem[0:CP, w_cnt + w_ekey + w_wtmp:w_cnt + w_ekey + w_wtmp + 16].rearrange("p (a h) -> p a h", a=8)
        sc_f, rows_f = sc[:, :, :].bitcast(F32), rows[:, :, :, :].bitcast(F32)

        psP = ps("psP", [P, NT, 512], F32)
        psA = ps("psA", [P, 2, 512], F32)
        psC = ps("psC", [P, 512], F32)

        x_padded = sem("x_padded")
        x_loaded = sem("x_loaded")
        edges_loaded = sem("edges_loaded")
        lnw_loaded = sem("lnw_loaded")
        lnwT_ready = sem("lnwT_ready")
        bias_loaded = sem("bias_loaded")
        gate_bias_loaded = sem("gate_bias_loaded")
        convb_loaded = sem("convb_loaded")
        stage_full = [sem(f"stage_full{s}") for s in range(2)]
        wo_tail_loaded = sem("wo_tail_loaded")
        consts_ready = sem("consts_ready")
        pool_steps = sem("pool_steps")
        pool_turns = sem("pool_turns")
        dve_steps = sem("dve_steps")
        keys_ready = sem("keys_ready")
        keys_turned = sem("keys_turned")
        keyT_ready = sem("keyT_ready")
        bounds_ready = sem("bounds_ready")
        bounds_max = sem("bounds_max")
        table_ready = sem("table_ready")
        onehot_free = sem("onehot_free")
        onehot_ready = sem("onehot_ready")
        chunk_ready = sem("chunk_ready")
        win_counted = sem("win_counted")
        counts_padded = sem("counts_padded")
        win_free = sem("win_free")
        deg0_full = sem("deg0_full")
        deg_full = sem("deg_full")
        sumsq_ready = sem("sumsq_ready")
        rms_std_ready = sem("rms_std_ready")
        rstd_ready = sem("rstd_ready")
        xs_ready = sem("xs_ready")
        turned = sem("turned")
        turned_hi = sem("turned_hi")
        turned_split = sem("turned_split")
        w0_loaded = [sem(f"w0_loaded{a}") for a in range(2)]
        w0_sums = sem("w0_sums")
        w0_scaled = sem("w0_scaled")
        w0_hi = sem("w0_hi")
        w0_lo = sem("w0_lo")
        wsum_ready = sem("wsum_ready")
        max_ready = sem("max_ready")
        scale_step = sem("scale_step")
        whi_ready = sem("whi_ready")
        wlo_ready = sem("wlo_ready")
        w_used = sem("w_used")
        wo_padded = sem("wo_padded")
        q_full = sem("q_full")
        q_hi = sem("q_hi")
        q_done = sem("q_done")
        x_doubled = sem("x_doubled")
        acc_padded = sem("acc_padded")
        agg0_full = sem("agg0_full")
        agg0_done = sem("agg0_done")
        elu_exp = sem("elu_exp")
        elu_done = sem("elu_done")
        cy_ready = sem("cy_ready")
        y_ready = sem("y_ready")
        y_turned = sem("y_turned")
        y_hi = sem("y_hi")
        y_lo = sem("y_lo")
        wo_full = sem("wo_full")
        wo_added = sem("wo_added")
        ln_var = [sem(f"ln_var{k}") for k in range(2)]
        ln_std = [sem(f"ln_std{k}") for k in range(2)]
        ln_factors = sem("ln_factors")
        x1_ready = sem("x1_ready")
        p_full = sem("p_full")
        p_hi = sem("p_hi")
        p_done = sem("p_done")
        coef_ready = sem("coef_ready")
        agg_full = sem("agg_full")
        agg_done = sem("agg_done")
        row_scaled = sem("row_scaled")
        us_ready = sem("us_ready")
        tanh_ready = sem("tanh_ready")
        z_full = sem("z_full")
        z_done = sem("z_done")
        out_ready = sem("out_ready")
        out_stored = sem("out_stored")

        block = ctx.enter_context(nc.Block())

        def unit_weights(i, slot):
            st, hi, lo = flat_weights(i, slot)
            c = FC if i == U_WO else DC
            return [v.rearrange("p (c f) -> p c f", c=c) for v in (st, hi, lo)]

        def flat_weights(i, slot):
            n = DC * F3 if i == U_W0 else FC * D if i == U_WO else DC * HALF
            if i == U_W0:
                return st_mem[:, 0:n], sp_mem[:, 0:n], sp_mem[:, n:2 * n]
            st = st_mem[:, wo_at:wo_at + n] if i == U_WO else root_stage if i == U_ROOT else stage[:, slot, :]
            return st, wsplit[:, slot, 0, 0:n], wsplit[:, slot, 1, 0:n]

        def scale_col(i, slot):
            return i if i <= U_WO else 2 + slot

        def blocks_of(t):
            first = isinstance(t, int) and t == 0
            k = AHEAD if first else AHEAD + sum(BLOCKS0) - sum(BLOCKS)
            for n in BLOCKS0 if first else BLOCKS:
                yield [(t * sum(BLOCKS) + (k + m), (k + m) % 2) for m in range(n)]
                k += n

        def by_twos(engine, j0, j1, window):
            if j1 - j0 > 3:
                with engine.Fori(0, (j1 - j0) // 2) as it:
                    for b in range(2):
                        window(2 * it + (j0 + b), (j0 + b) % 2)
                j0 = j1 - (j1 - j0) % 2
            for j in range(j0, j1):
                window(j, j % 2)

        GATE = [(0, 0), (1, 0), (0, 1), (1, 1)] + [(t, h) for t in range(2, NT) for h in range(2)]

        def gate_turn(n):
            t, h = GATE[n]
            return 2 * t + h

        REL = U_REL

        def slot_load(i):
            return 16 * ((i + 1) // 2)

        @block.sync
        def _(sp):
            for a, v in enumerate((src_d, dst_d, t8_d, t2_d)):
                sp.dma_start(edges[:, a, :, :], v.rearrange("(h p e) -> p h e", p=CP, e=EC)).then_inc(edges_loaded, 16)
            sp.dma_start(lnw[:, :], lnw_d.rearrange("(c p) -> c p", p=P)).then_inc(lnw_loaded, 16)
            sp.dma_start(x[:, 0:NT - 1, :], x_d[0:(NT - 1) * P, :].rearrange("(t p) d -> p t d", p=P)).then_inc(x_loaded, 16)
            sp.wait_ge(x_padded, 1)
            sp.dma_start(x[0:TAIL, NT - 1, :], x_d[(NT - 1) * P:NODES, :]).then_inc(x_loaded, 16)

            def by_chunk(v):
                return v.rearrange("(c p) f -> p c f", p=P)

            st0 = unit_weights(U_W0, 0)[0]
            for a in range(2):
                part = slice(a * DC // 2, (a + 1) * DC // 2)
                for n, v in enumerate((wroot_d, wrel_d[0], wrel_d[1])):
                    sp.dma_start(st0[:, part, n * F:(n + 1) * F], by_chunk(v)[:, part, :]).then_inc(w0_loaded[a], 16)
            sp.dma_start(convb[:, :], cb_d.partition_broadcast(P)).then_inc(convb_loaded, 16)
            sp.dma_start(vec[:, :], b1_d.partition_broadcast(P)).then_inc(bias_loaded, 16)

            def load(i, slot, src):
                sp.wait_ge(wlo_ready, i - 2)
                sp.dma_start(unit_weights(REL, slot)[0], src).then_inc(stage_full[slot], 16)

            sp.wait_ge(w0_lo, DC)
            sp.wait_ge(wo_padded, 1)
            st_wo = unit_weights(U_WO, 1)[0]
            sp.dma_start(st_wo[:, 0:FC - 1, :], by_chunk(wo_d[0:(FC - 1) * P, :])).then_inc(stage_full[1], 16)
            sp.dma_start(st_wo[0:F - (FC - 1) * P, FC - 1, :], wo_d[(FC - 1) * P:F, :]).then_inc(wo_tail_loaded, 16)
            sp.wait_ge(w_used, 1)
            sp.dma_start(unit_weights(U_ROOT, 0)[0], by_chunk(root_d[:, 0:HALF])).then_inc(stage_full[0], 16)
            load(U_ROOT + 1, 1, by_chunk(root_d[:, HALF:D]))
            sp.wait_ge(agg0_full, NT * R0)
            w1_v = w1_d.rearrange("r (c p) f -> p (r c) f", p=P)
            with sp.Fori(0, R1) as r:
                for h in range(2):
                    load(U_REL + 2 * r + h, h, w1_v[:, bass.ts(r, DC), h * HALF:(h + 1) * HALF])
            sp.wait_ge(p_done, 2 * NT)
            sp.dma_start(vec[:, :], bg_d.partition_broadcast(P)).then_inc(gate_bias_loaded, 16)
            for k, top in ((U_GX, D), (U_GU, 0)):
                for h in range(2):
                    load(k + h, h, by_chunk(wg_d[top:top + D, h * HALF:(h + 1) * HALF]))
            for t in range(NT):
                n = P if t < NT - 1 else TAIL
                sp.wait_ge(out_ready, t + 1)
                sp.dma_start(out_d[t * P:t * P + n, :], x[0:n, t, :]).then_inc(out_stored, 16)
            sp.wait_ge(out_stored, 16 * NT)

        @block.gpsimd
        def _(pool):
            nc.gpsimd.memset(x[:, NT - 1, :], 0.0).then_inc(x_padded, 1)
            nc.gpsimd.memset(ident[:, :], 0.0).then_inc(pool_steps, 1)
            pool.wait_ge(pool_steps, 1)
            nc.gpsimd.affine_select(out=ident[:, :], in_=ident[:, :], compare_op=ALU.not_equal, fill=1.0, base=0,
                                    pattern=[[-1, P]], channel_multiplier=1).then_inc(consts_ready, 1)
            loose = dict(channel_multiplier=0, allow_small_or_imprecise_dtypes=True)
            nc.gpsimd.iota(win_base[:, :], pattern=[[16 * WIN, NWIN]], base=0, **loose).then_inc(consts_ready, 1)
            nc.gpsimd.iota(ctmp[:, 0, :], pattern=[[-CP, 2]], base=200, channel_multiplier=-1,
                           allow_small_or_imprecise_dtypes=True).then_inc(consts_ready, 1)
            nc.gpsimd.iota(ctmp[:, 1, :], pattern=[[CP, 2]], base=1, channel_multiplier=1,
                           allow_small_or_imprecise_dtypes=True).then_inc(consts_ready, 1)
            nc.gpsimd.iota(iota_src[:, :], pattern=[[1, NPAD]], base=0, **loose).then_inc(consts_ready, 1)
            nc.gpsimd.iota(iota_win[:, 0:WIN * R1].rearrange("p (w r) -> p w r", r=R1), pattern=[[16, WIN], [1, R1]],
                           base=0, **loose).then_inc(consts_ready, 1)
            nc.gpsimd.iota(iota_win[:, WIN * R1:WCOLS].rearrange("p (w r) -> p w r", r=R0), pattern=[[16, WIN], [1, R0]],
                           base=0, **loose).then_inc(consts_ready, 1)
            nc.gpsimd.memset(ones[:, :], 1.0).then_inc(consts_ready, 1)
            nc.gpsimd.memset(eps[:, 0:1], EPS_RMS).then_inc(consts_ready, 1)
            nc.gpsimd.memset(eps[:, 1:2], EPS_LN).then_inc(consts_ready, 1)
            nc.gpsimd.memset(eps[:, 2:3], -1.0).then_inc(consts_ready, 1)
            nc.gpsimd.memset(wtmp[:, 22, :], 1.0).then_inc(consts_ready, 1)
            nc.gpsimd.memset(cnt8[:, :, :, NPAD - WPAD:NPAD], 0.0).then_inc(counts_padded, 1)
            nc.gpsimd.memset(cnt2[:, :, :, NPAD - WPAD:NPAD], 0.0).then_inc(counts_padded, 1)
            pool.wait_ge(bounds_ready, 1)
            nc.gpsimd.partition_all_reduce(wtmp[:, 10:12, :].rearrange("p a j -> p (a j)"),
                                           wtmp[:, 8:10, :].rearrange("p a j -> p (a j)"), CP, RMAX).then_inc(bounds_max, 1)

            def unit_max(i, slot):
                pool.wait_ge(wsum_ready, i)
                pool.sem_inc(pool_turns, 1)
                nc.gpsimd.partition_all_reduce(ar[:, slot:slot + 1], am[:, slot:slot + 1], P, RMAX).then_inc(max_ready, 1)

            pool.wait_ge(w0_sums, DC)
            pool.sem_inc(pool_turns, 1)
            nc.gpsimd.partition_all_reduce(ar0[:, :], am0[:, :], P, RMAX).then_inc(max_ready, 1)
            pool.wait_ge(w0_lo, DC)
            nc.gpsimd.memset(unit_weights(U_WO, 1)[0][:, FC - 1, :], 0.0).then_inc(wo_padded, 1)
            unit_max(U_WO, 1)
            with pool.Fori(1, UNITS // 2) as k:
                for s in range(2):
                    unit_max(2 * k + s, s)

        @block.scalar
        def _(act):
            act.wait_ge(x_loaded, 32)
            for t in range(NT):
                nc.scalar.activation(xs[:, t, :], x[:, t, :], ACT.Square, accum_out=ss[:, t:t + 1]).then_inc(sumsq_ready, 1)
            act.wait_ge(sumsq_ready, NT)
            act.wait_ge(consts_ready, 12)
            nc.scalar.activation(std[:, 0, :], ss[:, :], ACT.Sqrt, bias=eps[:, 0:1], scale=1.0 / D).then_inc(rms_std_ready, 1)

            def split_hi(k, t, dst, gain):
                if k == 1:
                    act.wait_ge(wlo_ready, U_ROOT)
                for g in range(2):
                    n = 2 * NT * k + 2 * t + g
                    act.wait_ge(turned, n + 1)
                    nc.scalar.activation(dst[:, 0, 4 * g:4 * g + 4, t * P:(t + 1) * P],
                                         psA[:, g, :].rearrange("p (c n) -> p c n", c=4),
                                         ACT.Copy, scale=gain).then_inc(turned_hi, 1)

            def slot_used(i, j):
                if j <= U_ROOT + 1 and j != REL:
                    act.wait_ge(w_used, 2 if j == U_ROOT + 1 else 1)
                else:
                    act.wait_ge(p_full, NT * (i - (U_ROOT + 1)))

            def weight_sum(i, slot, loads, shape_of=None):
                j = shape_of if shape_of is not None else i
                st, land, _ = flat_weights(j, slot)
                act.wait_ge(stage_full[slot], loads)
                if j == U_WO:
                    land = wo_land
                elif j == U_GU + 1:
                    land = gate_land
                else:
                    slot_used(i, j)
                nc.scalar.activation(land, st, ACT.Abs, accum_out=am[:, slot:slot + 1]).then_inc(wsum_ready, 1)

            def weight_hi(i, slot, shape_of=None):
                j = shape_of if shape_of is not None else i
                st, hi, _ = flat_weights(j, slot)
                act.wait_ge(scale_step, 4 * i + 4)
                if j in (U_WO, U_GU + 1):
                    slot_used(i, j)
                nc.scalar.activation(hi, st, ACT.Copy, scale=sc_f[:, scale_col(j, slot), 2:3]).then_inc(whi_ready, 1)

            act.wait_ge(table_ready, 1)
            most_chunks = act.value_load(most[0:1, 0:1], min_val=1, max_val=CH)

            def copy_window(j, b):
                for bank, s0, s1 in ((2 * b, 0, 3), (2 * b + 1, 3, NT)):
                    w = psP[:, bank, 0:(s1 - s0) * WCOLS].rearrange("p (s k) -> p s k", k=WCOLS)
                    w8 = w[:, :, 0:WIN * R1].rearrange("p s (w r) -> p s r w", r=R1)
                    w2 = w[:, :, WIN * R1:WCOLS].rearrange("p s (w r) -> p s r w", r=R0)
                    o8 = cnt8[:, :, s0:s1, bass.ts(j, WIN)].rearrange("p r s w -> p s r w")
                    o2 = cnt2[:, :, s0:s1, bass.ts(j, WIN)].rearrange("p r s w -> p s r w")
                    nc.scalar.activation(o8, w8, ACT.Copy)
                    last = nc.scalar.activation(o2, w2, ACT.Copy)
                last.then_inc(win_free, 1)

            def copy_few(j, b):
                act.wait_ge(win_counted, j + (1 + 2))
                copy_window(j, b)

            def copy_any(j, b):
                after = act.value_load(table[0:1, j, 3:4], min_val=1, max_val=CH * NWIN)
                act.wait_ge(onehot_free, after + RING)
                copy_window(j, b)

            def copy_windows(j0, j1):
                with act.If(most_chunks <= MEET):
                    by_twos(act, j0, j1, copy_few)
                with act.Else():
                    by_twos(act, j0, j1, copy_any)

            def q_high(t, h):
                act.wait_ge(q_full, 2 * t + h + 1)
                src, cols = ((psA[:, 0, F:FH], slice(0, FH - F)), (psA[:, 1, 0:FH], slice(FH - F, F3 - F)))[h]
                nc.scalar.activation(q_part[0][:, t, cols], src, ACT.Copy, scale=PROD_GAIN).then_inc(q_hi, 1)

            st0, hi0, _ = unit_weights(U_W0, 0)

            def w0_sum(a):
                act.wait_ge(lnwT_ready, 1)
                act.wait_ge(w0_loaded[a], 48)
                for c in range(a * DC // 2, (a + 1) * DC // 2):
                    if a:
                        act.wait_ge(w0_sums, c - DC // 2 + 1)
                    nc.scalar.activation(w0_land[:, c % (DC // 2), :], st0[:, c, :], ACT.Abs, scale=lnwT[:, c:c + 1],
                                         accum_out=am0[:, c:c + 1]).then_inc(w0_sums, 1)

            def norm_x(t):
                nc.scalar.activation(xs[:, t, :], x[:, t, :], ACT.Copy, scale=rstd[:, 0, t:t + 1]).then_inc(xs_ready, 1)

            def w0_high(a):
                for c in range(a * DC // 2, (a + 1) * DC // 2):
                    nc.scalar.activation(hi0[:, c, :], st0[:, c, :], ACT.Copy, scale=w0_scale[:, c:c + 1]).then_inc(w0_hi, 1)

            copy_windows(0, 1)
            act.wait_ge(rstd_ready, 1)
            norm_x(0)
            norm_x(1)
            split_hi(0, 0, xT, X_GAIN)
            copy_windows(1, 2)
            norm_x(2)
            split_hi(0, 1, xT, X_GAIN)
            norm_x(3)
            copy_windows(2, 3)
            split_hi(0, 2, xT, X_GAIN)
            norm_x(4)
            copy_windows(3, 4)
            split_hi(0, 3, xT, X_GAIN)
            split_hi(0, 4, xT, X_GAIN)
            w0_sum(0)
            copy_windows(4, 5)
            w0_sum(1)
            copy_windows(5, 7)
            act.wait_ge(w0_scaled, 1)
            w0_high(0)
            copy_windows(7, AHEAD)
            w0_high(1)
            act.wait_ge(xs_ready, NT)

            def copy_tile(t, copy):
                for n, windows in enumerate(blocks_of(t)):
                    for j, b in windows:
                        copy(j, b)
                    if n % 2:
                        q_high(t, n // 2)
                    if n == 1:
                        nc.scalar.activation(x[:, t, :], x[:, t, :], ACT.Copy, scale=2.0).then_inc(x_doubled, 1)

            def copy_tiles(copy):
                copy_tile(0, copy)
                with act.Fori(1, NT - 1) as t:
                    copy_tile(t, copy)
                act.wait_ge(wo_tail_loaded, 16)
                weight_sum(U_WO, 1, slot_load(U_WO))
                copy_tile(NT - 1, copy)

            with act.If(most_chunks <= MEET):
                copy_tiles(copy_few)
            with act.Else():
                copy_tiles(copy_any)
            weight_hi(U_WO, 1)

            def elu_exponential(t):
                act.wait_ge(agg0_done, R0 * t + R0)
                nc.scalar.activation(elu_tmp[:, t, :], acc0[:, t, 0:F], ACT.Exp, bias=eps[:, 2:3]).then_inc(elu_exp, 1)

            def y_high(t):
                act.wait_ge(y_turned, t + 1)
                nc.scalar.activation(yT[:, 0, :, t * P:(t + 1) * P],
                                     psA[:, t % 2, 0:FPAD].rearrange("p (c n) -> p c n", c=FC), ACT.Copy).then_inc(y_hi, 1)

            for t in range(NT - 1):
                elu_exponential(t)
            y_high(0)
            y_high(1)
            weight_sum(U_ROOT, 0, slot_load(U_ROOT))
            elu_exponential(NT - 1)
            y_high(2)
            y_high(3)
            weight_hi(U_ROOT, 0)
            y_high(4)

            def ln_deviation(k, t):
                act.wait_ge(ln_var[k], t + 1)
                nc.scalar.activation(std[:, 1 + k, t:t + 1], mv[:, k, t, 1:2], ACT.Sqrt, bias=eps[:, 1:2]).then_inc(ln_std[k], 1)

            def x1_apply(t):
                act.wait_ge(ln_factors, 2 * t + 2)
                nc.scalar.activation(x[:, t, :], x[:, t, :], ACT.Identity, bias=shift[:, t:t + 1],
                                     scale=rstd[:, 1, t:t + 1]).then_inc(x1_ready, 1)

            for t in range(NT):
                ln_deviation(0, t)
                x1_apply(t)
                if t >= 1:
                    split_hi(1, t - 1, xT, X_GAIN)
                if t == 3:
                    weight_sum(U_ROOT + 1, 1, slot_load(U_ROOT + 1))
            split_hi(1, NT - 1, xT, X_GAIN)
            weight_hi(U_ROOT + 1, 1)

            def p_high(i, slot, tiles, first=False):
                j = i - U_REL
                for t in tiles:
                    act.wait_ge(p_full, NT * (i - U_ROOT) + t + 1)
                    if t == 0 and not first:
                        act.wait_ge(agg_full, NT * (j - 1))
                    nc.scalar.activation(p_part[slot][0][:, t, :], psP[:, t, :], ACT.Copy, scale=PROD_GAIN).then_inc(p_hi, 1)

            weight_sum(U_REL, 0, slot_load(U_REL), REL)
            weight_hi(U_REL, 0)

            def rel_step(i, slot, loads, first=False):
                weight_sum(i + 1, 1 - slot, loads, REL)
                p_high(i, slot, range(0, 2), first)
                weight_hi(i + 1, 1 - slot, shape_of=REL)
                p_high(i, slot, range(2, NT), first)

            rel_step(U_REL, 0, slot_load(U_REL + 1), first=True)
            rel_step(U_REL + 1, 1, slot_load(U_REL + 2), first=True)
            rel_step(U_REL + 2, 0, slot_load(U_REL + 3))
            with act.Fori(0, R1 - 2) as k:
                for s in range(2):
                    rel_step(U_REL + 3 + 2 * k + s, 1 - s, slot_load(U_REL + 4 + s) + 16 * k)
            rel_step(U_GX - 1, 1, slot_load(U_GX))
            weight_sum(U_GX + 1, 1, slot_load(U_GX + 1))
            weight_hi(U_GX + 1, 1)
            weight_sum(U_GU, 0, slot_load(U_GU))
            act.wait_ge(row_scaled, 1)
            for t in range(NT):
                nc.scalar.activation(us[:, t, :], u[:, t, :], ACT.Copy, scale=rows_f[:, 1, 2, t:t + 1]).then_inc(us_ready, 1)
            split_hi(2, 0, uT, 1.0)
            weight_hi(U_GU, 0)
            weight_sum(U_GU + 1, 1, slot_load(U_GU + 1))
            split_hi(2, 1, uT, 1.0)

            def u_tanh(t):
                act.wait_ge(us_ready, t + 1)
                nc.scalar.activation(u[:, t, :], u[:, t, :], ACT.Tanh).then_inc(tanh_ready, 1)

            for t in range(3):
                u_tanh(t)
            weight_hi(U_GU + 1, 1)
            for t in range(3, NT):
                u_tanh(t)
            for t in range(NT):
                if t + 2 < NT:
                    split_hi(2, t + 2, uT, 1.0)
                ln_deviation(1, t)

        @block.tensor
        def _(pe):
            pe.wait_ge(consts_ready, 1)
            pe.wait_ge(keys_ready, 5)
            for a in range(3):
                for h in range(2):
                    last = nc.tensor.transpose(psC[0:EC, (2 * a + h) * CP:(2 * a + h + 1) * CP], ekey[:, a, h, :], ident[0:CP, 0:CP])
            pe.wait_ge(lnw_loaded, 16)
            last = nc.tensor.transpose(psC[:, 3 * CH:3 * CH + DC], lnw[:, :], ident[0:DC, 0:DC])
            last.then_inc(keys_turned, 1)

            def turn(k, t, src, ready):
                pe.wait_ge(ready, t + 1)
                for g in range(2):
                    n = 2 * NT * k + 2 * t + g
                    if n >= 2:
                        pe.wait_ge(turned_split, n - 1)
                    for c in range(4):
                        last = nc.tensor.transpose(psA[:, g, c * P:(c + 1) * P],
                                                   src[:, t, (4 * g + c) * P:(4 * g + c + 1) * P], ident[:, :])
                    last.then_inc(turned, 1)

            pe.wait_ge(table_ready, 1)
            most_chunks = pe.value_load(most[0:1, 0:1], min_val=1, max_val=CH)

            def count_chunk(b, src, win, first):
                for s in range(NT):
                    col = (s % 3) * WCOLS
                    last = nc.tensor.matmul(psP[:, 2 * b + s // 3, col:col + WCOLS], src[:, s * P:(s + 1) * P], win,
                                            start=(first and s % 3 == 0), stop=False, skip_group_check=True)
                return last

            def count_pair(b, slot, first):
                count_chunk(b, ring_src[:, slot, 0, :], ring_win[:, slot, 0, :], first)
                return count_chunk(b, ring_src[:, slot, 1, :], ring_win[:, slot, 1, :], False)

            def count_few(j, b):
                pe.wait_ge(win_free, j + 1)
                for k in range(MEET):
                    pe.wait_ge(chunk_ready, MEET * j + (k + 1))
                    last = count_chunk(b, oh_src[:, b, k, :], oh_win[:, b, k, :], k == 0)
                last.then_inc(win_counted, 1)

            def count_any(j, b):
                pairs = pe.value_load(table[0:1, j, 1:2], min_val=PAIRS, max_val=CP)
                before = pe.value_load(table[0:1, j, 2:3], min_val=0, max_val=CP * NWIN)
                pe.wait_ge(win_free, j + 1)
                pe.wait_ge(onehot_ready, before + 1)
                count_pair(b, before % RING, True).then_inc(onehot_free, 1)
                with pe.Fori(1, pairs) as p:
                    pe.wait_ge(onehot_ready, before + p + 1)
                    count_pair(b, (before + p) % RING, False).then_inc(onehot_free, 1)

            def count_windows(j0, j1):
                with pe.If(most_chunks <= MEET):
                    by_twos(pe, j0, j1, count_few)
                with pe.Else():
                    by_twos(pe, j0, j1, count_any)

            def product(out, lhs, i, slot, t, cols, part=None):
                _, hi, lo = unit_weights(i, slot)
                chunks = FC if i == U_WO else DC
                for c in part or range(chunks):
                    for a, w, first in ((0, hi, c == 0), (0, lo, False), (1, hi, False)):
                        last = nc.tensor.matmul(out, lhs[:, a, c, bass.ts(t, P)], w[:, c, cols],
                                                start=first, stop=(c == chunks - 1 and a == 1))
                return last

            def weights_ready(i):
                pe.wait_ge(whi_ready, i)
                pe.wait_ge(wlo_ready, i)

            def count_tile(t, count):
                for n, windows in enumerate(blocks_of(t)):
                    h, a = n // 2, n % 2
                    for j, b in windows:
                        count(j, b)
                    if a == 0:
                        pe.wait_ge(q_done, 3 * t + (2 + h))
                    pe.wait_ge(w0_lo, (a + 1) * DC // 2)
                    pe.wait_ge(turned_split, 2 * NT)
                    last = product(psA[:, h, 0:FH], xT, U_W0, 0, t, slice(h * FH, (h + 1) * FH),
                                   range(a * DC // 2, (a + 1) * DC // 2))
                    if a:
                        last.then_inc(q_full, 1)

            count_windows(0, 2)
            turn(0, 0, xs, xs_ready)
            turn(0, 1, xs, xs_ready)
            count_windows(2, 4)
            turn(0, 2, xs, xs_ready)
            turn(0, 3, xs, xs_ready)
            count_windows(4, 5)
            turn(0, 4, xs, xs_ready)
            count_windows(5, AHEAD)
            with pe.If(most_chunks <= MEET):
                count_tile(0, count_few)
                with pe.Fori(1, NT) as t:
                    count_tile(t, count_few)
            with pe.Else():
                count_tile(0, count_any)
                with pe.Fori(1, NT) as t:
                    count_tile(t, count_any)

            degrees = psC[:, 0:(R1 + R0) * NT].rearrange("p (r t) -> p r t", t=NT)

            def degree(r, counts):
                for t in range(NT):
                    for s in range(NT):
                        last = nc.tensor.matmul(degrees[:, r, t:t + 1], counts[:, s, t * P:(t + 1) * P], ones[:, :],
                                                start=(s == 0), stop=(s == NT - 1))
                return last

            def degrees8(r0, r1):
                for r in range(r0, r1):
                    degree(r, cnt8[:, r, :, :]).then_inc(deg_full, 1)

            pe.wait_ge(win_free, NWIN + 2)
            pe.wait_ge(keyT_ready, 1)
            pe.wait_ge(lnwT_ready, 1)
            pe.wait_ge(counts_padded, 2)
            for r in range(R0):
                last = degree(R1 + r, cnt2[:, r, :, :])
            last.then_inc(deg0_full, 1)
            pe.wait_ge(q_full, 2 * NT)
            pe.sem_inc(w_used, 1)

            pe.wait_ge(q_done, 3 * NT + 3)

            def aggregate0(t):
                for r in range(R0):
                    n = R0 * t + r
                    if n >= 3:
                        pe.wait_ge(agg0_done, n - 2)
                    for s in range(NT):
                        for a in range(2):
                            last = nc.tensor.matmul(psP[:, 2 + n % 3, 0:F], cnt2[:, r, s, t * P:(t + 1) * P],
                                                    q_part[a][:, s, r * F:(r + 1) * F],
                                                    start=(s == 0 and a == 0), stop=(s == NT - 1 and a == 1))
                    last.then_inc(agg0_full, 1)

            def turn_y(t):
                pe.wait_ge(y_ready, t + 1)
                if t >= 2:
                    pe.wait_ge(y_lo, t - 1)
                for c in range(FC):
                    last = nc.tensor.transpose(psA[:, t % 2, c * P:(c + 1) * P], acc0[:, t, c * P:(c + 1) * P], ident[:, :])
                last.then_inc(y_turned, 1)

            def wo_product(t):
                if t == 0:
                    weights_ready(U_WO)
                else:
                    pe.wait_ge(agg0_done, NT * R0)
                pe.wait_ge(y_hi, t + 1)
                pe.wait_ge(y_lo, t + 1)
                for n in range(2 * t, 2 * t + 2):
                    if n >= NT:
                        pe.wait_ge(wo_added, n - NT + 1)
                    product(psP[:, n % NT, :], yT, U_WO, 1, t, slice(n % 2 * HALF, (n % 2 + 1) * HALF)).then_inc(wo_full, 1)

            def tile_product(i, slot, t, first=False):
                if not first:
                    pe.wait_ge(p_done, NT * (i - U_ROOT - 1) + t + 1)
                product(psP[:, t, :], xT, REL, slot, t, slice(0, HALF)).then_inc(p_full, 1)

            def root_product(t):
                if t == 0:
                    weights_ready(U_ROOT)
                pe.wait_ge(wo_added, NT + t + 1)
                pe.wait_ge(turned_split, 2 * NT + 2 * t + 2)
                tile_product(U_ROOT, 0, t, first=True)

            for t in range(NT - 2):
                aggregate0(t)
            degrees8(0, 2)
            aggregate0(NT - 2)
            turn_y(0)
            turn_y(1)
            aggregate0(NT - 1)
            degrees8(2, 5)
            wo_product(0)
            turn_y(2)
            turn_y(3)
            wo_product(1)
            turn_y(4)
            wo_product(2)
            pe.wait_ge(y_lo, NT)
            turn(1, 0, x, x1_ready)
            wo_product(3)
            degrees8(5, 7)
            wo_product(4)
            pe.wait_ge(wo_full, 2 * NT)
            pe.sem_inc(w_used, 1)
            turn(1, 1, x, x1_ready)
            for t in range(2, NT):
                root_product(t - 2)
                if t == 3:
                    degrees8(7, R1)
                turn(1, t, x, x1_ready)
            root_product(NT - 2)
            root_product(NT - 1)

            def products(i, slot):
                weights_ready(i)
                for t in range(NT):
                    tile_product(i, slot, t)

            def aggregate(j, r, h, first=False):
                pe.wait_ge(p_done, NT * (j + U_REL - U_ROOT + 1))
                for t in range(NT):
                    if not (first and t < 2):
                        pe.wait_ge(agg_done, NT * j + t - 1)
                    for s in range(NT):
                        for a in range(2):
                            last = nc.tensor.matmul(psA[:, (NT * h + t) % 2, :], cnt8[:, r, s, t * P:(t + 1) * P],
                                                    p_part[h][a][:, s, :], start=(s == 0 and a == 0), stop=(s == NT - 1 and a == 1))
                    last.then_inc(agg_full, 1)

            products(U_ROOT + 1, 1)
            pe.wait_ge(turned_split, 4 * NT)
            products(U_REL, 0)
            products(U_REL + 1, 1)
            aggregate(0, 0, 0, first=True)
            products(U_REL + 2, 0)
            aggregate(1, 0, 1)
            with pe.Fori(0, R1 - 2) as k:
                products(U_REL + 3 + 2 * k, 1)
                aggregate(2 + 2 * k, k + 1, 0)
                products(U_REL + 4 + 2 * k, 0)
                aggregate(3 + 2 * k, k + 1, 1)
            products(U_GX - 1, 1)
            aggregate(2 * R1 - 2, R1 - 1, 0)
            products(U_GX, 0)
            aggregate(2 * R1 - 1, R1 - 1, 1)
            pe.wait_ge(agg_done, NT * 2 * R1)
            for t in range(NT):
                tile_product(U_GX + 1, 1, t)
                if t in (1, 3):
                    turn(2, t // 2, us, us_ready)

            def gate_product(n):
                t, h = GATE[n]
                pe.wait_ge(turned_hi, 4 * NT + 2 * t + 2)
                pe.wait_ge(turned_split, 4 * NT + 2 * t + 2)
                if t == 0:
                    weights_ready(U_GU + h)
                if n >= NT:
                    pe.wait_ge(z_done, 1 + gate_turn(n - NT))
                product(psP[:, n % NT, :], uT, REL, h, t, slice(0, HALF)).then_inc(z_full, 1)

            pe.wait_ge(p_done, NT * (U_GU - U_ROOT))
            gate_product(0)
            turn(2, 2, us, us_ready)
            for n in range(1, 4):
                gate_product(n)
            for t in range(2, NT):
                if t + 1 < NT:
                    turn(2, t + 1, us, us_ready)
                gate_product(2 * t)
                gate_product(2 * t + 1)

        @block.vector
        def _(dve):
            steps = [0]

            def step(ins):
                steps[0] += 1
                ins.then_inc(dve_steps, 1)
                dve.wait_ge(dve_steps, steps[0])

            ts, stt, tt = nc.vector.tensor_scalar, nc.vector.scalar_tensor_tensor, nc.vector.tensor_tensor

            def exponents(dst, bits, least=EXP_LEAST):
                return (lambda: ts(dst[0], bits, EXP_MASK, None, ALU.bitwise_and),
                        lambda: ts(dst[1], dst[0], float(least * EXP_ONE), None, ALU.max),
                        lambda: ts(dst[2], dst[1], -1.0, float((254 + TOP) * EXP_ONE), ALU.mult, ALU.add),
                        lambda: ts(dst[3], dst[1], float(TOP * EXP_ONE), None, ALU.subtract))

            def row_scales(dst, bits, ready=None, least=EXP_LEAST):
                *chain, last = exponents(dst, bits, least)
                for f in chain:
                    step(f())
                if ready:
                    last().then_inc(ready, 1)
                    dve.wait_ge(ready, 1)
                else:
                    step(last())

            dve.wait_ge(edges_loaded, 64)
            nc.vector.tensor_copy(ekey[:, 0, :, :], edges[:, 0, :, :]).then_inc(keys_ready, 1)
            stt(ekey[:, 1, :, :], edges[:, 1, :, :], 16.0, edges[:, 2, :, :], ALU.mult, ALU.add).then_inc(keys_ready, 1)
            stt(ekey[:, 2, :, :], edges[:, 1, :, :], 16.0, edges[:, 3, :, :], ALU.mult, ALU.add).then_inc(keys_ready, 1)
            nc.vector.tensor_reduce(ctmp[:, 2, :], edges[:, 1, :, :], AX.X, ALU.min).then_inc(keys_ready, 1)
            nc.vector.tensor_reduce(ctmp[:, 3, :], edges[:, 1, :, :], AX.X, ALU.max).then_inc(keys_ready, 1)
            dve.wait_ge(keys_ready, 5)
            step(ts(ctmp[:, 4, :], ctmp[:, 2, :], 16.0, 16.0 * (WIN - 1), ALU.mult, ALU.subtract))
            step(ts(ctmp[:, 5, :], ctmp[:, 3, :], 16.0, None, ALU.mult))
            dve.wait_ge(consts_ready, 12)
            base = win_base[0:CP, :]
            for h in range(2):
                step(ts(wtmp[:, h, :], base, ctmp[:, 5, h:h + 1], None, ALU.is_le))
                step(stt(wtmp[:, 2 + h, :], base, ctmp[:, 4, h:h + 1], wtmp[:, h, :], ALU.is_ge, ALU.mult))
                step(ts(wtmp[:, 4 + h, :], wtmp[:, 2 + h, :], ctmp[:, 0, h:h + 1], None, ALU.mult))
                step(ts(wtmp[:, 6 + h, :], wtmp[:, 2 + h, :], ctmp[:, 1, h:h + 1], None, ALU.mult))
            step(tt(wtmp[:, 8, :], wtmp[:, 4, :], wtmp[:, 5, :], ALU.max))
            tt(wtmp[:, 9, :], wtmp[:, 6, :], wtmp[:, 7, :], ALU.max).then_inc(bounds_ready, 1)
            dve.wait_ge(keys_turned, 1)
            nc.vector.tensor_copy(keyT[:, :, :].rearrange("p k a -> p a k"),
                                  psC[0:EC, 0:3 * CH].rearrange("p (a k) -> p a k", a=3)).then_inc(keyT_ready, 1)
            nc.vector.tensor_copy(lnwT[:, :], psC[:, 3 * CH:3 * CH + DC]).then_inc(lnwT_ready, 1)

            dve.wait_ge(bounds_max, 1)

            def row(a):
                return wtmp[0:1, a, :]
            step(ts(row(12), row(10), -1.0, 200.0, ALU.mult, ALU.add))
            step(tt(row(13), row(11), row(12), ALU.subtract))
            pairs_i = wtmp[0:1, 14, :].bitcast(I32)
            step(ts(pairs_i, row(13), 0.5, 0.25, ALU.mult, ALU.add))
            step(ts(row(15), pairs_i, float(PAIRS), None, ALU.max))
            step(ts(row(16), row(15), -2.0, float(CH), ALU.mult, ALU.add))
            step(nc.vector.tensor_tensor_scan(row(17), row(22), row(15), 0.0, ALU.mult, ALU.add))
            step(tt(table[:, :, 0], row(12), row(16), ALU.min))
            step(nc.vector.tensor_copy(table[:, :, 1], row(15)))
            step(tt(table[:, :, 2], row(17), row(15), ALU.subtract))
            step(nc.vector.tensor_copy(table[:, :, 3], row(17)))
            step(ts(table[:, :, 4], row(12), float(CH - MEET), None, ALU.min))
            nc.vector.tensor_reduce(most[:, :], row(13), AX.X, ALU.max).then_inc(table_ready, 1)

            def split_lo(k, t, dst, gain):
                for g in range(2):
                    n = 2 * NT * k + 2 * t + g
                    dve.wait_ge(turned_hi, n + 1)
                    hi = dst[:, 0, 4 * g:4 * g + 4, t * P:(t + 1) * P]
                    lo = dst[:, 1, 4 * g:4 * g + 4, t * P:(t + 1) * P]
                    stt(lo, psA[:, g, :].rearrange("p (c n) -> p c n", c=4), gain, hi,
                        ALU.mult, ALU.subtract).then_inc(turned_split, 1)

            def unit_scale(i, slot, shape_of=None):
                j = shape_of if shape_of is not None else i
                c = scale_col(j, slot)
                dve.wait_ge(max_ready, i + 1)
                for k, f in enumerate(exponents([sc[:, c, a:a + 1] for a in range(4)], ar[:, slot:slot + 1].bitcast(I32))):
                    if k in (1, 2):
                        dve.wait_ge(scale_step, 4 * i + k)
                    f().then_inc(scale_step, 1)

            def unit_lo(i, slot, shape_of=None):
                j = shape_of if shape_of is not None else i
                st, hi, lo = flat_weights(j, slot)
                dve.wait_ge(whi_ready, i)
                stt(lo, st, sc_f[:, scale_col(j, slot), 2:3], hi, ALU.mult, ALU.subtract).then_inc(wlo_ready, 1)

            dve.sem_inc(onehot_free, RING)
            dve.sem_inc(win_counted, 2)
            dve.sem_inc(win_free, 2)
            dve.sem_inc(q_done, 3)
            dve.wait_ge(table_ready, 1)
            dve.wait_ge(keyT_ready, 1)
            most_chunks = dve.value_load(most[0:1, 0:1], min_val=1, max_val=CH)
            win8 = iota_win[0:EC, 0:WIN * R1]
            win2 = iota_win[0:EC, WIN * R1:WCOLS]

            def onehot_few(j, b):
                chunk = dve.value_load(table[0:1, j, 4:5], min_val=0, max_val=CH - MEET)
                wb = win_base[0:EC, bass.ts(j, 1)]
                dve.wait_ge(win_counted, j + 1)
                for a, w, cols in ((1, win8, slice(0, WIN * R1)), (2, win2, slice(WIN * R1, WCOLS))):
                    n = w.shape[1]
                    stt(oh_win[:, b, :, cols], w.unsqueeze(1).broadcast_to([EC, MEET, n]), wb,
                        keyT[:, bass.ds(chunk, MEET), a:a + 1].broadcast_to([EC, MEET, n]), ALU.add, ALU.is_equal)
                for k in range(MEET):
                    ts(oh_src[:, b, k, :], iota_src[0:EC, :], keyT[:, chunk + k, 0:1], None,
                       ALU.is_equal).then_inc(chunk_ready, 1)

            def onehot_any(j, b):
                chunk = dve.value_load(table[0:1, j, 0:1], min_val=0, max_val=CH - 2 * PAIRS)
                pairs = dve.value_load(table[0:1, j, 1:2], min_val=PAIRS, max_val=CP)
                before = dve.value_load(table[0:1, j, 2:3], min_val=0, max_val=CP * NWIN)
                with dve.Fori(0, pairs) as p:
                    q = before + p
                    dve.wait_ge(onehot_free, q + 1)
                    slot = q % RING
                    wb = win_base[0:EC, bass.ts(j, 1)]
                    for e in range(2):
                        k = (chunk + 2 * p).with_bounds(min_val=0, max_val=CH - 2) + e
                        ts(ring_src[:, slot, e, :], iota_src[0:EC, :], keyT[:, k, 0:1], None, ALU.is_equal)
                        ts(ring_win[:, slot, e, 0:WIN * R1], win8, wb, keyT[:, k, 1:2], ALU.add, ALU.is_equal)
                        last = ts(ring_win[:, slot, e, WIN * R1:WCOLS], win2, wb, keyT[:, k, 2:3],
                                  ALU.add, ALU.is_equal)
                    last.then_inc(onehot_ready, 1)

            def onehot_windows(j0, j1):
                with dve.If(most_chunks <= MEET):
                    by_twos(dve, j0, j1, onehot_few)
                with dve.Else():
                    by_twos(dve, j0, j1, onehot_any)

            def first_sums(t, h):
                dve.wait_ge(q_hi, 2 * t + (h + 1))
                if h == 0:
                    stt(acc0[:, t, 0:F], psA[:, 0, 0:F], ci[:, 0:1], convb[:, :], ALU.mult, ALU.add).then_inc(q_done, 1)
                src, cols = ((psA[:, 0, F:FH], slice(0, FH - F)), (psA[:, 1, 0:FH], slice(FH - F, F3 - F)))[h]
                stt(q_part[1][:, t, cols], src, PROD_GAIN, q_part[0][:, t, cols], ALU.mult, ALU.subtract).then_inc(q_done, 1)

            st0, hi0, lo0 = unit_weights(U_W0, 0)

            def split_x_lo(*tiles):
                for t in tiles:
                    split_lo(0, t, xT, X_GAIN)

            onehot_windows(0, 2)
            dve.wait_ge(rms_std_ready, 1)
            nc.vector.reciprocal(rstd[:, 0, :], std[:, 0, :]).then_inc(rstd_ready, 1)
            onehot_windows(2, 4)
            split_x_lo(0, 1)
            onehot_windows(4, 5)
            split_x_lo(2, 3)
            onehot_windows(5, 6)
            split_x_lo(4)
            onehot_windows(6, AHEAD)
            dve.wait_ge(lnwT_ready, 1)
            dve.wait_ge(max_ready, 1)
            step(nc.vector.tensor_reduce(ar[:, 0:1], ar0[:, :], AX.X, ALU.add))
            unit_scale(U_W0, 0)
            dve.wait_ge(scale_step, 3)
            ts(w0_scale[:, :], lnwT[:, :], sc_f[:, U_W0, 2:3], None, ALU.mult).then_inc(w0_scaled, 1)
            nc.vector.memset(acc0[:, :, F:FPAD], 0.0).then_inc(acc_padded, 1)
            dve.wait_ge(scale_step, 4)
            step(ts(ci[:, 0:1], sc_f[:, U_W0, 3:4], 1.0 / X_GAIN, None, ALU.mult))
            step(ts(ci[:, 1:2], ci[:, 0:1], 1.0 / PROD_GAIN, None, ALU.mult))
            dve.wait_ge(convb_loaded, 16)
            step(ts(convb[:, :], convb[:, :], 1.0, None, ALU.add))
            dve.wait_ge(w0_scaled, 1)
            onehot_windows(AHEAD, FIRST - 1)

            def w0_low(a):
                for c in range(a * DC // 2, (a + 1) * DC // 2):
                    dve.wait_ge(w0_hi, c + 1)
                    stt(lo0[:, c, :], st0[:, c, :], w0_scale[:, c:c + 1], hi0[:, c, :], ALU.mult, ALU.subtract).then_inc(w0_lo, 1)

            w0_low(0)
            onehot_windows(FIRST - 1, FIRST)
            w0_low(1)

            def onehot_tile(t, onehots, first=False):
                for n, windows in enumerate(blocks_of(t)):
                    if not (first and n < 2):
                        for j, b in windows:
                            onehots(j, b)
                    if n == 0 and not first:
                        first_sums(t - 1, 1)
                    if n == 2:
                        first_sums(t, 0)

            def onehot_tiles(onehots):
                onehot_tile(0, onehots, first=True)
                with dve.Fori(1, NT) as t:
                    onehot_tile(t, onehots)
                first_sums(NT - 1, 1)

            with dve.If(most_chunks <= MEET):
                onehot_tiles(onehot_few)
            with dve.Else():
                onehot_tiles(onehot_any)
            unit_scale(U_WO, 1)
            dve.wait_ge(deg0_full, 1)
            rc0 = rcnt0[:, :, :].rearrange("p r t -> p (r t)")
            step(ts(rc0, psC[:, R1 * NT:(R1 + R0) * NT], 1.0, None, ALU.max))
            step(nc.vector.reciprocal(rc0, rc0))
            step(ts(coef0[:, :, :].rearrange("p r t -> p (r t)"), rc0, ci[:, 1:2], None, ALU.mult))
            dve.wait_ge(acc_padded, 1)
            dve.wait_ge(q_done, 3 * NT + 3)

            def agg0_add(t):
                for r in range(R0):
                    n = R0 * t + r
                    dve.wait_ge(agg0_full, n + 1)
                    if r:
                        dve.wait_ge(agg0_done, n)
                    stt(acc0[:, t, 0:F], psP[:, 2 + n % 3, 0:F], coef0[:, r, t:t + 1], acc0[:, t, 0:F],
                        ALU.mult, ALU.add).then_inc(agg0_done, 1)

            def elu_end(t0, t1):
                for t in range(t0, t1):
                    dve.wait_ge(elu_exp, t + 1)
                    stt(acc0[:, t, 0:F], elu_tmp[:, t, :], 1.0, acc0[:, t, 0:F], ALU.min, ALU.max).then_inc(elu_done, 1)
                dve.wait_ge(elu_done, t1)
                step(nc.vector.tensor_reduce(rowmax[:, 0, t0:t1], acc0[:, t0:t1, 0:F], AX.X, ALU.max))
                row_scales([rows[:, 0, a, t0:t1] for a in range(4)], rowmax[:, 0, t0:t1].bitcast(I32), least=127)
                for t in range(t0, t1):
                    ts(acc0[:, t, 0:F], acc0[:, t, 0:F], -1.0, rows_f[:, 0, 2, t:t + 1], ALU.add, ALU.mult).then_inc(y_ready, 1)
                ts(cy[:, t0:t1], rows_f[:, 0, 3, t0:t1], sc_f[:, U_WO, 3:4], None, ALU.mult).then_inc(cy_ready, 1)

            def y_low(t):
                dve.wait_ge(y_hi, t + 1)
                tt(yT[:, 1, :, t * P:(t + 1) * P], psA[:, t % 2, 0:FPAD].rearrange("p (c n) -> p c n", c=FC),
                   yT[:, 0, :, t * P:(t + 1) * P], ALU.subtract).then_inc(y_lo, 1)

            agg0_add(0)
            agg0_add(1)
            elu_end(0, 2)
            agg0_add(2)
            agg0_add(3)
            unit_lo(U_WO, 1)
            y_low(0)
            y_low(1)
            agg0_add(4)
            elu_end(2, 4)
            unit_scale(U_ROOT, 0)
            elu_end(4, NT)
            y_low(2)
            y_low(3)

            def norm_stats(k, t, h):
                step(nc.vector.bn_stats(stats[:, k, t, h, :], x[:, t, h * HALF:(h + 1) * HALF]))

            def norm_var(k, t):
                nc.vector.bn_aggr(mv[:, k, t, :], stats[:, k, t, :, :].rearrange("p h s -> p (h s)")).then_inc(ln_var[k], 1)

            def norm_reciprocal(k, t):
                dve.wait_ge(ln_std[k], t + 1)
                dve.wait_ge(ln_var[k], t + 1)
                return nc.vector.reciprocal(rstd[:, 1 + k, t:t + 1], std[:, 1 + k, t:t + 1])

            def norm_apply(k, t, ready):
                step(norm_reciprocal(k, t))
                ts(x[:, t, :], x[:, t, :], mv[:, k, t, 0:1], rstd[:, 1 + k, t:t + 1], ALU.subtract, ALU.mult).then_inc(ready, 1)

            dve.wait_ge(x_doubled, NT)
            for t in range(NT):
                for h in range(2):
                    n = 2 * t + h
                    dve.wait_ge(wo_full, n + 1)
                    xv = x[:, t, h * HALF:(h + 1) * HALF]
                    dve.wait_ge(cy_ready, t // 2 + 1)
                    stt(xv, psP[:, n % NT, :], cy[:, t:t + 1], xv, ALU.mult, ALU.add).then_inc(wo_added, 1)
                    dve.wait_ge(wo_added, n + 1)
                    norm_stats(0, t, h)
                norm_var(0, t)
                norm_reciprocal(0, t).then_inc(ln_factors, 1)
                dve.wait_ge(ln_factors, 2 * t + 1)
                ts(shift[:, t:t + 1], mv[:, 0, t, 0:1], rstd[:, 1, t:t + 1], -1.0, ALU.mult, ALU.mult).then_inc(ln_factors, 1)
                if t == 0:
                    y_low(4)
                if t == 1:
                    unit_lo(U_ROOT, 0)
                if t >= 2:
                    split_lo(1, t - 2, xT, X_GAIN)
            split_lo(1, NT - 2, xT, X_GAIN)
            unit_scale(U_ROOT + 1, 1)
            split_lo(1, NT - 1, xT, X_GAIN)
            unit_lo(U_ROOT + 1, 1)

            def evacuate(i, slot, t, kind, h=0):
                k = NT * (i - U_ROOT) + t + 1
                src = psP[:, t, :]
                if kind == "rel":
                    dve.wait_ge(p_hi, NT * (i - U_REL) + t + 1)
                    ins = stt(p_part[slot][1][:, t, :], src, PROD_GAIN, p_part[slot][0][:, t, :], ALU.mult, ALU.subtract)
                else:
                    dve.wait_ge(p_full, k)
                    dst = u[:, t, h * HALF:(h + 1) * HALF] if kind == "root" else zx[h][:, t, :]
                    ins = stt(dst, src, ci[:, 3:4], vec[:, h * HALF:(h + 1) * HALF], ALU.mult, ALU.add)
                ins.then_inc(p_done, 1)

            def agg_coef(j, r, slot):
                if not (isinstance(j, int) and j == 0):
                    dve.wait_ge(agg_done, NT * j)
                ts(coef[:, :], rcnt[:, r, :], sc_f[:, scale_col(REL, slot), 3:4], 1.0 / (X_GAIN * PROD_GAIN),
                   ALU.mult, ALU.mult).then_inc(coef_ready, 1)

            def agg_add(j, h):
                dve.wait_ge(coef_ready, j + 1)
                for t in range(NT):
                    uv = u[:, t, h * HALF:(h + 1) * HALF]
                    dve.wait_ge(agg_full, NT * j + t + 1)
                    stt(uv, psA[:, (NT * h + t) % 2, :], coef[:, t:t + 1], uv, ALU.mult, ALU.add).then_inc(agg_done, 1)

            def plain_factor(i, slot):
                if i != U_ROOT:
                    dve.wait_ge(p_done, NT * (i - U_ROOT))
                step(ts(ci[:, 3:4], sc_f[:, scale_col(REL, slot), 3:4], 1.0 / X_GAIN, None, ALU.mult))

            def root_step(i, slot):
                plain_factor(i, slot)
                for t in range(NT):
                    evacuate(i, slot, t, "root", slot)
                    if slot and t == 0:
                        unit_scale(i + 1, 1 - slot, REL)
                    if slot and t == 1:
                        unit_lo(i + 1, 1 - slot, REL)

            def rel_step(i, slot, agg=None):
                if agg:
                    agg_coef(agg[0], agg[1], 1 - slot)
                evacuate(i, slot, 0, "rel")
                unit_scale(i + 1, 1 - slot, REL)
                evacuate(i, slot, 1, "rel")
                evacuate(i, slot, 2, "rel")
                unit_lo(i + 1, 1 - slot, REL)
                evacuate(i, slot, 3, "rel")
                evacuate(i, slot, 4, "rel")
                if agg:
                    agg_add(agg[0], 1 - slot)

            dve.wait_ge(bias_loaded, 16)
            root_step(U_ROOT, 0)
            root_step(U_ROOT + 1, 1)
            dve.wait_ge(deg_full, R1)
            rc = rcnt[:, :, :].rearrange("p r t -> p (r t)")
            step(ts(rc, psC[:, 0:R1 * NT], 1.0, None, ALU.max))
            step(nc.vector.reciprocal(rc, rc))
            rel_step(U_REL, 0)
            rel_step(U_REL + 1, 1, (0, 0))
            rel_step(U_REL + 2, 0, (1, 0))
            with dve.Fori(0, R1 - 2) as k:
                rel_step(U_REL + 3 + 2 * k, 1, (2 + 2 * k, k + 1))
                rel_step(U_REL + 4 + 2 * k, 0, (3 + 2 * k, k + 1))
            rel_step(U_GX - 1, 1, (2 * R1 - 2, R1 - 1))

            dve.wait_ge(gate_bias_loaded, 16)
            agg_coef(2 * R1 - 1, R1 - 1, 1)
            plain_factor(U_GX, 0)
            evacuate(U_GX, 0, 0, "gate", 0)
            unit_scale(U_GX + 1, 1)
            evacuate(U_GX, 0, 1, "gate", 0)
            evacuate(U_GX, 0, 2, "gate", 0)
            unit_lo(U_GX + 1, 1)
            evacuate(U_GX, 0, 3, "gate", 0)
            evacuate(U_GX, 0, 4, "gate", 0)
            unit_scale(U_GU, 0)
            agg_add(2 * R1 - 1, 1)
            plain_factor(U_GX + 1, 1)
            dve.wait_ge(agg_done, 2 * R1 * NT)
            for t in range(NT):
                step(nc.vector.tensor_reduce(rowmax[:, 1, t:t + 1], u[:, t, :], AX.X, ALU.max, apply_absolute_value=True))
            row_scales([rows[:, 1, a, :] for a in range(4)], rowmax[:, 1, :].bitcast(I32), row_scaled)
            split_lo(2, 0, uT, 1.0)
            unit_lo(U_GU, 0)
            step(ts(cz[:, 0, :], rows_f[:, 1, 3, :], sc_f[:, scale_col(REL, 0), 3:4], None, ALU.mult))
            for t in range(NT):
                evacuate(U_GX + 1, 1, t, "gate", 1)
            split_lo(2, 1, uT, 1.0)
            unit_scale(U_GU + 1, 1)
            unit_lo(U_GU + 1, 1)
            dve.wait_ge(scale_step, 4 * UNITS)
            step(ts(cz[:, 1, :], rows_f[:, 1, 3, :], sc_f[:, scale_col(REL, 1), 3:4], None, ALU.mult))
            for t in range(NT):
                if t + 2 < NT:
                    split_lo(2, t + 2, uT, 1.0)
                dve.wait_ge(tanh_ready, t + 1)
                step(tt(u[:, t, :], u[:, t, :], x[:, t, :], ALU.subtract))
                for h in range(2):
                    n = 2 * t + h
                    cols = slice(h * HALF, (h + 1) * HALF)
                    at = GATE.index((t, h))
                    dve.wait_ge(z_full, at + 1)
                    stt(zx[h][:, t, :], psP[:, at % NT, :], cz[:, h, t:t + 1], zx[h][:, t, :], ALU.mult, ALU.add).then_inc(z_done, 1)
                    dve.wait_ge(z_done, n + 1)
                    step(tt(zx[h][:, t, :], zx[h][:, t, :], u[:, t, cols], ALU.mult))
                    step(stt(x[:, t, cols], x[:, t, cols], 2.0, zx[h][:, t, :], ALU.mult, ALU.add))
                    norm_stats(1, t, h)
                    if t and h == 0:
                        norm_apply(1, t - 1, out_ready)
                norm_var(1, t)
            norm_apply(1, NT - 1, out_ready)


_INS = ["x", "src", "dst", "edge_type_2", "edge_type_8", "L0_gnn_ln_weight", "L0_gnn_W_rel", "L0_gnn_W_root",
        "L0_gnn_conv_bias", "L0_gnn_wo_weight", "L1_gnn_weight", "L1_gnn_root", "L1_gnn_bias", "L1_gnn_w_gate",
        "L1_gnn_b_gate"]


def kernel(**inputs):
    import numpy as np
    import concourse.bacc as bacc
    from concourse.bass_utils import run_bass_kernel_spmd

    nc = bacc.Bacc("TRN2", target_bir_lowering=False, num_devices=1)
    arrays, args = {}, []
    for name in _INS:
        a = np.ascontiguousarray(inputs[name])
        arrays[f"in_{name}"] = a
        args.append(nc.dram_tensor(f"in_{name}", a.shape, mybir.dt.from_np(a.dtype), kind="ExternalInput").ap())
    out = nc.dram_tensor("out", (NODES, D), F32, kind="ExternalOutput").ap()
    build(nc, *args, out)
    r = run_bass_kernel_spmd(nc, [arrays], core_ids=[0])
    return r.results[0]["out"]
```
